# Optimizing a Trainium2 kernel written in Bass

```python
import numpy as np
import jax
import jax.numpy as jnp

def _softmax(x, axis=-1):
    return jax.nn.softmax(x, axis=axis)

def _gelu(x):
    return jax.nn.gelu(x, approximate=True)

def _silu(x):
    return jax.nn.silu(x)

def _sigmoid(x):
    return jax.nn.sigmoid(x)

def _layernorm(x, axis=-1, eps=1e-05):
    m = jnp.mean(x, axis=axis, keepdims=True)
    v = jnp.var(x, axis=axis, keepdims=True)
    return (x - m) / jnp.sqrt(v + eps)

def _scatter_add(tgt, idx, src, axis=0):
    return tgt.at[idx].add(src)

def _segment_sum(src, seg, n):
    return jax.ops.segment_sum(src, seg, n)
kernel_name = 'mk_decoder_postln_d1_seqx_r8_fb142f'

def setup_inputs(seed: int=0):
    np.random.seed(seed)
    _w = jnp.asarray

    def _rec_inputs():
        import jax
        import jax.numpy as jnp
        _rk = jax.random.key(seed)
        x = -0.0003929 + 0.9999 * jax.random.normal(jax.random.fold_in(_rk, 1), (4, 512, 128), jnp.float32)
        _lenS = 512 - jax.random.randint(jax.random.fold_in(_rk, 7), (4,), 0, max(1, 512 // 4) + 1, jnp.int32)
        _lenS2 = 154 - jax.random.randint(jax.random.fold_in(_rk, 8), (4,), 0, max(1, 154 // 4) + 1, jnp.int32)
        _ctx_1024P = jax.random.normal(jax.random.fold_in(_rk, 11), (4, 16, 128), jnp.float32)
        _ctx_1024c = jax.random.dirichlet(jax.random.fold_in(_rk, 511), 0.3 * jnp.ones((16,), jnp.float32), (4, 154))
        _ctx_1024t = jnp.einsum('bsk,bkd->bsd', _ctx_1024c, _ctx_1024P)
        _ctx_1024t = _ctx_1024t * jax.lax.rsqrt(jnp.mean(jnp.square(_ctx_1024t)) + 1e-12) * 0.953939
        ctx_1024 = 2.81802e-05 + 1.00001 * (_ctx_1024t + 0.3 * jax.random.normal(jax.random.fold_in(_rk, 611), (4, 154, 128), jnp.float32))
        return (x, ctx_1024)
    x, ctx_1024 = _rec_inputs()

    def _L0_attn_setup():
        import jax, jax.numpy as jnp
        import numpy as np
        B, T, D_MODEL = (2, 64, 128)
        D_INNER, D_HEAD, D_CONV = (256, 64, 4)
        N_HEADS, D_STATE = (32, 32)
        DT_MIN, DT_MAX, K_MAX, EPS = (0.0001, 0.1, 0.5, 1e-08)

        def _forward(x, W_in, dw_weight, dw_bias, W_bc, W_out, skip, A_log, dt_bias):
            Bsz, Tlen, D = x.shape
            DI, K = dw_weight.shape
            H, N = A_log.shape
            DH = DI // H
            proj = jnp.einsum('btd,od->bto', x, W_in)
            gate = proj[..., :DI]
            value_raw = proj[..., DI:2 * DI]
            params = proj[..., 2 * DI:].reshape(Bsz, Tlen, H, 2)
            xp = jnp.pad(value_raw, ((0, 0), (K - 1, 0), (0, 0)))
            conv = dw_bias + sum((xp[:, k:k + Tlen, :] * dw_weight[:, k] for k in range(K)))
            value = jax.nn.silu(conv)
            dt = jnp.clip(jax.nn.softplus(params[..., 0] + dt_bias), DT_MIN, DT_MAX)
            kd = K_MAX * jax.nn.sigmoid(params[..., 1])
            A = jnp.exp(A_log)
            bc = jnp.einsum('bti,oi->bto', value, W_bc).reshape(Bsz, Tlen, H, 4, N)
            bc = bc / (jnp.sqrt(jnp.sum(bc * bc, axis=-1, keepdims=True)) + EPS)
            Bz, Bx, Cz, Cx = (bc[..., 0, :], bc[..., 1, :], bc[..., 2, :], bc[..., 3, :])
            u = value.reshape(Bsz, Tlen, H, DH)

            def step(carry, inp):
                z, s = carry
                u_t, dt_t, k_t, Bz_t, Bx_t, Cz_t, Cx_t = inp
                dtE = dt_t[:, :, None, None]
                S = 1.0 / (1.0 + dt_t[..., None] * k_t[..., None] + (dt_t * dt_t)[..., None] * A)
                z = S[..., None] * (z - dtE * A[None, :, :, None] * s + dtE * (Bz_t[..., None] * u_t[:, :, None, :]))
                s = s + dtE * z + dtE * (Bx_t[..., None] * u_t[:, :, None, :])
                y = jnp.einsum('bhn,bhnd->bhd', Cz_t, z) + jnp.einsum('bhn,bhnd->bhd', Cx_t, s)
                return ((z, s), y)
            tm = lambda a: jnp.moveaxis(a, 1, 0)
            init = (jnp.zeros((Bsz, H, N, DH), x.dtype), jnp.zeros((Bsz, H, N, DH), x.dtype))
            _, ys = jax.lax.scan(step, init, (tm(u), tm(dt), tm(kd), tm(Bz), tm(Bx), tm(Cz), tm(Cx)))
            y = jnp.moveaxis(ys, 0, 1).reshape(Bsz, Tlen, DI)
            y = (y + skip * value) * jax.nn.silu(gate)
            return jnp.einsum('bti,oi->bto', y, W_out)
        key = jax.random.key(seed)
        ks = jax.random.split(key, 8)
        n = lambda k, sh, s=1.0: jax.random.normal(k, sh, jnp.float32) * s
        return {'x': n(ks[0], (B, T, D_MODEL)), 'W_in': n(ks[1], (2 * D_INNER + N_HEADS * 2, D_MODEL), D_MODEL ** (-0.5)), 'dw_weight': n(ks[2], (D_INNER, D_CONV), D_CONV ** (-0.5)), 'dw_bias': n(ks[3], (D_INNER,), 0.1), 'W_bc': n(ks[4], (N_HEADS * 4 * D_STATE, D_INNER), D_INNER ** (-0.5)), 'W_out': n(ks[5], (D_MODEL, D_INNER), D_INNER ** (-0.5)), 'skip': jnp.ones((D_INNER,), jnp.float32), 'A_log': n(ks[6], (N_HEADS, D_STATE), 0.5), 'dt_bias': n(ks[7], (N_HEADS,), 0.5)}
    _L0_attn_all = _L0_attn_setup()
    _L0_attn_in = {k: v for k, v in _L0_attn_all.items() if k in ('W_in', 'dw_weight', 'dw_bias', 'W_bc', 'W_out', 'skip', 'A_log', 'dt_bias')}
    del _L0_attn_all

    def _L0_xattn_setup():
        import jax, jax.numpy as jnp
        import numpy as np
        B, L, D = (8, 256, 128)
        key = jax.random.key(seed)
        ks = jax.random.split(key, 9)
        scale = 1.0 / np.sqrt(D)
        return {'query_source': jax.random.normal(ks[0], (B, L, D), dtype=jnp.float32), 'key_source': jax.random.normal(ks[1], (B, L, D), dtype=jnp.float32), 'value_source': jax.random.normal(ks[2], (B, L, D), dtype=jnp.float32), 'Wq': jax.random.normal(ks[3], (D, D), dtype=jnp.float32) * scale, 'bq': jnp.zeros((D,), dtype=jnp.float32), 'Wk': jax.random.normal(ks[4], (D, D), dtype=jnp.float32) * scale, 'bk': jnp.zeros((D,), dtype=jnp.float32), 'Wv': jax.random.normal(ks[5], (D, D), dtype=jnp.float32) * scale, 'bv': jnp.zeros((D,), dtype=jnp.float32)}
    _L0_xattn_all = _L0_xattn_setup()
    _L0_xattn_in = {k: v for k, v in _L0_xattn_all.items() if k in ('Wq', 'bq', 'Wk', 'bk', 'Wv', 'bv')}
    del _L0_xattn_all

    def _L0_ffn_setup():
        import jax, jax.numpy as jnp
        import numpy as np
        S, B, D = (128, 2, 128)
        E, TOPK = (15, 3)
        F = 128
        FS = 256

        def _uinit(k, shape, out_dim):
            std = out_dim ** (-0.5)
            return jax.random.uniform(k, shape, jnp.float32, -std, std)
        key = jax.random.key(seed)
        ks = jax.random.split(key, 10)
        return {'x': jax.random.normal(ks[0], (S, B, D), jnp.float32), 'gate_w': jax.random.normal(ks[1], (E, D), jnp.float32) * D ** (-0.5), 'fc1_w': _uinit(ks[2], (E, 2 * F, D), 2 * F), 'fc1_b': _uinit(ks[3], (E, 2 * F), 2 * F), 'geglu_mult': jnp.ones((E, F), jnp.float32), 'fc2_w': _uinit(ks[4], (E, D, F), D), 'fc2_b': _uinit(ks[5], (E, D), D), 's_fc1_w': _uinit(ks[6], (2 * FS, D), 2 * FS), 's_fc1_b': _uinit(ks[7], (2 * FS,), 2 * FS), 's_geglu_mult': jnp.ones((FS,), jnp.float32), 's_fc2_w': _uinit(ks[8], (D, FS), D), 's_fc2_b': _uinit(ks[9], (D,), D)}
    _L0_ffn_all = _L0_ffn_setup()
    _L0_ffn_in = {k: v for k, v in _L0_ffn_all.items() if k in ('gate_w', 'fc1_w', 'fc1_b', 'geglu_mult', 'fc2_w', 'fc2_b', 's_fc1_w', 's_fc1_b', 's_geglu_mult', 's_fc2_w', 's_fc2_b')}
    del _L0_ffn_all
    return {'x': x, 'ctx_1024': ctx_1024, 'L0_attn_W_in': _L0_attn_in['W_in'], 'L0_attn_dw_weight': _L0_attn_in['dw_weight'], 'L0_attn_dw_bias': _L0_attn_in['dw_bias'], 'L0_attn_W_bc': _L0_attn_in['W_bc'], 'L0_attn_W_out': _L0_attn_in['W_out'], 'L0_attn_skip': _L0_attn_in['skip'], 'L0_attn_A_log': _L0_attn_in['A_log'], 'L0_attn_dt_bias': _L0_attn_in['dt_bias'], 'L0_xattn_Wq': _L0_xattn_in['Wq'], 'L0_xattn_bq': _L0_xattn_in['bq'], 'L0_xattn_Wk': _L0_xattn_in['Wk'], 'L0_xattn_bk': _L0_xattn_in['bk'], 'L0_xattn_Wv': _L0_xattn_in['Wv'], 'L0_xattn_bv': _L0_xattn_in['bv'], 'L0_ffn_gate_w': _L0_ffn_in['gate_w'], 'L0_ffn_fc1_w': _L0_ffn_in['fc1_w'], 'L0_ffn_fc1_b': _L0_ffn_in['fc1_b'], 'L0_ffn_geglu_mult': _L0_ffn_in['geglu_mult'], 'L0_ffn_fc2_w': _L0_ffn_in['fc2_w'], 'L0_ffn_fc2_b': _L0_ffn_in['fc2_b'], 'L0_ffn_s_fc1_w': _L0_ffn_in['s_fc1_w'], 'L0_ffn_s_fc1_b': _L0_ffn_in['s_fc1_b'], 'L0_ffn_s_geglu_mult': _L0_ffn_in['s_geglu_mult'], 'L0_ffn_s_fc2_w': _L0_ffn_in['s_fc2_w'], 'L0_ffn_s_fc2_b': _L0_ffn_in['s_fc2_b']}

def reference(x, ctx_1024, L0_attn_W_in, L0_attn_dw_weight, L0_attn_dw_bias, L0_attn_W_bc, L0_attn_W_out, L0_attn_skip, L0_attn_A_log, L0_attn_dt_bias, L0_xattn_Wq, L0_xattn_bq, L0_xattn_Wk, L0_xattn_bk, L0_xattn_Wv, L0_xattn_bv, L0_ffn_gate_w, L0_ffn_fc1_w, L0_ffn_fc1_b, L0_ffn_geglu_mult, L0_ffn_fc2_w, L0_ffn_fc2_b, L0_ffn_s_fc1_w, L0_ffn_s_fc1_b, L0_ffn_s_geglu_mult, L0_ffn_s_fc2_w, L0_ffn_s_fc2_b):
    import jax
    import jax.numpy as jnp

    def _L0_attn_ref(x, W_in, dw_weight, dw_bias, W_bc, W_out, skip, A_log, dt_bias):
        import jax, jax.numpy as jnp
        import numpy as np
        B, T, D_MODEL = (2, 64, 128)
        D_INNER, D_HEAD, D_CONV = (256, 64, 4)
        N_HEADS, D_STATE = (32, 32)
        DT_MIN, DT_MAX, K_MAX, EPS = (0.0001, 0.1, 0.5, 1e-08)

        def _forward(x, W_in, dw_weight, dw_bias, W_bc, W_out, skip, A_log, dt_bias):
            Bsz, Tlen, D = x.shape
            DI, K = dw_weight.shape
            H, N = A_log.shape
            DH = DI // H
            proj = jnp.einsum('btd,od->bto', x, W_in)
            gate = proj[..., :DI]
            value_raw = proj[..., DI:2 * DI]
            params = proj[..., 2 * DI:].reshape(Bsz, Tlen, H, 2)
            xp = jnp.pad(value_raw, ((0, 0), (K - 1, 0), (0, 0)))
            conv = dw_bias + sum((xp[:, k:k + Tlen, :] * dw_weight[:, k] for k in range(K)))
            value = jax.nn.silu(conv)
            dt = jnp.clip(jax.nn.softplus(params[..., 0] + dt_bias), DT_MIN, DT_MAX)
            kd = K_MAX * jax.nn.sigmoid(params[..., 1])
            A = jnp.exp(A_log)
            bc = jnp.einsum('bti,oi->bto', value, W_bc).reshape(Bsz, Tlen, H, 4, N)
            bc = bc / (jnp.sqrt(jnp.sum(bc * bc, axis=-1, keepdims=True)) + EPS)
            Bz, Bx, Cz, Cx = (bc[..., 0, :], bc[..., 1, :], bc[..., 2, :], bc[..., 3, :])
            u = value.reshape(Bsz, Tlen, H, DH)

            def step(carry, inp):
                z, s = carry
                u_t, dt_t, k_t, Bz_t, Bx_t, Cz_t, Cx_t = inp
                dtE = dt_t[:, :, None, None]
                S = 1.0 / (1.0 + dt_t[..., None] * k_t[..., None] + (dt_t * dt_t)[..., None] * A)
                z = S[..., None] * (z - dtE * A[None, :, :, None] * s + dtE * (Bz_t[..., None] * u_t[:, :, None, :]))
                s = s + dtE * z + dtE * (Bx_t[..., None] * u_t[:, :, None, :])
                y = jnp.einsum('bhn,bhnd->bhd', Cz_t, z) + jnp.einsum('bhn,bhnd->bhd', Cx_t, s)
                return ((z, s), y)
            tm = lambda a: jnp.moveaxis(a, 1, 0)
            init = (jnp.zeros((Bsz, H, N, DH), x.dtype), jnp.zeros((Bsz, H, N, DH), x.dtype))
            _, ys = jax.lax.scan(step, init, (tm(u), tm(dt), tm(kd), tm(Bz), tm(Bx), tm(Cz), tm(Cx)))
            y = jnp.moveaxis(ys, 0, 1).reshape(Bsz, Tlen, DI)
            y = (y + skip * value) * jax.nn.silu(gate)
            return jnp.einsum('bti,oi->bto', y, W_out)
        return _forward(x, W_in, dw_weight, dw_bias, W_bc, W_out, skip, A_log, dt_bias)

    def _L0_xattn_ref(query_source, key_source, value_source, Wq, bq, Wk, bk, Wv, bv):
        import jax, jax.numpy as jnp
        import numpy as np
        B, L, D = (8, 256, 128)
        q = query_source @ Wq + bq
        k = key_source @ Wk + bk
        v = value_source @ Wv + bv
        scores = jnp.einsum('bqd,bkd->bqk', q, k)
        attn = jax.nn.softmax(scores, axis=-1)
        out = jnp.einsum('bqk,bkd->bqd', attn, v)
        return out

    def _L0_ffn_ref(x, gate_w, fc1_w, fc1_b, geglu_mult, fc2_w, fc2_b, s_fc1_w, s_fc1_b, s_geglu_mult, s_fc2_w, s_fc2_b):
        import jax, jax.numpy as jnp
        import numpy as np
        S, B, D = (128, 2, 128)
        E, TOPK = (15, 3)
        F = 128
        FS = 256

        def _uinit(k, shape, out_dim):
            std = out_dim ** (-0.5)
            return jax.random.uniform(k, shape, jnp.float32, -std, std)
        s, b, d = x.shape
        xt = x.reshape(-1, d)
        T = xt.shape[0]
        logits = xt @ gate_w.T
        scores = jax.nn.softmax(logits, axis=-1)
        topk_w, topk_idx = jax.lax.top_k(scores, TOPK)
        topk_w = topk_w / (jnp.sum(topk_w, axis=-1, keepdims=True) + 1e-20)
        comb = jnp.zeros((T, E), xt.dtype).at[jnp.arange(T)[:, None], topk_idx].add(topk_w)
        h = jnp.einsum('td,efd->etf', xt, fc1_w) + fc1_b[:, None, :]
        xh, g = (h[..., :F], h[..., F:])
        a = jax.nn.gelu(g, approximate=False) * xh * geglu_mult[:, None, :]
        yexp = jnp.einsum('etf,edf->etd', a, fc2_w) + fc2_b[:, None, :]
        y = jnp.einsum('etd,te->td', yexp, comb)
        hs = xt @ s_fc1_w.T + s_fc1_b
        xs, gs = (hs[..., :FS], hs[..., FS:])
        as_ = jax.nn.gelu(gs, approximate=False) * xs * s_geglu_mult
        ys = as_ @ s_fc2_w.T + s_fc2_b
        return (y + ys).reshape(s, b, d)
    x = _layernorm(x + _L0_attn_ref(x, L0_attn_W_in, L0_attn_dw_weight, L0_attn_dw_bias, L0_attn_W_bc, L0_attn_W_out, L0_attn_skip, L0_attn_A_log, L0_attn_dt_bias), axis=-1)
    x = _layernorm(x + _L0_xattn_ref(x, ctx_1024, ctx_1024, L0_xattn_Wq, L0_xattn_bq, L0_xattn_Wk, L0_xattn_bk, L0_xattn_Wv, L0_xattn_bv), axis=-1)
    x = _layernorm(x + _L0_ffn_ref(x, L0_ffn_gate_w, L0_ffn_fc1_w, L0_ffn_fc1_b, L0_ffn_geglu_mult, L0_ffn_fc2_w, L0_ffn_fc2_b, L0_ffn_s_fc1_w, L0_ffn_s_fc1_b, L0_ffn_s_geglu_mult, L0_ffn_s_fc2_w, L0_ffn_s_fc2_b), axis=-1)
    return x

_drawn_inputs = setup_inputs


def setup_inputs(seed=0):
    import zlib

    import numpy as np

    out = dict(_drawn_inputs(seed))
    spreads = {'L0_attn_skip': (1.0, 0.2),
     'L0_xattn_bq': (0.0, 0.1),
     'L0_xattn_bk': (0.0, 0.8),
     'L0_xattn_bv': (0.0, 0.1),
     'L0_ffn_geglu_mult': (1.0, 0.6),
     'L0_ffn_s_geglu_mult': (1.0, 0.6)}
    factors = {'L0_attn_dt_bias': 7.063, 'L0_ffn_fc1_b': 8.0, 'L0_ffn_s_fc1_b': 8.0}
    for name, (base, spread) in spreads.items():
        noise = np.random.default_rng([zlib.crc32(name.encode()), seed]).standard_normal(out[name].shape)
        drawn = base * np.exp(spread * noise) if base else spread * noise
        out[name] = jnp.asarray(drawn.astype(out[name].dtype))
    for name, factor in factors.items():
        out[name] = (out[name] * factor).astype(out[name].dtype)
    return out
```

```python
import concourse.bass as bass
from concourse import mybir
from contextlib import ExitStack

B, T, D = 4, 512, 128
DI, H, NS, DH, KW = 256, 32, 32, 8, 4
L = 32
NC = T // L
HG = 4
G = H // HG
TT = T // 128
CT = 128 // L
S = 154
SH = S // 2
E, F, TOPK = 15, 128, 3
NE = E + 2
DT_MIN, DT_MAX, K_MAX = 1e-4, 0.1, 0.5
EXP_CAP = 0.106
LOG_TERMS = 9
EPS_NORM, EPS_LN, EPS_TOP = 1e-8, 1e-5, 1e-20
BZ, BX, CZ, CX = range(4)
ORDER = [E, E + 1] + list(range(E))
LN_STEPS = 2 * TT + 1 + TT
DT_STEPS = 2 + (LOG_TERMS - 1) + 4
REC_STEPS = 3 + 4 * (L - 1)
RN_STEPS = 3
MAIN_STEPS = 10
STATE_STEPS = 4
X_STEPS = 1 + TT + LN_STEPS
ROUTE_STEPS = 4 + TT + 2 + TT + 4
ACC_STEPS = 1 + TT * E + LN_STEPS
ZZ, ZS, SZ, SS = range(4)


class Counts:

    def __init__(self):
        self.value = {}

    def one(self, sem):
        self.value[sem.num] = self.value.get(sem.num, 0) + 1
        return 1

    def made(self, sem):
        return self.value.get(sem.num, 0)


def ring_orders():
    act = [("dt",), ("kd",), ("val", 0), ("val", 1)]
    for g in range(G):
        act += [("na", g), ("dtb", g)]
    act += [("ut", 0), ("ut", 1)] + [("w", g) for g in range(G)]
    act += [("nrm", g, c) for g in range(G) for c in range(4)]
    for g in range(3):
        act += [("bc", g, c) for c in range(4)]
    for g in range(G):
        act += [("kt", g, j) for j in range(2)]
        if g + 3 < G:
            act += [("bc", g + 3, c) for c in range(4)]
    dve = [("c", g) for g in range(G)] + [("ub", k) for k in range(NC // 2)]
    for g in range(3):
        dve += [("rn", g, c) for c in (BX, CZ, CX, BZ)]
    for g in range(G):
        dve.append(("g", g))
        if g + 3 < G:
            dve += [("rn", g + 3, c) for c in (BX, CZ, CX, BZ)]
    return act, dve


def build(nc, xT, x, ctxT, WinT, Wbc, WoutT, skip, A_log, dtb, cw, cb, Wq, bq, Wk, bk, Wv, bv,
          gwT, fc1T, fcol, fc2T, fc2b, heads, onehot, tiled_eye, causal, chunk_on, own_head,
          eye, out):
    f32 = mybir.dt.float32
    ALU = mybir.AluOpType
    ACT = mybir.ActivationFunctionType
    AX = mybir.AxisListType.X
    ctx = ExitStack()
    with ctx:
        def sb(name, *shape):
            return ctx.enter_context(nc.sbuf_tensor(name, list(shape), f32))

        signals = []
        counts = Counts()
        one, made = counts.one, counts.made

        def sig(name):
            s = ctx.enter_context(nc.semaphore(name))
            signals.append(s)
            return s

        heads_sb = sb("heads_sb", 128, H * NS)
        coef_w = sb("coef_w", 128, H * NS)
        onehot_sb = sb("onehot_sb", 128, 252)
        tiled_sb = sb("tiled_sb", 128, 128)
        causal_sb = sb("causal_sb", 128, L)
        chunk_sb = sb("chunk_sb", 128, T)
        own_sb = sb("own_sb", 128, HG)
        eye_sb = sb("eye_sb", 128, 128)
        win_sb = sb("win_sb", 128, 768)
        wout_sb = sb("wout_sb", 128, 2, 128)
        skip_sb = sb("skip_sb", 128, DI)
        dtb_sb = sb("dtb_sb", 128, 1)
        cw_sb = sb("cw_sb", 128, 2, KW)
        cb_sb = sb("cb_sb", 128, 2)
        wqkv_sb = sb("wqkv_sb", 128, 3, 128)
        bqk_sb = sb("bqk_sb", 128, 2)
        bv_sb = sb("bv_sb", 1, 128)
        ones_sb = sb("ones_sb", 1, 128)
        gw_sb = sb("gw_sb", 128, E)
        eps_sb = sb("eps_sb", 128, 1)

        x_in = sb("x_in", 128, T)
        NT = sb("NT", 128, 4, G * T)
        coef = sb("coef", 128, 2, G * T)
        dt_rep = sb("dt_rep", 128, G * T)
        winv = sb("winv", 128, G * T)
        raw_sb = sb("raw_sb", 128, 2, 4, T)
        wbc_sb = sb("wbc_sb", 128, 2, 4, 2, 128)
        vT = sb("vT", 128, 2, T)
        u_tok = sb("u_tok", 128, TT, DI)
        prod = sb("prod", 128, 2, 2, T)
        nag = sb("nag", 128, 2, T)
        small = sb("small", 128, T)
        rn = sb("rn", 128, T)
        phi = sb("phi", 128, 4, G * NC)
        xres = sb("xres", 128, TT, D)
        stats = sb("stats", 128, TT, 6)
        mv = sb("mv", 128, TT, 2)
        rstd = sb("rstd", 128, TT)

        v_pad = prod[:, :, :, :].rearrange("p a b t -> p (a b t)")[:, 0:2 * (T + 3)] \
            .rearrange("p (h t) -> p h t", h=2)
        prodf = prod[:, :, :, :].rearrange("p a b t -> p (a b t)")
        step_a = prodf[:, 0:512].rearrange("p (r j m) -> p r j m", r=2, j=2)
        step_b = prodf[:, 512:1024].rearrange("p (s j m) -> p s j m", s=2, j=2)
        dX = coef[:, 0, 0:2048].rearrange("p (c m) -> p c m", c=NC)
        X = coef[:, 0, 2048:2304].rearrange("p (s j m) -> p s j m", s=2, j=2)
        st = coef[:, 0, 2304:2688].rearrange("p (s j m) -> p s j m", s=3, j=2)
        conv = raw_sb[:, 0, 0:2, :]
        exp_dt = raw_sb[:, 1, 0, :]
        sig_k = raw_sb[:, 1, 1, :]
        log_p = raw_sb[:, 1, 2, :]
        sq = nag
        u_bd = dt_rep
        gm = winv
        kT_sb = coef[:, 1, 0:4 * 512].rearrange("p (s c t k) -> p s c t k", s=2, c=2, t=TT)
        raw3 = coef[:, 1, 2048:4096].rearrange("p (c t) -> p c t", c=4)
        x_bd = prod[:, :, :, :].rearrange("p s a t -> p s (a t)")[:, :, 0:512]
        wide = raw_sb[:, :, :, :].rearrange("p s c t -> p (s c t)")
        su = wide[:, 0:1024].rearrange("p (t i) -> p t i", t=TT)
        sg = wide[:, 1024:2048].rearrange("p (t i) -> p t i", t=TT)
        yf = wide[:, 2048:3072].rearrange("p (t i) -> p t i", t=TT)
        yfT = wide[:, 3072:4096].rearrange("p (k t) -> p k t", k=2)

        def raw(g):
            return raw3 if g % 3 == 2 else raw_sb[:, g % 3]

        NTf = NT[:, :, :].rearrange("p a t -> p (a t)")
        at = [0]

        def over(n):
            at[0] += n
            return NTf[:, at[0] - n:at[0]]

        fc1_sb = over(NE * 256).rearrange("p (e f) -> p e f", e=NE)
        fc2_raw = over(NE * 128).rearrange("p (e f) -> p e f", e=NE)
        coeff = coef[:, :, :].rearrange("p a t -> p (a t)")
        at2 = [0]

        def over2(n):
            at2[0] += n
            return coeff[:, at2[0] - n:at2[0]]

        fc2_sb = over2(NE * 128).rearrange("p (e f) -> p e f", e=NE)
        fb_sb = over2(NE * 3).rearrange("p (e f) -> p e f", e=NE)
        fcb_sb = over2(128)
        ctx_sb = over2(S)
        x1T = over2(T)
        qT = over2(T)
        kcT = over2(S)
        v_sb = over2(2 * 128).rearrange("p (j d) -> p j d", j=2)
        probs = over2(TT * S).rearrange("p (t s) -> p t s", t=TT)
        pT = over2(TT * 2 * 128).rearrange("p (t j q) -> p t j q", t=TT, j=2)
        x2T = over2(T)
        combT = over2(T)
        ga = dt_rep[:, 0:1024].rearrange("p (s t) -> p s t", s=2)
        act_a = dt_rep[:, 1024:2048].rearrange("p (s t) -> p s t", s=2)
        acc = dt_rep[:, 2048:2560].rearrange("p (t d) -> p t d", t=TT)
        tiny = dt_rep[:, 2560:3072]
        negmax = tiny[:, 0:4]
        sums = tiny[:, 4:8]
        rsum = tiny[:, 8:12]
        score = tiny[:, 16:16 + TT * E].rearrange("p (t e) -> p t e", t=TT)
        top8 = tiny[:, 80:112].rearrange("p (t e) -> p t e", t=TT)
        left = tiny[:, 112:112 + TT * E].rearrange("p (t e) -> p t e", t=TT)
        comb = tiny[:, 176:240].rearrange("p (t e) -> p t e", t=TT)
        topsum = tiny[:, 240:244]
        gmax = tiny[:, 244:248]
        gsum = tiny[:, 248:252]
        grec = tiny[:, 252:256]

        P = [ctx.enter_context(nc.psum_tensor(f"bank{i}", [128, 512], f32)) for i in range(8)]

        consts_in = sig("consts_in")
        prep_act = sig("prep_act")
        prep_dve = sig("prep_dve")
        prep_pool = sig("prep_pool")
        x_loaded = sig("x_loaded")
        wbc_loaded = [sig("wbc_loaded0"), sig("wbc_loaded1")]
        a_full = sig("a_full")
        a_free = sig("a_free")
        v_full = sig("v_full")
        v_free = sig("v_free")
        pads = sig("pads")
        dt_steps = sig("dt_steps")
        conv_steps = sig("conv_steps")
        silu_done = sig("silu_done")
        rec_steps = sig("rec_steps")
        sums_done = sig("sums_done")
        inv_done = sig("inv_done")
        norm_acc = sig("norm_acc")
        norm_root = sig("norm_root")
        rn_steps = sig("rn_steps")
        pool_main = sig("pool_main")
        main_steps = sig("main_steps")
        phi_done = sig("phi_done")
        dx_psum = sig("dx_psum")
        dx_done = sig("dx_done")
        gate_full = sig("gate_full")
        gate_done = sig("gate_done")
        su_done = sig("su_done")
        state_steps = sig("state_steps")
        xbd_done = sig("xbd_done")
        y_done = sig("y_done")
        yf_steps = sig("yf_steps")
        yft_full = sig("yft_full")
        yft_done = sig("yft_done")
        mix_full = sig("mix_full")
        ln_steps = sig("ln_steps")
        ln_root = sig("ln_root")
        ub_first = sig("ub_first")

        ffn_in = sig("ffn_in")
        x1_full = sig("x1_full")
        x1_done = sig("x1_done")
        qkv_full = sig("qkv_full")
        qkv_done = sig("qkv_done")
        s_full = sig("s_full")
        s_max = sig("s_max")
        p_done = sig("p_done")
        pt_full = sig("pt_full")
        pt_done = sig("pt_done")
        o_full = sig("o_full")
        x_steps = sig("x_steps")
        ln2_root = sig("ln2_root")
        x2_full = sig("x2_full")
        x2_done = sig("x2_done")
        lg_full = sig("lg_full")
        lg_exp = sig("lg_exp")
        route = sig("route")
        ct_full = sig("ct_full")
        ct_done = sig("ct_done")
        hg_full = sig("hg_full")
        hx_full = sig("hx_full")
        gelu_done = sig("gelu_done")
        glu_done = sig("glu_done")
        base = sig("base")
        e_full = sig("e_full")
        acc_steps = sig("acc_steps")
        ln3_root = sig("ln3_root")
        scaled = sig("scaled")
        stored = sig("stored")

        act_ring, dve_ring = ring_orders()
        a_at = {k: i for i, k in enumerate(act_ring)}
        v_at = {k: i for i, k in enumerate(dve_ring)}

        def a_bank(key):
            return P[a_at[key] % 2]

        def v_bank(key):
            return P[2 + v_at[key] % 2]

        def grp(g):
            return slice(g * T, (g + 1) * T)

        def layer_norm(dve, steps, root, src, dst):
            if made(steps):
                dve.wait_ge(steps, made(steps))
            for t in range(TT):
                dve.bn_stats(stats[:, t, :], src[:, t, :]).then_inc(steps, one(steps))
            dve.wait_ge(steps, made(steps))
            for t in range(TT):
                dve.bn_aggr(mv[:, t, :], stats[:, t, :]).then_inc(steps, one(steps))
            dve.wait_ge(root, 1)
            dve.reciprocal(rstd[:, :], rstd[:, :]).then_inc(steps, one(steps))
            dve.wait_ge(steps, made(steps))
            for t in range(TT):
                dve.tensor_scalar(dst[:, t, :], src[:, t, :], mv[:, t, 0:1], rstd[:, t:t + 1],
                                           ALU.subtract, ALU.mult).then_inc(steps, one(steps))

        CONSTS = [(heads_sb, heads), (onehot_sb, onehot), (tiled_sb, tiled_eye), (causal_sb, causal),
                  (chunk_sb, chunk_on), (own_sb, own_head), (eye_sb, eye), (win_sb, WinT),
                  (dtb_sb, dtb), (cb_sb, cb), (gw_sb, gwT), (bv_sb, bv)]

        a_in = raw_sb[:, 0, 0, 0:NS]
        a_exp = raw_sb[:, 0, 1, 0:NS]
        n_in = 16 * (len(CONSTS) + 10)
        with nc.Block() as block:
            @block.sync
            def _(sp):
                for dst, src in CONSTS:
                    sp.dma_start(dst[:, :], src).then_inc(consts_in, 16)
                sp.dma_start(wout_sb[:, :, :], WoutT).then_inc(consts_in, 16)
                sp.dma_start(skip_sb[:, :], skip.partition_broadcast(128)).then_inc(consts_in, 16)
                sp.dma_start(cw_sb[:, :, :], cw).then_inc(consts_in, 16)
                for j, w in enumerate((Wq, Wk, Wv)):
                    sp.dma_start(wqkv_sb[:, j, :], w).then_inc(consts_in, 16)
                sp.dma_start(bqk_sb[:, 0:1], bq).then_inc(consts_in, 16)
                sp.dma_start(bqk_sb[:, 1:2], bk).then_inc(consts_in, 16)
                sp.wait_ge(prep_dve, 1)
                sp.dma_start(a_in[0:32, :], A_log).then_inc(consts_in, 16)
                sp.dma_start(a_in[96:128, :], A_log).then_inc(consts_in, 16)

            @block.gpsimd
            def _(pool):
                pool.memset(ones_sb[:, :], 1.0).then_inc(prep_pool, 1)

            @block.vector
            def _(dve):
                dve.memset(a_in, 0.0).then_inc(prep_dve, one(prep_dve))
                dve.memset(eps_sb[:, :], EPS_LN).then_inc(prep_dve, one(prep_dve))
                dve.wait_ge(prep_act, 1)
                dve.wait_ge(consts_in, n_in)
                dve.tensor_tensor(
                    coef_w[:, :].rearrange("p (h n) -> p h n", h=H),
                    heads_sb[:, :].rearrange("p (h n) -> p h n", h=H),
                    a_exp.unsqueeze(1).to_broadcast([128, H, NS]), ALU.mult).then_inc(prep_dve, one(prep_dve))
                dve.wait_ge(prep_dve, made(prep_dve))
                dve.tensor_scalar(coef_w[0:32, :], coef_w[0:32, :], -1.0, None, ALU.mult).then_inc(prep_dve, one(prep_dve))

            @block.scalar
            def _(act):
                act.wait_ge(consts_in, n_in)
                act.activation(a_exp, a_in, ACT.Exp).then_inc(prep_act, 1)

        nc.all_engine_barrier()

        with nc.Fori(0, B) as b:
            with nc.Block() as block:
                @block.sync
                def _(sp):
                    sp.dma_start(x_in[:, :], xT[:, bass.ds(b * T, T)]).then_inc(x_loaded, 16)
                    sp.dma_start(
                        xres[:, :, :], x[bass.ds(b * T, T), :].rearrange("(t p) d -> p t d", p=128)).then_inc(x_loaded, 16)
                    for k in range(2 * G):
                        if k >= 2:
                            used = ("nrm", k - 2, 3) if k - 2 < G else ("bc", k - 2 - G, 3)
                            sp.wait_ge(a_full, a_at[used] + 1)
                        sp.dma_start(
                            wbc_sb[:, k % 2].rearrange("p c k m -> p (c k m)"),
                            Wbc[(k % G) * 128:(k % G) * 128 + 128, :]).then_inc(wbc_loaded[k % 2], 16)

                @block.tensor
                def _(pe):
                    def ring_a(key, weights, moving):
                        k = a_at[key]
                        if k >= 2:
                            pe.wait_ge(a_free, k - 1)
                        pe.matmul(P[k % 2][:, :], weights, moving, start=True, stop=True).then_inc(a_full, 1)

                    def ring_v(key, weights, moving):
                        k = v_at[key]
                        if k >= 2:
                            pe.wait_ge(v_free, k - 1)
                        pe.matmul(P[2 + k % 2][:, :], weights, moving, start=True,
                                  stop=True).then_inc(v_full, 1)

                    pe.wait_ge(x_loaded, 32)
                    for key, col in ((("dt",), 512), (("kd",), 640), (("val", 0), 256), (("val", 1), 384)):
                        ring_a(key, win_sb[:, col:col + 128], x_in[:, :])

                    pe.wait_ge(dt_steps, DT_STEPS)
                    for g in range(G):
                        cols = slice(g * 128, g * 128 + 128)
                        ring_a(("na", g), coef_w[0:32, cols], small[0:32, :])
                        ring_a(("dtb", g), heads_sb[0:32, cols], small[0:32, :])
                        ring_v(("c", g), heads_sb[64:96, cols], small[64:96, :])
                    pe.wait_ge(silu_done, 2)
                    for j in range(2):
                        pe.wait_ge(a_free, a_at[("ut", j)] - 1)
                        for t in (2 * j, 2 * j + 1):
                            for h in range(2):
                                last = pe.transpose(
                                    a_bank(("ut", j))[:, (t % 2) * 256 + h * 128:(t % 2) * 256 + h * 128 + 128],
                                    vT[:, h, t * 128:t * 128 + 128], eye_sb[:, :])
                        last.then_inc(a_full, 1)
                    for g in range(G):
                        cols = slice(g * 128, g * 128 + 128)
                        ring_a(("w", g), coef_w[64:128, cols], small[64:128, :])

                    def bc(kind, g, c, k):
                        key = (kind, g, c)
                        o = a_bank(key)
                        if c == 0:
                            pe.wait_ge(wbc_loaded[k % 2], 16 * (k // 2 + 1))
                        pe.wait_ge(a_free, a_at[key] - 1)
                        pe.matmul(o[:, :], wbc_sb[:, k % 2, c, 0, :], vT[:, 0, :], start=True, stop=False)
                        pe.matmul(o[:, :], wbc_sb[:, k % 2, c, 1, :], vT[:, 1, :], start=False,
                                  stop=True).then_inc(a_full, 1)

                    def norm_sum(n):
                        g, c = divmod(n, 4)
                        off = 124 - (c * 32 + g * HG)
                        pe.wait_ge(a_free, a_at[("nrm", g, c)] + 1)
                        pe.matmul(P[4][:, :], onehot_sb[:, off:off + 128], sq[:, n % 2, :],
                                              start=(n == 0), stop=(n == 4 * G - 1)).then_inc(norm_acc, 1)

                    for n in range(4 * G):
                        bc("nrm", n // 4, n % 4, n // 4)
                        if n >= 1:
                            norm_sum(n - 1)
                    norm_sum(4 * G - 1)

                    def u_blocks():
                        pe.wait_ge(a_free, a_at[("ut", 1)] + 1)
                        for k in range(NC // 2):
                            o = v_bank(("ub", k))
                            pe.wait_ge(v_free, v_at[("ub", k)] - 1)
                            for i in range(2):
                                ch = 2 * k + i
                                r = 32 * (ch % CT)
                                if i:
                                    pe.wait_ge(ub_first, k + 1)
                                ins = pe.matmul(o[:, i * DI:(i + 1) * DI], tiled_sb[r:r + 32, :],
                                                u_tok[r:r + 32, ch // CT, :], start=True, stop=True)
                                ins.then_inc((v_full if i else ub_first), 1)

                    u_blocks()

                    def rn_cast(g):
                        pe.wait_ge(rn_steps, RN_STEPS)
                        for c in (BX, CZ, CX, BZ):
                            ring_v(("rn", g, c), heads_sb[32 * c:32 * c + 32, g * 128:g * 128 + 128],
                                   rn[32 * c:32 * c + 32, :])

                    def bc_main(g):
                        for c in range(4):
                            bc("bc", g, c, G + g)

                    def kt(g):
                        pe.wait_ge(main_steps, MAIN_STEPS * (g + 1))
                        for j in range(2):
                            o = a_bank(("kt", g, j))
                            pe.wait_ge(a_free, a_at[("kt", g, j)] - 1)
                            for t in range(TT):
                                last = pe.transpose(
                                    o[:, t * 128:t * 128 + 128],
                                    NT[:, 2 + j, g * T + t * 128:g * T + t * 128 + 128], eye_sb[:, :])
                            last.then_inc(a_full, 1)

                    def attend(g):
                        o = v_bank(("g", g))
                        pe.wait_ge(v_free, v_at[("g", g)] - 1)
                        for ch in range(NC):
                            s = slice(g * T + ch * L, g * T + ch * L + L)
                            for j in range(2):
                                for h in range(HG):
                                    r = slice(32 * h, 32 * h + 32)
                                    last = pe.matmul(o[r, ch * L:ch * L + L], NT[r, 2 + j, s], NT[r, j, s],
                                                     start=(j == 0), stop=(j == 1))
                        last.then_inc(v_full, 1)

                    def chunk_inputs(g):
                        pe.wait_ge(a_free, a_at[("kt", g, 1)] + 1)
                        if g == 0:
                            pe.wait_ge(norm_root, 1)
                        for t in range(TT):
                            for j in range(2):
                                for h in range(HG):
                                    for c in range(CT):
                                        r = slice(32 * c, 32 * c + 32)
                                        col = t * 128 + j * G * DH + g * DH
                                        last = pe.matmul(
                                            P[4 + c][32 * h:32 * h + 32, col:col + DH],
                                            kT_sb[r, g % 2, j, t, 32 * h:32 * h + 32],
                                            u_tok[r, t, (g * HG + h) * DH:(g * HG + h + 1) * DH],
                                            start=True, stop=True)
                        last.then_inc(dx_psum, 1)

                    for g in range(3):
                        bc_main(g)
                        rn_cast(g)
                    for g in range(G):
                        kt(g)
                        attend(g)
                        if g + 3 < G:
                            bc_main(g + 3)
                            rn_cast(g + 3)
                        chunk_inputs(g)

                    pe.wait_ge(v_free, len(dve_ring))
                    for j in range(2):
                        for t in (2 * j, 2 * j + 1):
                            last = pe.matmul(P[2 + j][:, (t % 2) * DI:(t % 2 + 1) * DI],
                                             x_in[:, t * 128:t * 128 + 128], win_sb[:, 0:DI],
                                             start=True, stop=True)
                        last.then_inc(gate_full, 1)

                    pe.wait_ge(a_free, len(act_ring))
                    for ch in range(NC):
                        t, c = divmod(ch, CT)
                        o = P[t // 2]
                        if ch:
                            pe.wait_ge(xbd_done, HG * ch)
                        for g in range(G):
                            col = (t % 2) * DI + g * 32
                            oo = o[32 * c:32 * c + 32, col:col + 32]
                            s = slice(g * T + ch * L, g * T + ch * L + L)
                            last = pe.matmul(oo, gm[:, s], u_bd[:, ch * DI + g * 32:ch * DI + g * 32 + 32],
                                             start=True, stop=(ch == 0))
                            if ch:
                                for j in range(2):
                                    last = pe.matmul(oo, NT[:, j, s],
                                                     x_bd[:, ch % 2, (j * G + g) * 32:(j * G + g) * 32 + 32],
                                                     start=False, stop=(j == 1))
                        last.then_inc(y_done, 1)

                    for k in range(2):
                        pe.wait_ge(yf_steps, 4)
                        for t in range(TT):
                            last = pe.transpose(P[4 + k][:, t * 128:t * 128 + 128],
                                                yf[:, t, k * 128:k * 128 + 128], eye_sb[:, :])
                        last.then_inc(yft_full, 1)
                    pe.wait_ge(yft_done, 2)
                    for t in range(TT):
                        for k in range(2):
                            last = pe.matmul(P[6][:, t * 128:t * 128 + 128], yfT[:, k, t * 128:t * 128 + 128],
                                             wout_sb[:, k, :], start=(k == 0), stop=(k == 1))
                    last.then_inc(mix_full, 1)

                @block.scalar
                def _(act):
                    def drain(key, o, i, func, **kw):
                        act.wait_ge(a_full, a_at[key] + 1)
                        act.activation(o, i, func, **kw).then_inc(a_free, 1)

                    drain(("dt",), exp_dt, a_bank(("dt",))[:, :], ACT.Exp, bias=dtb_sb[:, :])
                    drain(("kd",), sig_k, a_bank(("kd",))[:, :], ACT.Sigmoid)
                    for h in range(2):
                        drain(("val", h), v_pad[:, h, 3:3 + T], a_bank(("val", h))[:, :], ACT.Copy)
                    for g in range(G):
                        drain(("na", g), coef[:, 0, grp(g)], a_bank(("na", g))[:, :], ACT.Copy)
                        drain(("dtb", g), dt_rep[:, grp(g)], a_bank(("dtb", g))[:, :], ACT.Copy)
                        if g == 3:
                            for h in range(2):
                                act.wait_ge(conv_steps, 2 * KW)
                                act.activation(vT[:, h, :], conv[:, h, :], ACT.Silu).then_inc(silu_done, 1)
                    for j in range(2):
                        drain(("ut", j), u_tok[:, 2 * j:2 * j + 2, :].rearrange("p t i -> p (t i)"),
                              a_bank(("ut", j))[:, :], ACT.Copy)
                    for g in range(G):
                        drain(("w", g), winv[:, grp(g)], a_bank(("w", g))[:, :], ACT.Ln)
                    for n in range(4 * G):
                        key = ("nrm", n // 4, n % 4)
                        if n >= 2:
                            act.wait_ge(norm_acc, n - 1)
                        drain(key, sq[:, n % 2, :], a_bank(key)[:, :], ACT.Square)
                    act.wait_ge(norm_acc, 4 * G)
                    act.activation(rn[:, :], P[4][:, :], ACT.Sqrt).then_inc(norm_root, 1)
                    for g in range(G):
                        act.wait_ge(sums_done, g + 1)
                        act.activation(winv[:, grp(g)], winv[:, grp(g)], ACT.Exp, scale=-1.0).then_inc(inv_done, 1)

                    def drain_bc(g):
                        if g == 0:
                            act.wait_ge(conv_steps, 2 * KW)
                        if g == 2:
                            act.wait_ge(rec_steps, REC_STEPS)
                        if g >= 3:
                            act.wait_ge(main_steps, MAIN_STEPS * (g - 2))
                        for c in range(4):
                            drain(("bc", g, c), raw(g)[:, c, :], a_bank(("bc", g, c))[:, :], ACT.Copy)

                    for g in range(3):
                        drain_bc(g)
                    for g in range(G):
                        if g >= 2:
                            act.wait_ge(dx_psum, g - 1)
                        for j in range(2):
                            drain(("kt", g, j), kT_sb[:, g % 2, j].rearrange("p t k -> p (t k)"),
                                  a_bank(("kt", g, j))[:, :], ACT.Copy)
                        if g + 3 < G:
                            drain_bc(g + 3)
                    act.wait_ge(main_steps, MAIN_STEPS * G)
                    for j in range(2):
                        act.wait_ge(gate_full, j + 1)
                        act.activation(sg[:, 2 * j:2 * j + 2, :].rearrange("p t i -> p (t i)"),
                                                    P[2 + j][:, :], ACT.Silu).then_inc(gate_done, 1)
                    act.wait_ge(dx_psum, G)
                    for c in range(CT):
                        act.activation(dX[:, c::CT, :],
                                                  P[4 + c][:, :].rearrange("p (t m) -> p t m", t=TT), ACT.Copy).then_inc(dx_done, 1)
                    for ch in range(1, NC):
                        act.wait_ge(state_steps, STATE_STEPS * ch)
                        if ch >= 2:
                            act.wait_ge(y_done, ch - 1)
                        for h in range(HG):
                            act.activation(
                                x_bd[:, ch % 2].rearrange("p (m h d) -> p m h d", h=HG, d=DH)[:, :, h, :],
                                X[:, ch % 2].rearrange("p j (g d) -> p (j g) d", d=DH),
                                ACT.Copy, scale=own_sb[:, h:h + 1]).then_inc(xbd_done, 1)
                    for k in range(2):
                        act.wait_ge(yft_full, k + 1)
                        act.activation(yfT[:, k, :], P[4 + k][:, :], ACT.Copy).then_inc(yft_done, 1)
                    act.wait_ge(ln_steps, 9)
                    act.activation(rstd[:, :], mv[:, :, 1], ACT.Sqrt, bias=eps_sb[:, :]).then_inc(ln_root, 1)

                @block.gpsimd
                def _(pool):
                    pool.memset(v_pad[:, :, 0:3], 0.0).then_inc(pads, 1)
                    pool.memset(NT[:, ZZ, ::L], 1.0).then_inc(pads, 1)
                    for g in range(G):
                        r = raw(g)
                        pool.wait_ge(inv_done, G)
                        if g == 0:
                            pool.wait_ge(rec_steps, REC_STEPS)
                            pool.tensor_tensor(
                                phi[:, :, :], NT[:, :, L - 1::L],
                                winv[:, L - 1::L].unsqueeze(1).to_broadcast([128, 4, G * NC]), ALU.mult).then_inc(phi_done, 1)
                        pool.wait_ge(v_free, v_at[("rn", g, BX)] + 1)
                        if g >= 2:
                            pool.wait_ge(main_steps, MAIN_STEPS * (g - 1))
                        pool.tensor_tensor(nag[:, g % 2, :], coef[:, 0, grp(g)], r[:, BX, :],
                                                        ALU.mult).then_inc(pool_main, 1)
                        for c in (CZ, CX):
                            pool.wait_ge(v_free, v_at[("rn", g, c)] + 1)
                            pool.tensor_tensor(r[:, c, :], r[:, c, :], winv[:, grp(g)],
                                                            ALU.mult).then_inc(pool_main, 1)
                    pool.wait_ge(main_steps, MAIN_STEPS * G)
                    pool.tensor_tensor(su, u_tok[:, :, :],
                                                  skip_sb[:, :].unsqueeze(1).to_broadcast([128, TT, DI]),
                                                  ALU.mult).then_inc(su_done, 1)
                    pool.wait_ge(dx_done, CT)
                    phv = phi[:, :, :].rearrange("p (a j) (g c) -> p a j g c", a=2, g=G)
                    for ch in range(NC - 1):
                        nx = (ch + 1) % 2
                        if ch == 0:
                            pool.tensor_copy(st[:, 0], dX[:, 0].rearrange("p (j m) -> p j m", j=2)).then_inc(state_steps, one(state_steps))
                        else:
                            pool.wait_ge(state_steps, made(state_steps))
                            pool.tensor_tensor(
                                st[:, 0], X[:, ch % 2], dX[:, ch].rearrange("p (j m) -> p j m", j=2), ALU.add).then_inc(state_steps, one(state_steps))
                        pool.wait_ge(state_steps, made(state_steps))
                        for j in range(2):
                            pool.tensor_tensor(
                                st[:, 1 + j].rearrange("p a (g d) -> p a g d", g=G),
                                phv[:, :, j, :, ch].unsqueeze(3).to_broadcast([128, 2, G, DH]),
                                st[:, 0, j].rearrange("p (g d) -> p g d", g=G).unsqueeze(1)
                                .to_broadcast([128, 2, G, DH]), ALU.mult).then_inc(state_steps, one(state_steps))
                        pool.wait_ge(state_steps, made(state_steps))
                        if ch >= 2:
                            pool.wait_ge(xbd_done, HG * (ch - 1))
                        pool.tensor_tensor(X[:, nx], st[:, 1], st[:, 2], ALU.add).then_inc(state_steps, one(state_steps))

                @block.vector
                def _(dve):
                    dve.wait_ge(a_free, a_at[("dt",)] + 1)
                    dve.tensor_scalar(exp_dt, exp_dt, EXP_CAP, None, ALU.min).then_inc(dt_steps, one(dt_steps))
                    dve.wait_ge(dt_steps, made(dt_steps))
                    dve.tensor_scalar(log_p, exp_dt, -1.0 / LOG_TERMS * (-1) ** LOG_TERMS, None,
                                                  ALU.mult).then_inc(dt_steps, one(dt_steps))
                    for k in range(LOG_TERMS - 1, 0, -1):
                        dve.wait_ge(dt_steps, made(dt_steps))
                        dve.scalar_tensor_tensor(
                            out=log_p, in0=log_p, scalar=(1.0 if k % 2 else -1.0) / k, in1=exp_dt,
                            op0=ALU.add, op1=ALU.mult).then_inc(dt_steps, one(dt_steps))
                    dve.wait_ge(dt_steps, made(dt_steps))
                    dve.tensor_scalar(small[:, :], log_p, DT_MIN, DT_MAX, ALU.max, ALU.min).then_inc(dt_steps, one(dt_steps))
                    dve.wait_ge(dt_steps, made(dt_steps))
                    dve.wait_ge(a_free, a_at[("kd",)] + 1)
                    dve.scalar_tensor_tensor(
                        out=small[64:96, :], in0=sig_k[64:96, :], scalar=K_MAX, in1=small[64:96, :],
                        op0=ALU.mult, op1=ALU.mult).then_inc(dt_steps, one(dt_steps))
                    dve.tensor_tensor(small[96:128, :], small[96:128, :], small[96:128, :],
                                                  ALU.mult).then_inc(dt_steps, one(dt_steps))
                    dve.wait_ge(dt_steps, made(dt_steps))
                    dve.tensor_scalar(small[64:96, :], small[64:96, :], 1.0, None, ALU.add).then_inc(dt_steps, one(dt_steps))
                    assert made(dt_steps) == DT_STEPS

                    def drain_c(g):
                        dve.wait_ge(v_full, v_at[("c", g)] + 1)
                        dve.tensor_copy(coef[:, 1, grp(g)], v_bank(("c", g))[:, :]).then_inc(v_free, one(v_free))

                    for g in range(2):
                        drain_c(g)
                    dve.wait_ge(a_free, a_at[("val", 1)] + 1)
                    dve.wait_ge(pads, 2)
                    for k in range(KW):
                        for h in range(2):
                            if made(conv_steps) > 1:
                                dve.wait_ge(conv_steps, made(conv_steps) - 1)
                            if k == 0:
                                ins = dve.tensor_scalar(conv[:, h, :], v_pad[:, h, 0:T], cw_sb[:, h, 0:1],
                                                        cb_sb[:, h:h + 1], ALU.mult, ALU.add)
                            else:
                                ins = dve.scalar_tensor_tensor(
                                    out=conv[:, h, :], in0=v_pad[:, h, k:k + T], scalar=cw_sb[:, h, k:k + 1],
                                    in1=conv[:, h, :], op0=ALU.mult, op1=ALU.add)
                            ins.then_inc(conv_steps, one(conv_steps))
                    for g in range(2, G):
                        drain_c(g)

                    dve.wait_ge(a_free, a_at[("dtb", G - 1)] + 1)
                    dve.wait_ge(v_free, made(v_free))
                    dve.wait_ge(conv_steps, made(conv_steps))
                    dve.tensor_copy(NT[:, ZS, ::L], coef[:, 0, ::L]).then_inc(rec_steps, one(rec_steps))
                    dve.tensor_copy(NT[:, SZ, ::L], dt_rep[:, ::L]).then_inc(rec_steps, one(rec_steps))
                    dve.tensor_copy(NT[:, SS, ::L], coef[:, 1, ::L]).then_inc(rec_steps, one(rec_steps))
                    GC = G * NC
                    for t in range(1, L):
                        dve.wait_ge(rec_steps, made(rec_steps) - (1 if t > 1 else 0))
                        dve.tensor_tensor(
                            step_b[:, t % 2], NT[:, 0:2, t - 1::L],
                            dt_rep[:, t::L].unsqueeze(1).to_broadcast([128, 2, GC]), ALU.mult).then_inc(rec_steps, one(rec_steps))
                        if made(rec_steps) > 1:
                            dve.wait_ge(rec_steps, made(rec_steps) - 1)
                        dve.tensor_tensor(
                            step_a[:, :, :, :],
                            NT[:, 2:4, t - 1::L].unsqueeze(1).to_broadcast([128, 2, 2, GC]),
                            coef[:, :, t::L].unsqueeze(2).to_broadcast([128, 2, 2, GC]), ALU.mult).then_inc(rec_steps, one(rec_steps))
                        dve.wait_ge(rec_steps, made(rec_steps))
                        dve.tensor_tensor(NT[:, 0:2, t::L], NT[:, 0:2, t - 1::L],
                                                       step_a[:, 0], ALU.add).then_inc(rec_steps, one(rec_steps))
                        dve.tensor_tensor(NT[:, 2:4, t::L], step_b[:, t % 2], step_a[:, 1],
                                                       ALU.add).then_inc(rec_steps, one(rec_steps))
                        if t >= L - G:
                            g = t - (L - G)
                            dve.wait_ge(a_free, a_at[("w", g)] + 1)
                            dve.tensor_tensor_scan(winv[:, grp(g)], chunk_sb[:, :],
                                                                winv[:, grp(g)], 0.0, ALU.mult, ALU.add).then_inc(sums_done, 1)
                    assert made(rec_steps) == REC_STEPS

                    dve.wait_ge(rec_steps, made(rec_steps))
                    for k in range(NC // 2):
                        dve.wait_ge(v_full, v_at[("ub", k)] + 1)
                        dve.tensor_tensor(
                            u_bd[:, k * 512:k * 512 + 512].rearrange("p (m h d) -> p m h d", h=HG, d=DH),
                            v_bank(("ub", k))[:, :].rearrange("p (m h d) -> p m h d", h=HG, d=DH),
                            own_sb[:, :].unsqueeze(1).unsqueeze(3).to_broadcast([128, 2 * G, HG, DH]),
                            ALU.mult).then_inc(v_free, one(v_free))
                    dve.wait_ge(norm_root, 1)
                    dve.tensor_scalar(rn[:, :], rn[:, :], EPS_NORM, None, ALU.add).then_inc(rn_steps, one(rn_steps))
                    dve.wait_ge(rn_steps, made(rn_steps))
                    dve.reciprocal(rn[:, :], rn[:, :]).then_inc(rn_steps, one(rn_steps))
                    dve.wait_ge(rn_steps, made(rn_steps))
                    dve.tensor_tensor(rn[0:64, :], rn[0:64, :], small[0:64, :], ALU.mult).then_inc(rn_steps, one(rn_steps))
                    assert made(rn_steps) == RN_STEPS

                    def normalise(g):
                        for c in (BX, CZ, CX, BZ):
                            dve.wait_ge(a_free, a_at[("bc", g, c)] + 1)
                            dve.wait_ge(v_full, v_at[("rn", g, c)] + 1)
                            dve.tensor_tensor(raw(g)[:, c, :], raw(g)[:, c, :],
                                                        v_bank(("rn", g, c))[:, :], ALU.mult).then_inc(v_free, one(v_free))

                    def plane(p, g):
                        return NT[:, p, grp(g)]

                    def before(a):
                        return a.rearrange("p (c t) -> p c t", t=L)[:, :, 0:L - 1]

                    def after(a):
                        return a.rearrange("p (c t) -> p c t", t=L)[:, :, 1:L]

                    def q_kappa(g):
                        r = raw(g)
                        dve.wait_ge(pool_main, 3 * g + 1)
                        dve.wait_ge(v_free, made(v_free))
                        dve.tensor_tensor(r[:, BZ, :], r[:, BZ, :], nag[:, g % 2, :],
                                                        ALU.subtract).then_inc(main_steps, one(main_steps))
                        dve.tensor_tensor(after(prod[:, 0, 1, :]), before(plane(ZZ, g)),
                                                        after(r[:, BX, :]), ALU.mult).then_inc(main_steps, one(main_steps))
                        if made(main_steps) > 1:
                            dve.wait_ge(main_steps, made(main_steps) - 1)
                        dve.tensor_tensor(after(prod[:, 1, 0, :]), before(plane(ZS, g)),
                                                        after(r[:, BX, :]), ALU.mult).then_inc(main_steps, one(main_steps))
                        if made(main_steps) > 1:
                            dve.wait_ge(main_steps, made(main_steps) - 1)
                        dve.tensor_tensor(after(prod[:, 0, 0, :]), before(plane(SS, g)),
                                                        after(r[:, BZ, :]), ALU.mult).then_inc(main_steps, one(main_steps))
                        if made(main_steps) > 1:
                            dve.wait_ge(main_steps, made(main_steps) - 1)
                        dve.tensor_tensor(after(prod[:, 1, 1, :]), before(plane(SZ, g)),
                                                        after(r[:, BZ, :]), ALU.mult).then_inc(main_steps, one(main_steps))
                        dve.wait_ge(pool_main, 3 * g + 3)
                        dve.wait_ge(phi_done, 1)
                        if made(main_steps) > 1:
                            dve.wait_ge(main_steps, made(main_steps) - 1)
                        dve.tensor_tensor(
                            NT[:, 0:2, grp(g)], NT[:, 0:2, grp(g)],
                            r[:, CZ, :].unsqueeze(1).to_broadcast([128, 2, T]), ALU.mult).then_inc(main_steps, one(main_steps))
                        if made(main_steps) > 1:
                            dve.wait_ge(main_steps, made(main_steps) - 1)
                        dve.tensor_tensor(
                            NT[:, 2:4, grp(g)], NT[:, 2:4, grp(g)],
                            r[:, CX, :].unsqueeze(1).to_broadcast([128, 2, T]), ALU.mult).then_inc(main_steps, one(main_steps))
                        dve.wait_ge(main_steps, made(main_steps))
                        dve.tensor_tensor(NT[:, 0:2, grp(g)], NT[:, 0:2, grp(g)],
                                                        NT[:, 2:4, grp(g)], ALU.add).then_inc(main_steps, one(main_steps))
                        dve.wait_ge(main_steps, made(main_steps))
                        kv = NT[:, 2:4, grp(g)].rearrange("p j (c t) -> p j c t", t=L)
                        pv = prod[:, :, :, :].rearrange("p s j (c t) -> p s j c t", t=L)
                        dve.tensor_tensor(kv[:, :, :, 1:L], pv[:, 0, :, :, 1:L],
                                                        pv[:, 1, :, :, 1:L], ALU.subtract).then_inc(main_steps, one(main_steps))
                        dve.tensor_copy(kv[:, :, :, 0],
                                                      r[:, 0:2, :].rearrange("p j (c t) -> p j c t", t=L)[:, :, :, 0]).then_inc(main_steps, one(main_steps))
                        assert made(main_steps) == MAIN_STEPS * (g + 1)

                    def mask(g):
                        dve.wait_ge(v_full, v_at[("g", g)] + 1)
                        dve.tensor_tensor(
                            gm[:, grp(g)].rearrange("p (c t) -> p c t", t=L),
                            v_bank(("g", g))[:, :].rearrange("p (c t) -> p c t", t=L),
                            causal_sb[:, :].unsqueeze(1).to_broadcast([128, NC, L]), ALU.mult).then_inc(v_free, one(v_free))

                    normalise(0)
                    normalise(1)
                    for g in range(G):
                        if g:
                            dve.wait_ge(main_steps, made(main_steps))
                        q_kappa(g)
                        if g == 0:
                            normalise(2)
                        else:
                            mask(g - 1)
                            if g + 2 < G:
                                normalise(g + 2)
                    mask(G - 1)

                    dve.wait_ge(su_done, 1)
                    dve.wait_ge(gate_done, 2)
                    for j in range(2):
                        dve.wait_ge(y_done, 8 * (j + 1))
                        dve.tensor_tensor(
                            yf[:, 2 * j:2 * j + 2, :].rearrange("p t i -> p (t i)"), P[j][:, :],
                            su[:, 2 * j:2 * j + 2, :].rearrange("p t i -> p (t i)"), ALU.add).then_inc(yf_steps, one(yf_steps))
                        dve.wait_ge(yf_steps, made(yf_steps))
                        dve.tensor_tensor(yf[:, 2 * j:2 * j + 2, :], yf[:, 2 * j:2 * j + 2, :],
                                                      sg[:, 2 * j:2 * j + 2, :], ALU.mult).then_inc(yf_steps, one(yf_steps))
                    dve.wait_ge(mix_full, 1)
                    dve.tensor_tensor(xres[:, :, :], xres[:, :, :],
                                                  P[6][:, :].rearrange("p (t d) -> p t d", t=TT), ALU.add).then_inc(ln_steps, one(ln_steps))
                    layer_norm(dve, ln_steps, ln_root, xres, xres)

            with nc.Block() as block:
                @block.sync
                def _(sp):
                    sp.dma_start(ctx_sb, ctxT[:, bass.ds(b * S, S)]).then_inc(ffn_in, 16)
                    sp.dma_start(fb_sb, fcol).then_inc(ffn_in, 16)
                    sp.dma_start(fcb_sb[0:E + 1, :], fc2b).then_inc(ffn_in, 16)
                    sp.dma_start(fc2_raw, fc2T).then_inc(ffn_in, 16)
                    sp.dma_start(fc1_sb, fc1T).then_inc(ffn_in, 16)
                    sp.wait_ge(acc_steps, ACC_STEPS)
                    sp.dma_start(
                        out[bass.ds(b * T, T), :].rearrange("(t p) d -> p t d", p=128), acc).then_inc(stored, 16)
                    sp.wait_ge(stored, 16)

                @block.gpsimd
                def _(pool):
                    pool.wait_ge(ffn_in, 80)
                    for e in range(NE):
                        pool.tensor_scalar(fc2_sb[:, e, :], fc2_raw[:, e, :], fb_sb[:, e, 2:3], 1.0,
                                                     ALU.mult, ALU.mult).then_inc(scaled, 1)

                @block.tensor
                def _(pe):
                    for t in range(TT):
                        last = pe.transpose(P[0][:, t * 128:t * 128 + 128], xres[:, t, :], eye_sb[:, :])
                    last.then_inc(x1_full, 1)
                    pe.wait_ge(ffn_in, 80)
                    pe.matmul(P[2][:, 0:S], wqkv_sb[:, 1, :], ctx_sb, start=True, stop=True).then_inc(qkv_full, 1)
                    for j in range(2):
                        pe.matmul(P[3][0:SH, j * 128:j * 128 + 128], ctx_sb[:, j * SH:(j + 1) * SH],
                                  wqkv_sb[:, 2, :], start=True, stop=False)
                        last = pe.matmul(P[3][0:SH, j * 128:j * 128 + 128], ones_sb[0:1, 0:SH], bv_sb[0:1, :],
                                         start=False, stop=True)
                    last.then_inc(qkv_full, 1)
                    pe.wait_ge(x1_done, 1)
                    pe.matmul(P[1][:, :], wqkv_sb[:, 0, :], x1T, start=True, stop=True).then_inc(qkv_full, 1)
                    pe.wait_ge(qkv_done, 3)
                    for t in range(TT):
                        last = pe.matmul(P[4 + t // 2][:, (t % 2) * S:(t % 2 + 1) * S],
                                         qT[:, t * 128:t * 128 + 128], kcT, start=True, stop=True)
                        last.then_inc(s_full, 1)
                    for t in range(TT):
                        pe.wait_ge(p_done, t + 1)
                        for j in range(2):
                            last = pe.transpose(
                                P[6 + t // 2][0:SH, (t % 2) * 256 + j * 128:(t % 2) * 256 + j * 128 + 128],
                                probs[:, t, j * SH:(j + 1) * SH], eye_sb[:, :])
                        last.then_inc(pt_full, 1)
                    for t in range(TT):
                        pe.wait_ge(pt_done, t // 2 + 1)
                        for j in range(2):
                            last = pe.matmul(P[0][:, t * 128:t * 128 + 128], pT[0:SH, t, j, :], v_sb[0:SH, j, :],
                                             start=(j == 0), stop=(j == 1))
                    last.then_inc(o_full, 1)
                    pe.wait_ge(x_steps, X_STEPS)
                    for t in range(TT):
                        last = pe.transpose(P[1][:, t * 128:t * 128 + 128], xres[:, t, :], eye_sb[:, :])
                    last.then_inc(x2_full, 1)
                    pe.wait_ge(x2_done, 1)
                    for t in range(TT):
                        last = pe.matmul(P[2][:, t * E:(t + 1) * E], x2T[:, t * 128:t * 128 + 128], gw_sb[:, :],
                                         start=True, stop=True)
                    last.then_inc(lg_full, 1)

                    def up(i):
                        e = ORDER[i]
                        if i >= 2:
                            pe.wait_ge(gelu_done, i - 1)
                        pe.matmul(P[4 + i % 2][:, :], fc1_sb[:, e, 128:256], x2T,
                                             start=True, stop=True).then_inc(hg_full, 1)
                        if i >= 2:
                            pe.wait_ge(glu_done, i - 1)
                        pe.matmul(P[6 + i % 2][:, :], fc1_sb[:, e, 0:128], x2T,
                                             start=True, stop=True).then_inc(hx_full, 1)

                    def down(i):
                        e = ORDER[i]
                        pe.wait_ge(glu_done, i + 1)
                        pe.wait_ge(scaled, e + 1)
                        if e >= E:
                            for t in range(TT):
                                last = pe.matmul(P[3][:, t * 128:t * 128 + 128],
                                                 act_a[:, i % 2, t * 128:t * 128 + 128], fc2_sb[:, e, :],
                                                 start=(e == E and t == 0), stop=False, skip_group_check=True)
                            last.then_inc(base, 1)
                            if e == NE - 1:
                                pe.wait_ge(ct_done, 1)
                                for t in range(TT):
                                    last = pe.matmul(P[3][:, t * 128:t * 128 + 128],
                                                     combT[0:E + 1, t * 128:t * 128 + 128], fcb_sb[0:E + 1, :],
                                                     start=False, stop=(t == TT - 1), skip_group_check=True)
                                last.then_inc(base, 1)
                        else:
                            if e >= 2:
                                pe.wait_ge(acc_steps, 1 + TT * (e - 1))
                            for t in range(TT):
                                last = pe.matmul(P[e % 2][:, t * 128:t * 128 + 128],
                                                 act_a[:, i % 2, t * 128:t * 128 + 128], fc2_sb[:, e, :],
                                                 start=True, stop=True)
                            last.then_inc(e_full, 1)

                    up(0)
                    pe.wait_ge(route, ROUTE_STEPS)
                    for t in range(TT):
                        last = pe.transpose(P[2][0:E + 1, t * 128:t * 128 + 128], comb[:, t, :], eye_sb[:, :])
                    last.then_inc(ct_full, 1)
                    for i in range(NE):
                        if i + 1 < NE:
                            up(i + 1)
                        down(i)

                @block.scalar
                def _(act):
                    act.wait_ge(x1_full, 1)
                    act.activation(x1T, P[0][:, :], ACT.Copy).then_inc(x1_done, 1)
                    act.wait_ge(qkv_full, 1)
                    act.activation(kcT, P[2][:, 0:S], ACT.Identity, bias=bqk_sb[:, 1:2]).then_inc(qkv_done, 1)
                    act.wait_ge(qkv_full, 2)
                    act.activation(v_sb[0:SH].rearrange("p j d -> p (j d)"), P[3][0:SH, 0:256],
                                               ACT.Copy).then_inc(qkv_done, 1)
                    act.wait_ge(qkv_full, 3)
                    act.activation(qT, P[1][:, :], ACT.Identity, bias=bqk_sb[:, 0:1]).then_inc(qkv_done, 1)
                    for t in range(TT):
                        act.wait_ge(s_max, t // 2 + 1)
                        act.activation(probs[:, t, :], P[4 + t // 2][:, (t % 2) * S:(t % 2 + 1) * S],
                                                 ACT.Exp, bias=negmax[:, t:t + 1], accum_out=sums[:, t:t + 1]).then_inc(p_done, 1)
                    for j in range(2):
                        act.wait_ge(pt_full, 2 * j + 2)
                        act.activation(
                            pT[0:SH, 2 * j:2 * j + 2].rearrange("p t j q -> p (t j q)"), P[6 + j][0:SH, :],
                            ACT.Copy).then_inc(pt_done, 1)
                    act.wait_ge(x_steps, X_STEPS - 1 - TT)
                    act.activation(rstd[:, :], mv[:, :, 1], ACT.Sqrt, bias=eps_sb[:, :]).then_inc(ln2_root, 1)
                    act.wait_ge(x2_full, 1)
                    act.activation(x2T, P[1][:, :], ACT.Copy).then_inc(x2_done, 1)
                    for t in range(TT):
                        act.wait_ge(route, 2)
                        act.activation(score[:, t, :], P[2][:, t * E:(t + 1) * E], ACT.Exp,
                                                 bias=gmax[:, t:t + 1], accum_out=gsum[:, t:t + 1]).then_inc(lg_exp, 1)
                    for i in range(NE):
                        e = ORDER[i]
                        act.wait_ge(hg_full, i + 1)
                        if i >= 2:
                            act.wait_ge(glu_done, i - 1)
                        act.activation(ga[:, i % 2, :], P[4 + i % 2][:, :], ACT.Gelu,
                                                    bias=fb_sb[:, e, 0:1]).then_inc(gelu_done, 1)
                        if i == 0:
                            act.wait_ge(ct_full, 1)
                            act.activation(combT[0:E + 1, :], P[2][0:E + 1, :], ACT.Copy).then_inc(ct_done, 1)
                    act.wait_ge(acc_steps, ACC_STEPS - 1 - TT)
                    act.activation(rstd[:, :], mv[:, :, 1], ACT.Sqrt, bias=eps_sb[:, :]).then_inc(ln3_root, 1)

                @block.vector
                def _(dve):
                    for j in range(2):
                        dve.wait_ge(s_full, 2 * j + 2)
                        dve.tensor_reduce(
                            out=negmax[:, 2 * j:2 * j + 2],
                            in_=P[4 + j][:, 0:2 * S].rearrange("p (t s) -> p t s", s=S), axis=AX,
                            op=ALU.max, negate=True).then_inc(s_max, 1)
                    dve.wait_ge(p_done, TT)
                    dve.reciprocal(rsum, sums).then_inc(x_steps, one(x_steps))
                    dve.wait_ge(o_full, 1)
                    dve.wait_ge(x_steps, made(x_steps))
                    for t in range(TT):
                        dve.scalar_tensor_tensor(
                            out=xres[:, t, :], in0=P[0][:, t * 128:t * 128 + 128], scalar=rsum[:, t:t + 1],
                            in1=xres[:, t, :], op0=ALU.mult, op1=ALU.add).then_inc(x_steps, one(x_steps))
                    layer_norm(dve, x_steps, ln2_root, xres, xres)
                    assert made(x_steps) == X_STEPS
                    dve.wait_ge(lg_full, 1)
                    lg = P[2][:, 0:TT * E].rearrange("p (t e) -> p t e", t=TT)
                    dve.tensor_reduce(out=gmax, in_=lg, axis=AX, op=ALU.max, negate=True).then_inc(route, one(route))
                    dve.memset(comb[:, :, E:E + 1], 1.0).then_inc(route, one(route))
                    dve.wait_ge(lg_exp, TT)
                    dve.reciprocal(grec, gsum).then_inc(route, one(route))
                    dve.wait_ge(route, made(route))
                    dve.tensor_tensor(score, score, grec.unsqueeze(2).to_broadcast([128, TT, E]),
                                               ALU.mult).then_inc(route, one(route))
                    dve.wait_ge(route, made(route))
                    for t in range(TT):
                        dve.max(top8[:, t, :], score[:, t, :]).then_inc(route, one(route))
                    dve.wait_ge(route, made(route))
                    dve.tensor_reduce(out=topsum, in_=top8[:, :, 0:TOPK], axis=AX, op=ALU.add).then_inc(route, one(route))
                    dve.memset(top8[:, :, TOPK:8], -1.0).then_inc(route, one(route))
                    dve.wait_ge(route, made(route))
                    for t in range(TT):
                        dve.match_replace(left[:, t, :], top8[:, t, :], score[:, t, :], -2.0).then_inc(route, one(route))
                    dve.tensor_scalar(topsum, topsum, EPS_TOP, None, ALU.add).then_inc(route, one(route))
                    dve.wait_ge(route, made(route))
                    dve.reciprocal(topsum, topsum).then_inc(route, one(route))
                    dve.scalar_tensor_tensor(out=comb[:, :, 0:E], in0=left, scalar=0.0, in1=score,
                                                      op0=ALU.is_lt, op1=ALU.mult).then_inc(route, one(route))
                    dve.wait_ge(route, made(route))
                    dve.tensor_tensor(comb[:, :, 0:E], comb[:, :, 0:E],
                                               topsum.unsqueeze(2).to_broadcast([128, TT, E]), ALU.mult).then_inc(route, one(route))
                    assert made(route) == ROUTE_STEPS
                    dve.wait_ge(route, made(route))

                    def glu(i):
                        e = ORDER[i]
                        dve.wait_ge(hx_full, i + 1)
                        dve.wait_ge(gelu_done, i + 1)
                        dve.scalar_tensor_tensor(
                            out=act_a[:, i % 2, :], in0=P[6 + i % 2][:, :], scalar=fb_sb[:, e, 1:2],
                            in1=ga[:, i % 2, :], op0=ALU.add, op1=ALU.mult).then_inc(glu_done, 1)

                    def add_up(e):
                        dve.wait_ge(e_full, e + 1)
                        for t in range(TT):
                            if t == 0:
                                dve.wait_ge(acc_steps, made(acc_steps))
                            dve.scalar_tensor_tensor(
                                out=acc[:, t, :], in0=P[e % 2][:, t * 128:t * 128 + 128],
                                scalar=comb[:, t, e:e + 1], in1=acc[:, t, :], op0=ALU.mult, op1=ALU.add).then_inc(acc_steps, one(acc_steps))

                    for i in range(NE):
                        if i >= 2:
                            if i - 2 < 2:
                                dve.wait_ge(base, 1 if i == 2 else 3)
                            else:
                                dve.wait_ge(e_full, i - 3)
                        glu(i)
                        if i == 2:
                            dve.wait_ge(base, 3)
                            dve.tensor_tensor(
                                acc, P[3][:, :].rearrange("p (t d) -> p t d", t=TT), xres[:, :, :], ALU.add).then_inc(acc_steps, one(acc_steps))
                        if i >= 3:
                            add_up(i - 3)
                    add_up(E - 1)
                    layer_norm(dve, acc_steps, ln3_root, acc, acc)
                    assert made(acc_steps) == ACC_STEPS

            nc.all_engine_barrier(sems_to_clear=range(signals[0].num, signals[-1].num + 1))


def kernel(**inputs):
    import numpy as np
    import concourse.bacc as bacc
    from concourse.bass_utils import run_bass_kernel_spmd as run

    a = {k: np.asarray(v) for k, v in inputs.items()}
    w_in = a["L0_attn_W_in"]
    par = w_in[2 * DI:].reshape(H, 2, D)
    part = np.arange(128)
    f1 = a["L0_ffn_fc1_w"].transpose(2, 0, 1)
    s1 = a["L0_ffn_s_fc1_w"].reshape(2, 2, F, D).transpose(3, 1, 0, 2).reshape(D, 2, 2 * F)
    b1 = a["L0_ffn_fc1_b"].reshape(E, 2, F).transpose(2, 0, 1)[:, :, ::-1]
    sb1 = a["L0_ffn_s_fc1_b"].reshape(2, 2, F).transpose(2, 1, 0)[:, :, ::-1]
    f2 = a["L0_ffn_fc2_w"].transpose(2, 0, 1)
    s2 = a["L0_ffn_s_fc2_w"].reshape(D, 2, F).transpose(2, 1, 0)
    head_of = np.repeat(np.arange(H), NS)
    f = np.float32
    data = {
        "xT": a["x"].reshape(B * T, D).T,
        "x": a["x"].reshape(B * T, D),
        "ctxT": a["ctx_1024"].reshape(B * S, D).T,
        "WinT": np.concatenate([w_in[:2 * DI], np.tile(par[:, 0], (4, 1)), np.tile(par[:, 1], (4, 1))]).T,
        "Wbc": a["L0_attn_W_bc"].reshape(G, HG, 4, NS, 2, 128).transpose(0, 5, 2, 4, 1, 3)
        .reshape(G * 128, 1024),
        "WoutT": a["L0_attn_W_out"].T.reshape(2, 128, D).transpose(1, 0, 2),
        "skip": a["L0_attn_skip"],
        "A_log": a["L0_attn_A_log"],
        "dtb": np.tile(a["L0_attn_dt_bias"], 4)[:, None],
        "cw": a["L0_attn_dw_weight"].reshape(2, 128, KW).transpose(1, 0, 2),
        "cb": a["L0_attn_dw_bias"].reshape(2, 128).T,
        "Wq": a["L0_xattn_Wq"], "bq": a["L0_xattn_bq"][:, None],
        "Wk": a["L0_xattn_Wk"], "bk": a["L0_xattn_bk"][:, None],
        "Wv": a["L0_xattn_Wv"], "bv": a["L0_xattn_bv"][None, :],
        "gwT": a["L0_ffn_gate_w"].T,
        "fc1T": np.concatenate([f1, s1], 1),
        "fcol": np.concatenate([
            np.concatenate([b1, sb1], 1),
            np.concatenate([a["L0_ffn_geglu_mult"].T, a["L0_ffn_s_geglu_mult"].reshape(2, F).T], 1)[:, :, None]], 2),
        "fc2T": np.concatenate([f2, s2], 1),
        "fc2b": np.concatenate([a["L0_ffn_fc2_b"], a["L0_ffn_s_fc2_b"][None, :]], 0),
        "heads": (part[:, None] % H == head_of[None, :]).astype(f),
        "onehot": (124 + part[:, None] // NS == np.arange(252)[None, :]).astype(f),
        "tiled_eye": (part[:, None] % L == part[None, :] % L).astype(f),
        "causal": (np.arange(L)[None, :] >= part[:, None] % L).astype(f),
        "chunk_on": np.tile((np.arange(T) % L != 0).astype(f), (128, 1)),
        "own_head": (part[:, None] // NS == np.arange(HG)[None, :]).astype(f),
        "eye": np.eye(128, dtype=f),
    }
    nc = bacc.Bacc("TRN2", target_bir_lowering=False, num_devices=1)
    arrays, args = {}, {}
    for name, v in data.items():
        arrays[f"in_{name}"] = v = np.ascontiguousarray(v)
        args[name] = nc.dram_tensor(f"in_{name}", v.shape, mybir.dt.float32, kind="ExternalInput").ap()
    args["out"] = nc.dram_tensor("out_x", (B * T, D), mybir.dt.float32, kind="ExternalOutput").ap()
    build(nc, **args)
    r = run(nc, [arrays], core_ids=[0])
    return r.results[0]["out_x"].reshape(B, T, D)
```

```python
import concourse.bass as bass
from concourse import mybir
from contextlib import ExitStack

B, T, D = 4, 512, 128
DI, H, NS, DH, KW = 256, 32, 32, 8, 4
L = 32
NC = T // L
HG = 4
G = H // HG
UG = 4
U = G // UG
UT = UG * T
TT = T // 128
CT = 128 // L
S = 154
SH = S // 2
E, F, TOPK = 15, 128, 3
NE = E + 2
DT_MIN, DT_MAX, K_MAX = 1e-4, 0.1, 0.5
EXP_CAP = 0.106
LOG_TERMS = 9
EPS_NORM, EPS_LN, EPS_TOP = 1e-8, 1e-5, 1e-20
BZ, BX, CZ, CX = range(4)
ORDER = [E, E + 1] + list(range(E))
LN_STEPS = 2 * TT + 1 + TT
DT_STEPS = 3 + (LOG_TERMS - 1) + 4
C_STEPS = DT_STEPS + 2 + 4
REC_STEPS = 3 + 4 * (L - 1)
RN_STEPS = 7
MAIN_STEPS = 10
STATE_STEPS = 4
X_STEPS = 1 + TT + LN_STEPS
ROUTE_STEPS = 4 + TT + 2 + TT + 4
ACC_STEPS = 1 + TT * E + LN_STEPS
ZZ, ZS, SZ, SS = range(4)


class Counts:

    def __init__(self):
        self.value = {}

    def one(self, sem):
        self.value[sem.num] = self.value.get(sem.num, 0) + 1
        return 1

    def made(self, sem):
        return self.value.get(sem.num, 0)


def ring_orders():
    act = [("dt",), ("kd",), ("val", 0), ("val", 1)] + [("dtb", g) for g in range(UG)]
    act += [("ut", 0), ("ut", 1)]
    dve = [("c", g) for g in range(UG)]
    for u in range(U):
        act += [("bc", u * UG + s, c) for s in range(UG) for c in range(4)]
        dve += [("ub", u, c) for c in range(CT)] + [("dtn", u)]
        dve += [("rn", u * UG + s, c) for s in range(2) for c in (BX, CZ, CX, BZ)]
        for s in range(UG):
            g = u * UG + s
            act += [("kt", g, j) for j in range(2)]
            dve.append(("g", g))
            if s + 2 < UG:
                dve += [("rn", g + 2, c) for c in (BX, CZ, CX, BZ)]
            if u + 1 < U:
                act += [("dtb", g + UG), ("c", g + UG)]
    return act, dve


def build(nc, xT, x, ctxT, WinT, Wbc, WoutT, skip, A_log, dtb, cw, cb, Wq, bq, Wk, bk, Wv, bv,
          gwT, fc1T, fcol, fc2T, fc2b, heads, dt_rows, rn_pick, onehot, tiled_eye, causal,
          chunk_on, own_head, eye, out):
    f32 = mybir.dt.float32
    bf16 = mybir.dt.bfloat16
    ALU = mybir.AluOpType
    ACT = mybir.ActivationFunctionType
    AX = mybir.AxisListType.X
    ctx = ExitStack()
    with ctx:
        def sb(name, *shape, dtype=f32):
            return ctx.enter_context(nc.sbuf_tensor(name, list(shape), dtype))

        signals = []
        counts = Counts()
        one, made = counts.one, counts.made

        def sig(name):
            s = ctx.enter_context(nc.semaphore(name))
            signals.append(s)
            return s

        heads_sb = sb("heads_sb", 128, H * NS, dtype=bf16)
        dt_rows_sb = sb("dt_rows_sb", 128, U * 128, dtype=bf16)
        rn_pick_sb = sb("rn_pick_sb", 128, UG * 4 * 128, dtype=bf16)
        neg_a = sb("neg_a", 128, G)
        onehot_sb = sb("onehot_sb", 128, 252)
        tiled_sb = sb("tiled_sb", 128, 128)
        causal_sb = sb("causal_sb", 128, L)
        chunk_sb = sb("chunk_sb", 128, T)
        own_sb = sb("own_sb", 128, HG)
        eye_sb = sb("eye_sb", 128, 128)
        win_sb = sb("win_sb", 128, 768)
        wout_sb = sb("wout_sb", 128, 2, 128)
        skip_sb = sb("skip_sb", 128, DI)
        dtb_sb = sb("dtb_sb", 128, 1)
        cw_sb = sb("cw_sb", 128, 2, KW)
        cb_sb = sb("cb_sb", 128, 2)
        wqkv_sb = sb("wqkv_sb", 128, 3, 128)
        bqk_sb = sb("bqk_sb", 128, 2)
        bv_sb = sb("bv_sb", 1, 128)
        ones_sb = sb("ones_sb", 1, 128)
        gw_sb = sb("gw_sb", 128, E)
        eps_sb = sb("eps_sb", 128, 1)

        x_in = sb("x_in", 128, T)
        NT = sb("NT", 128, 4, G * T)
        coef = sb("coef", 128, 2, G * T)
        dt_rep = sb("dt_rep", 128, G * T)
        winv = sb("winv", 128, G * T)
        raw_sb = sb("raw_sb", 128, 2, 4, T)
        wbc_sb = sb("wbc_sb", 128, 2, 4, 2, 128)
        vT = sb("vT", 128, 2, T)
        u_tok = sb("u_tok", 128, TT, DI)
        prod = sb("prod", 128, 2, 2, T)
        nag = sb("nag", 128, 2, T)
        dt_parts = sb("dt_parts", 128, T, dtype=bf16)
        c_parts = sb("c_parts", 128, T, dtype=bf16)
        rn = sb("rn", 128, T)
        rn_hm = sb("rn_hm", 128, T, dtype=bf16)
        rn_lo = sb("rn_lo", 64, T, dtype=bf16)
        dX = sb("dX", 128, NC, 2, UG, DH)
        ctx_sb = sb("ctx_sb", 128, S)
        phi = sb("phi", 128, 4, G * NC)
        xres = sb("xres", 128, TT, D)
        stats = sb("stats", 128, TT, 6)
        mv = sb("mv", 128, TT, 2)
        rstd = sb("rstd", 128, TT)

        v_pad = prod[:, :, :, :].rearrange("p a b t -> p (a b t)")[:, 0:2 * (T + 3)] \
            .rearrange("p (h t) -> p h t", h=2)
        prodf = prod[:, :, :, :].rearrange("p a b t -> p (a b t)")
        step_a = prodf[:, 0:256].rearrange("p (r j m) -> p r j m", r=2, j=2)
        step_b = prodf[:, 256:512].rearrange("p (s j m) -> p s j m", s=2, j=2)
        x_bd = prodf[:, 512:1024].rearrange("p (s m) -> p s m", s=2)
        X = prodf[:, 1024:1152].rearrange("p (s j m) -> p s j m", s=2, j=2)
        st = prodf[:, 1152:1344].rearrange("p (s j m) -> p s j m", s=3, j=2)
        conv = raw_sb[:, 0, 0:2, :]
        exp_dt = raw_sb[:, 1, 0, :]
        sig_k = raw_sb[:, 1, 1, :]
        log_p = raw_sb[:, 1, 2, :]
        rest = raw_sb[:, 1, 3, :]
        sq = nag
        gm = winv

        def u_bd(u):
            return dt_rep[:, u * UT:(u + 1) * UT].rearrange("p (c t m) -> p c t m", c=CT, t=TT)

        def um(g):
            return coef[:, 0, g * T:(g + 1) * T].rearrange("p (t c m) -> p t c m", t=TT, c=CT)

        def kT(u):
            return coef[:, 1, u * UT:(u + 1) * UT].rearrange("p (s c t k) -> p s c t k", s=2, c=2, t=TT)
        wide = raw_sb[:, :, :, :].rearrange("p s c t -> p (s c t)")
        su = wide[:, 0:1024].rearrange("p (t i) -> p t i", t=TT)
        sg = wide[:, 1024:2048].rearrange("p (t i) -> p t i", t=TT)
        yf = wide[:, 2048:3072].rearrange("p (t i) -> p t i", t=TT)
        yfT = wide[:, 3072:4096].rearrange("p (k t) -> p k t", k=2)

        def raw(g):
            u, s = divmod(g, UG)
            if s < 2:
                return raw_sb[:, s]
            if u == 0:
                return NT[:, s, UT:2 * UT].rearrange("p (c t) -> p c t", c=4)
            return coef[:, s - 2, 0:UT].rearrange("p (c t) -> p c t", c=4)

        NTf = NT[:, :, :].rearrange("p a t -> p (a t)")
        at = [0]

        def over(n):
            at[0] += n
            return NTf[:, at[0] - n:at[0]]

        fc1_sb = over(NE * 256).rearrange("p (e f) -> p e f", e=NE)
        fc2_raw = over(NE * 128).rearrange("p (e f) -> p e f", e=NE)
        coeff = coef[:, :, :].rearrange("p a t -> p (a t)")
        at2 = [0]

        def over2(n):
            at2[0] += n
            return coeff[:, at2[0] - n:at2[0]]

        fc2_sb = over2(NE * 128).rearrange("p (e f) -> p e f", e=NE)
        fb_sb = over2(NE * 3).rearrange("p (e f) -> p e f", e=NE)
        fcb_sb = over2(128)
        x1T = over2(T)
        qT = over2(T)
        kcT = over2(S)
        v_sb = over2(2 * 128).rearrange("p (j d) -> p j d", j=2)
        probs = over2(TT * S).rearrange("p (t s) -> p t s", t=TT)
        pT = over2(TT * 2 * 128).rearrange("p (t j q) -> p t j q", t=TT, j=2)
        x2T = over2(T)
        combT = over2(T)
        ga = dt_rep[:, 0:1024].rearrange("p (s t) -> p s t", s=2)
        act_a = dt_rep[:, 1024:2048].rearrange("p (s t) -> p s t", s=2)
        acc = dt_rep[:, 2048:2560].rearrange("p (t d) -> p t d", t=TT)
        tiny = dt_rep[:, 2560:3072]
        negmax = tiny[:, 0:4]
        sums = tiny[:, 4:8]
        rsum = tiny[:, 8:12]
        score = tiny[:, 16:16 + TT * E].rearrange("p (t e) -> p t e", t=TT)
        top8 = tiny[:, 80:112].rearrange("p (t e) -> p t e", t=TT)
        left = tiny[:, 112:112 + TT * E].rearrange("p (t e) -> p t e", t=TT)
        comb = tiny[:, 176:240].rearrange("p (t e) -> p t e", t=TT)
        topsum = tiny[:, 240:244]
        gmax = tiny[:, 244:248]
        gsum = tiny[:, 248:252]
        grec = tiny[:, 252:256]

        P = [ctx.enter_context(nc.psum_tensor(f"bank{i}", [128, 512], f32)) for i in range(8)]

        consts_in = sig("consts_in")
        prep_act = sig("prep_act")
        prep_dve = sig("prep_dve")
        prep_pool = sig("prep_pool")
        x_loaded = sig("x_loaded")
        wbc_loaded = [sig("wbc_loaded0"), sig("wbc_loaded1")]
        a_full = sig("a_full")
        a_free = sig("a_free")
        v_full = sig("v_full")
        v_free = sig("v_free")
        pads = sig("pads")
        dt_steps = sig("dt_steps")
        conv_steps = sig("conv_steps")
        silu_done = sig("silu_done")
        na_done = sig("na_done")
        w_steps = sig("w_steps")
        lnw_done = sig("lnw_done")
        sq_done = sig("sq_done")
        rec_steps = sig("rec_steps")
        sums_done = sig("sums_done")
        inv_done = sig("inv_done")
        norm_acc = sig("norm_acc")
        norm_root = sig("norm_root")
        rn_steps = sig("rn_steps")
        pool_main = sig("pool_main")
        main_steps = sig("main_steps")
        phi_done = sig("phi_done")
        um_done = sig("um_done")
        dx_psum = sig("dx_psum")
        dx_done = sig("dx_done")
        gate_full = sig("gate_full")
        gate_done = sig("gate_done")
        su_done = sig("su_done")
        state_steps = sig("state_steps")
        xbd_done = sig("xbd_done")
        y_done = sig("y_done")
        yf_steps = sig("yf_steps")
        yft_full = sig("yft_full")
        yft_done = sig("yft_done")
        mix_full = sig("mix_full")
        ln_steps = sig("ln_steps")
        ln_root = sig("ln_root")
        ctx_in = sig("ctx_in")

        ffn_in = sig("ffn_in")
        x1_full = sig("x1_full")
        x1_done = sig("x1_done")
        qkv_full = sig("qkv_full")
        qkv_done = sig("qkv_done")
        s_full = sig("s_full")
        s_max = sig("s_max")
        p_done = sig("p_done")
        pt_full = sig("pt_full")
        pt_done = sig("pt_done")
        o_full = sig("o_full")
        x_steps = sig("x_steps")
        ln2_root = sig("ln2_root")
        x2_full = sig("x2_full")
        x2_done = sig("x2_done")
        lg_full = sig("lg_full")
        lg_exp = sig("lg_exp")
        route = sig("route")
        ct_full = sig("ct_full")
        ct_done = sig("ct_done")
        hg_full = sig("hg_full")
        hx_full = sig("hx_full")
        gelu_done = sig("gelu_done")
        glu_done = sig("glu_done")
        base = sig("base")
        e_full = sig("e_full")
        acc_steps = sig("acc_steps")
        ln3_root = sig("ln3_root")
        scaled = sig("scaled")
        stored = sig("stored")

        act_ring, dve_ring = ring_orders()
        a_at = {k: i for i, k in enumerate(act_ring)}
        v_at = {k: i for i, k in enumerate(dve_ring)}

        def a_bank(key):
            return P[a_at[key] % 2]

        def v_bank(key):
            return P[2 + v_at[key] % 2]

        def grp(g):
            return slice(g * T, (g + 1) * T)

        def layer_norm(dve, steps, root, src, dst):
            if made(steps):
                dve.wait_ge(steps, made(steps))
            for t in range(TT):
                dve.bn_stats(stats[:, t, :], src[:, t, :]).then_inc(steps, one(steps))
            dve.wait_ge(steps, made(steps))
            for t in range(TT):
                dve.bn_aggr(mv[:, t, :], stats[:, t, :]).then_inc(steps, one(steps))
            dve.wait_ge(root, 1)
            dve.reciprocal(rstd[:, :], rstd[:, :]).then_inc(steps, one(steps))
            dve.wait_ge(steps, made(steps))
            for t in range(TT):
                dve.tensor_scalar(dst[:, t, :], src[:, t, :], mv[:, t, 0:1], rstd[:, t:t + 1],
                                           ALU.subtract, ALU.mult).then_inc(steps, one(steps))

        CONSTS = [(onehot_sb, onehot), (tiled_sb, tiled_eye), (causal_sb, causal),
                  (chunk_sb, chunk_on), (own_sb, own_head), (eye_sb, eye), (win_sb, WinT),
                  (dtb_sb, dtb), (cb_sb, cb), (gw_sb, gwT), (bv_sb, bv)]

        a_in = prodf[:, 0:G]
        heads_f = raw_sb[:, 0, 0:2, :].rearrange("p a t -> p (a t)")
        dt_rows_f = raw_sb[:, 0, 2, 0:U * 128]
        rn_pick_f = raw_sb[:, 1].rearrange("p a t -> p (a t)")
        n_in = 16 * (len(CONSTS) + 12)
        with nc.Block() as block:
            @block.sync
            def _(sp):
                for dst, src in CONSTS:
                    sp.dma_start(dst[:, :], src).then_inc(consts_in, 16)
                sp.dma_start(wout_sb[:, :, :], WoutT).then_inc(consts_in, 16)
                sp.dma_start(skip_sb[:, :], skip.partition_broadcast(128)).then_inc(consts_in, 16)
                sp.dma_start(cw_sb[:, :, :], cw).then_inc(consts_in, 16)
                for j, w in enumerate((Wq, Wk, Wv)):
                    sp.dma_start(wqkv_sb[:, j, :], w).then_inc(consts_in, 16)
                sp.dma_start(bqk_sb[:, 0:1], bq).then_inc(consts_in, 16)
                sp.dma_start(bqk_sb[:, 1:2], bk).then_inc(consts_in, 16)
                sp.dma_start(a_in, A_log).then_inc(consts_in, 16)
                sp.dma_start(heads_f, heads).then_inc(consts_in, 16)
                sp.dma_start(dt_rows_f, dt_rows).then_inc(consts_in, 16)
                sp.dma_start(rn_pick_f, rn_pick).then_inc(consts_in, 16)

            @block.gpsimd
            def _(pool):
                pool.memset(ones_sb[:, :], 1.0).then_inc(prep_pool, 1)

            @block.vector
            def _(dve):
                dve.memset(eps_sb[:, :], EPS_LN).then_inc(prep_dve, 1)
                dve.wait_ge(consts_in, n_in)
                dve.tensor_copy(heads_sb[:, :], heads_f).then_inc(prep_dve, 1)
                dve.tensor_copy(dt_rows_sb[:, :], dt_rows_f).then_inc(prep_dve, 1)
                dve.tensor_copy(rn_pick_sb[:, :], rn_pick_f).then_inc(prep_dve, 1)
                dve.wait_ge(prep_act, 1)
                dve.tensor_scalar(neg_a[:, :], neg_a[:, :], -1.0, None, ALU.mult).then_inc(prep_dve, 1)

            @block.scalar
            def _(act):
                act.wait_ge(consts_in, n_in)
                act.activation(neg_a[:, :], a_in, ACT.Exp).then_inc(prep_act, 1)

        nc.all_engine_barrier()

        with nc.Fori(0, B) as b:
            with nc.Block() as block:
                @block.sync
                def _(sp):
                    sp.dma_start(x_in[:, :], xT[:, bass.ds(b * T, T)]).then_inc(x_loaded, 16)
                    sp.dma_start(
                        xres[:, :, :], x[bass.ds(b * T, T), :].rearrange("(t p) d -> p t d", p=128)).then_inc(x_loaded, 16)
                    sp.dma_start(ctx_sb[:, :], ctxT[:, bass.ds(b * S, S)]).then_inc(ctx_in, 16)
                    for g in range(G):
                        if g >= 2:
                            sp.wait_ge(a_full, a_at[("bc", g - 2, 3)] + 1)
                        sp.dma_start(
                            wbc_sb[:, g % 2].rearrange("p c k m -> p (c k m)"),
                            Wbc[g * 128:(g + 1) * 128, :]).then_inc(wbc_loaded[g % 2], 16)
                    sp.wait_ge(ctx_in, 16)

                @block.tensor
                def _(pe):
                    def ring_a(key, weights, moving):
                        k = a_at[key]
                        if k >= 2:
                            pe.wait_ge(a_free, k - 1)
                        pe.matmul(P[k % 2][:, :], weights, moving, start=True, stop=True).then_inc(a_full, 1)

                    def ring_v(key, weights, moving):
                        k = v_at[key]
                        if k >= 2:
                            pe.wait_ge(v_free, k - 1)
                        pe.matmul(P[2 + k % 2][:, :], weights, moving, start=True,
                                  stop=True).then_inc(v_full, 1)

                    pe.wait_ge(x_loaded, 32)
                    for key, col in ((("dt",), 512), (("kd",), 640), (("val", 0), 256), (("val", 1), 384)):
                        ring_a(key, win_sb[:, col:col + 128], x_in[:, :])

                    pe.wait_ge(dt_steps, DT_STEPS)
                    for g in range(UG):
                        ring_a(("dtb", g), heads_sb[:, g * 128:g * 128 + 128], dt_parts[:, :])
                    pe.wait_ge(dt_steps, C_STEPS)
                    for g in range(UG):
                        ring_v(("c", g), heads_sb[:, g * 128:g * 128 + 128], c_parts[:, :])
                    pe.wait_ge(silu_done, 2)
                    for j in range(2):
                        pe.wait_ge(a_free, a_at[("ut", j)] - 1)
                        for t in (2 * j, 2 * j + 1):
                            for h in range(2):
                                last = pe.transpose(
                                    a_bank(("ut", j))[:, (t % 2) * 256 + h * 128:(t % 2) * 256 + h * 128 + 128],
                                    vT[:, h, t * 128:t * 128 + 128], eye_sb[:, :])
                        last.then_inc(a_full, 1)

                    def bc(g, c):
                        o = a_bank(("bc", g, c))
                        if c == 0:
                            pe.wait_ge(wbc_loaded[g % 2], 16 * (g // 2 + 1))
                        pe.wait_ge(a_free, a_at[("bc", g, c)] - 1)
                        pe.matmul(o[:, :], wbc_sb[:, g % 2, c, 0, :], vT[:, 0, :], start=True, stop=False)
                        pe.matmul(o[:, :], wbc_sb[:, g % 2, c, 1, :], vT[:, 1, :], start=False,
                                  stop=True).then_inc(a_full, 1)

                    def norm_sum(u, n):
                        s, c = divmod(n, 4)
                        off = 124 - (c * 4 * UG + s * HG)
                        pe.wait_ge(sq_done, 4 * UG * u + n + 1)
                        if u and n == 0:
                            pe.wait_ge(dx_done, 2 * HG * UG * u)
                        pe.matmul(P[4][:, :], onehot_sb[:, off:off + 128], sq[:, n % 2, :],
                                  start=(n == 0), stop=(n == 4 * UG - 1)).then_inc(norm_acc, 1)

                    def u_blocks(u):
                        if u == 0:
                            pe.wait_ge(a_free, a_at[("ut", 1)] + 1)
                        for c in range(CT):
                            k = v_at[("ub", u, c)]
                            pe.wait_ge(v_free, k - 1)
                            pe.matmul(P[2 + k % 2][:, :].rearrange("p (t m) -> p t m", t=TT),
                                      tiled_sb[32 * c:32 * c + 32, :],
                                      u_tok[32 * c:32 * c + 32, :, u * 128:u * 128 + 128],
                                      start=True, stop=True).then_inc(v_full, 1)

                    def rn_cast(g):
                        for c in (BX, CZ, CX, BZ):
                            k = v_at[("rn", g, c)]
                            pick = slice((g % UG * 4 + c) * 128, (g % UG * 4 + c) * 128 + 128)
                            pe.wait_ge(v_free, k - 1)
                            pe.matmul(P[2 + k % 2][:, :], rn_pick_sb[:, pick], rn_hm[:, :],
                                      start=True, stop=False)
                            pe.matmul(P[2 + k % 2][:, :], rn_pick_sb[0:64, pick], rn_lo[:, :],
                                      start=False, stop=True).then_inc(v_full, 1)

                    def kt(g):
                        pe.wait_ge(main_steps, MAIN_STEPS * (g + 1))
                        for j in range(2):
                            o = a_bank(("kt", g, j))
                            pe.wait_ge(a_free, a_at[("kt", g, j)] - 1)
                            for t in range(TT):
                                last = pe.transpose(
                                    o[:, t * 128:t * 128 + 128],
                                    NT[:, 2 + j, g * T + t * 128:g * T + t * 128 + 128], eye_sb[:, :])
                            last.then_inc(a_full, 1)

                    def attend(g):
                        o = v_bank(("g", g))
                        pe.wait_ge(v_free, v_at[("g", g)] - 1)
                        for ch in range(NC):
                            s = slice(g * T + ch * L, g * T + ch * L + L)
                            for j in range(2):
                                for h in range(HG):
                                    r = slice(32 * h, 32 * h + 32)
                                    last = pe.matmul(o[r, ch * L:ch * L + L], NT[r, 2 + j, s], NT[r, j, s],
                                                     start=(j == 0), stop=(j == 1))
                        last.then_inc(v_full, 1)

                    def chunk_inputs(g):
                        pe.wait_ge(a_free, a_at[("kt", g, 1)] + 1)
                        pe.wait_ge(um_done, g + 1)
                        if g % UG == 0:
                            pe.wait_ge(norm_root, g // UG + 1)
                        else:
                            pe.wait_ge(dx_done, 2 * HG * g)
                        for j in range(2):
                            for t in range(TT):
                                last = pe.matmul(P[4 + j][:, t * 128:t * 128 + 128],
                                                 kT(g // UG)[:, g % 2, j, t, :],
                                                 um(g)[:, t, :, :].rearrange("p c m -> p (c m)"),
                                                 start=True, stop=True)
                            last.then_inc(dx_psum, 1)

                    def outputs(u, ch):
                        t, c = divmod(ch, CT)
                        o = P[6 + t // 2]
                        if ch == 0:
                            pe.wait_ge(v_free, v_at[("g", u * UG + UG - 1)] + 1)
                        else:
                            pe.wait_ge(xbd_done, HG * (u * (NC - 1) + ch))
                        for m in range(UG):
                            g = u * UG + m
                            col = (t % 2) * DI + g * 32
                            oo = o[32 * c:32 * c + 32, col:col + 32]
                            s = slice(g * T + ch * L, g * T + ch * L + L)
                            last = pe.matmul(oo, gm[:, s], u_bd(u)[:, c, t, m * 32:m * 32 + 32],
                                             start=True, stop=(ch == 0))
                            if ch:
                                for j in range(2):
                                    last = pe.matmul(
                                        oo, NT[:, j, s],
                                        x_bd[:, ch % 2, (j * UG + m) * 32:(j * UG + m) * 32 + 32],
                                        start=False, stop=(j == 1))
                        last.then_inc(y_done, 1)

                    for u in range(U):
                        for n in range(4 * UG):
                            bc(u * UG + n // 4, n % 4)
                            if n >= 1:
                                norm_sum(u, n - 1)
                            if u:
                                outputs(u - 1, n)
                        norm_sum(u, 4 * UG - 1)
                        u_blocks(u)
                        ring_v(("dtn", u), dt_rows_sb[:, u * 128:u * 128 + 128], dt_parts[:, :])
                        pe.wait_ge(rn_steps, RN_STEPS * (u + 1))
                        for s in range(2):
                            rn_cast(u * UG + s)
                        for s in range(UG):
                            g = u * UG + s
                            kt(g)
                            attend(g)
                            if u + 1 < U:
                                k = g + UG
                                ring_a(("dtb", k), heads_sb[:, k * 128:k * 128 + 128], dt_parts[:, :])
                                ring_a(("c", k), heads_sb[:, k * 128:k * 128 + 128], c_parts[:, :])
                            if s + 2 < UG:
                                rn_cast(g + 2)
                            chunk_inputs(g)

                    pe.wait_ge(v_free, len(dve_ring))
                    for j in range(2):
                        for t in (2 * j, 2 * j + 1):
                            last = pe.matmul(P[2 + j][:, (t % 2) * DI:(t % 2 + 1) * DI],
                                             x_in[:, t * 128:t * 128 + 128], win_sb[:, 0:DI],
                                             start=True, stop=True)
                        last.then_inc(gate_full, 1)

                    for ch in range(NC):
                        outputs(U - 1, ch)

                    pe.wait_ge(dx_done, 2 * HG * G)
                    for k in range(2):
                        pe.wait_ge(yf_steps, 4)
                        for t in range(TT):
                            last = pe.transpose(P[4 + k][:, t * 128:t * 128 + 128],
                                                yf[:, t, k * 128:k * 128 + 128], eye_sb[:, :])
                        last.then_inc(yft_full, 1)
                    pe.wait_ge(yft_done, 2)
                    for t in range(TT):
                        for k in range(2):
                            last = pe.matmul(P[0][:, t * 128:t * 128 + 128], yfT[:, k, t * 128:t * 128 + 128],
                                             wout_sb[:, k, :], start=(k == 0), stop=(k == 1))
                    last.then_inc(mix_full, 1)

                @block.scalar
                def _(act):
                    def drain(key, o, i, func, **kw):
                        act.wait_ge(a_full, a_at[key] + 1)
                        act.activation(o, i, func, **kw).then_inc(a_free, 1)

                    drain(("dt",), exp_dt, a_bank(("dt",))[:, :], ACT.Exp, bias=dtb_sb[:, :])
                    drain(("kd",), sig_k, a_bank(("kd",))[:, :], ACT.Sigmoid)
                    for h in range(2):
                        drain(("val", h), v_pad[:, h, 3:3 + T], a_bank(("val", h))[:, :], ACT.Copy)

                    def drain_dt(g):
                        act.wait_ge(a_full, a_at[("dtb", g)] + 1)
                        act.activation(coef[:, 0, grp(g)], a_bank(("dtb", g))[:, :], ACT.Copy,
                                       scale=neg_a[:, g:g + 1]).then_inc(na_done, 1)
                        act.activation(dt_rep[:, grp(g)], a_bank(("dtb", g))[:, :],
                                       ACT.Copy).then_inc(a_free, 1)

                    for g in range(UG):
                        drain_dt(g)
                    for h in range(2):
                        act.wait_ge(conv_steps, 2 * KW)
                        act.activation(vT[:, h, :], conv[:, h, :], ACT.Silu).then_inc(silu_done, 1)
                    for j in range(2):
                        drain(("ut", j), u_tok[:, 2 * j:2 * j + 2, :].rearrange("p t i -> p (t i)"),
                              a_bank(("ut", j))[:, :], ACT.Copy)

                    def drain_bc(g, c):
                        n = 4 * g + c
                        if n == 4:
                            act.wait_ge(dt_steps, C_STEPS)
                        if n == 4 * UG:
                            act.wait_ge(main_steps, MAIN_STEPS * UG)
                            act.wait_ge(dx_psum, 2 * UG)
                        if n >= 2:
                            act.wait_ge(norm_acc, n - 1)
                        act.wait_ge(a_full, a_at[("bc", g, c)] + 1)
                        act.activation(sq[:, n % 2, :], a_bank(("bc", g, c))[:, :],
                                       ACT.Square).then_inc(sq_done, 1)
                        if n == 0:
                            act.wait_ge(silu_done, 2)
                        act.activation(raw(g)[:, c, :], a_bank(("bc", g, c))[:, :],
                                       ACT.Copy).then_inc(a_free, 1)

                    def drain_dx(g):
                        for j in range(2):
                            act.wait_ge(dx_psum, 2 * g + j + 1)
                            if g == UG:
                                act.wait_ge(state_steps, STATE_STEPS * (NC - 1))
                            for h in range(HG):
                                r = slice(32 * h, 32 * h + 32)
                                act.activation(
                                    dX[r, :, j, g % UG, :],
                                    P[4 + j][r, :].rearrange("p (n h d) -> p n h d", h=HG, d=DH)[:, :, h, :],
                                    ACT.Copy).then_inc(dx_done, 1)

                    def spread(u, ch):
                        act.wait_ge(state_steps, STATE_STEPS * (u * (NC - 1) + ch))
                        if ch >= 2:
                            act.wait_ge(y_done, NC * u + ch - 1)
                        for h in range(HG):
                            act.activation(
                                x_bd[:, ch % 2].rearrange("p (m h d) -> p m h d", h=HG, d=DH)[:, :, h, :],
                                X[:, ch % 2].rearrange("p j (g d) -> p (j g) d", d=DH),
                                ACT.Copy, scale=own_sb[:, h:h + 1]).then_inc(xbd_done, 1)

                    def logs(u):
                        for g in range(u * UG, (u + 1) * UG):
                            act.wait_ge(w_steps, 2 * (g + 1))
                            act.activation(winv[:, grp(g)], winv[:, grp(g)], ACT.Ln).then_inc(lnw_done, 1)

                    for u in range(U):
                        for n in range(4 * UG):
                            drain_bc(u * UG + n // 4, n % 4)
                            if n == 3:
                                logs(u)
                            if u and n + 1 < NC:
                                spread(u - 1, n + 1)
                        act.wait_ge(norm_acc, 4 * UG * (u + 1))
                        act.activation(rn[:, :], P[4][:, :], ACT.Sqrt).then_inc(norm_root, 1)
                        for g in range(u * UG, (u + 1) * UG):
                            act.wait_ge(sums_done, g + 1)
                            act.activation(winv[:, grp(g)], winv[:, grp(g)], ACT.Exp,
                                           scale=-1.0).then_inc(inv_done, 1)
                        for g in range(u * UG, (u + 1) * UG):
                            if g % UG >= 2:
                                act.wait_ge(dx_psum, 2 * (g - 1))
                            for j in range(2):
                                drain(("kt", g, j), kT(u)[:, g % 2, j].rearrange("p t k -> p (t k)"),
                                      a_bank(("kt", g, j))[:, :], ACT.Copy)
                            if u + 1 < U:
                                drain_dt(g + UG)
                                drain(("c", g + UG), coef[:, 1, grp(g + UG)],
                                      a_bank(("c", g + UG))[:, :], ACT.Copy)
                            drain_dx(g)
                    act.wait_ge(main_steps, MAIN_STEPS * G)
                    for j in range(2):
                        act.wait_ge(gate_full, j + 1)
                        act.activation(sg[:, 2 * j:2 * j + 2, :].rearrange("p t i -> p (t i)"),
                                                    P[2 + j][:, :], ACT.Silu).then_inc(gate_done, 1)
                    for ch in range(1, NC):
                        spread(U - 1, ch)
                    for k in range(2):
                        act.wait_ge(yft_full, k + 1)
                        act.activation(yfT[:, k, :], P[4 + k][:, :], ACT.Copy).then_inc(yft_done, 1)
                    act.wait_ge(ln_steps, 9)
                    act.activation(rstd[:, :], mv[:, :, 1], ACT.Sqrt, bias=eps_sb[:, :]).then_inc(ln_root, 1)

                @block.gpsimd
                def _(pool):
                    pool.memset(v_pad[:, :, 0:3], 0.0).then_inc(pads, 1)
                    pool.memset(NT[:, ZZ, 0:UT:L], 1.0).then_inc(pads, 1)
                    pool.memset(NT[:, ZZ, UT::L], 1.0).then_inc(pads, 1)

                    def find_w(g):
                        pool.wait_ge(a_free, a_at[("dtb", g)] + 1)
                        pool.wait_ge(na_done, g + 1)
                        pool.tensor_tensor(winv[:, grp(g)], dt_rep[:, grp(g)], coef[:, 0, grp(g)],
                                           ALU.mult).then_inc(w_steps, 1)
                        if g < UG:
                            pool.wait_ge(v_free, v_at[("c", g)] + 1)
                        else:
                            pool.wait_ge(a_free, a_at[("c", g)] + 1)
                        pool.wait_ge(w_steps, 2 * g + 1)
                        pool.tensor_tensor(winv[:, grp(g)], coef[:, 1, grp(g)], winv[:, grp(g)],
                                           ALU.subtract).then_inc(w_steps, 1)

                    def states(u):
                        pool.wait_ge(dx_done, 2 * HG * UG * (u + 1))
                        phv = phi[:, :, u * UG * NC:(u + 1) * UG * NC].rearrange(
                            "p (a j) (g c) -> p a j g c", a=2, g=UG)
                        for ch in range(NC - 1):
                            if ch == 0:
                                pool.wait_ge(main_steps, MAIN_STEPS * UG * (u + 1))
                                pool.tensor_copy(
                                    st[:, 0], dX[:, 0].rearrange("p j g d -> p j (g d)")).then_inc(
                                        state_steps, one(state_steps))
                            else:
                                pool.wait_ge(state_steps, made(state_steps))
                                pool.tensor_tensor(
                                    st[:, 0], X[:, ch % 2], dX[:, ch].rearrange("p j g d -> p j (g d)"),
                                    ALU.add).then_inc(state_steps, one(state_steps))
                            pool.wait_ge(state_steps, made(state_steps))
                            for j in range(2):
                                pool.tensor_tensor(
                                    st[:, 1 + j].rearrange("p a (g d) -> p a g d", g=UG),
                                    phv[:, :, j, :, ch].unsqueeze(3).to_broadcast([128, 2, UG, DH]),
                                    st[:, 0, j].rearrange("p (g d) -> p g d", g=UG).unsqueeze(1)
                                    .to_broadcast([128, 2, UG, DH]), ALU.mult).then_inc(
                                        state_steps, one(state_steps))
                            pool.wait_ge(state_steps, made(state_steps))
                            if ch >= 2:
                                pool.wait_ge(xbd_done, HG * (u * (NC - 1) + ch - 1))
                            pool.tensor_tensor(X[:, (ch + 1) % 2], st[:, 1], st[:, 2],
                                               ALU.add).then_inc(state_steps, one(state_steps))

                    for g in range(UG):
                        find_w(g)
                    for u in range(U):
                        pool.wait_ge(rec_steps, REC_STEPS * (u + 1))
                        pool.wait_ge(inv_done, UG * (u + 1))
                        part = slice(u * UG * NC, (u + 1) * UG * NC)
                        pool.tensor_tensor(
                            phi[:, :, part], NT[:, :, u * UT + L - 1:(u + 1) * UT:L],
                            winv[:, u * UT + L - 1:(u + 1) * UT:L].unsqueeze(1)
                            .to_broadcast([128, 4, UG * NC]), ALU.mult).then_inc(phi_done, 1)
                        for g in range(u * UG, (u + 1) * UG):
                            r = raw(g)
                            pool.wait_ge(v_free, v_at[("rn", g, BX)] + 1)
                            if g >= 2:
                                pool.wait_ge(main_steps, MAIN_STEPS * (g - 1))
                            pool.tensor_tensor(nag[:, g % 2, :], coef[:, 0, grp(g)], r[:, BX, :],
                                               ALU.mult).then_inc(pool_main, 1)
                            for c in (CZ, CX):
                                pool.wait_ge(v_free, v_at[("rn", g, c)] + 1)
                                pool.tensor_tensor(r[:, c, :], r[:, c, :], winv[:, grp(g)],
                                                   ALU.mult).then_inc(pool_main, 1)
                            if g == 0:
                                pool.wait_ge(a_free, a_at[("ut", 1)] + 1)
                            pool.wait_ge(pool_main, 3 * g + 2)
                            pool.tensor_tensor(
                                um(g), u_tok[:, :, g * 32:g * 32 + 32].unsqueeze(2)
                                .to_broadcast([128, TT, CT, 32]),
                                own_sb[:, :].unsqueeze(1).unsqueeze(3).to_broadcast([128, TT, CT, 32]),
                                ALU.mult).then_inc(um_done, 1)
                            if u + 1 < U and g % UG:
                                find_w(g - 1 + UG)
                        if u + 1 < U:
                            find_w((u + 2) * UG - 1)
                        states(u)

                @block.vector
                def _(dve):
                    dve.wait_ge(a_free, a_at[("dt",)] + 1)
                    dve.tensor_scalar(exp_dt, exp_dt, EXP_CAP, None, ALU.min).then_inc(dt_steps, one(dt_steps))
                    dve.wait_ge(dt_steps, made(dt_steps))
                    dve.tensor_scalar(log_p, exp_dt, -1.0 / LOG_TERMS * (-1) ** LOG_TERMS, None,
                                                  ALU.mult).then_inc(dt_steps, one(dt_steps))
                    for k in range(LOG_TERMS - 1, 0, -1):
                        dve.wait_ge(dt_steps, made(dt_steps))
                        dve.scalar_tensor_tensor(
                            out=log_p, in0=log_p, scalar=(1.0 if k % 2 else -1.0) / k, in1=exp_dt,
                            op0=ALU.add, op1=ALU.mult).then_inc(dt_steps, one(dt_steps))
                    dve.wait_ge(dt_steps, made(dt_steps))
                    dve.tensor_scalar(exp_dt, log_p, DT_MIN, DT_MAX, ALU.max, ALU.min).then_inc(dt_steps, one(dt_steps))

                    def split(parts, value, residue):
                        dve.wait_ge(dt_steps, made(dt_steps))
                        dve.tensor_copy(parts[:, :], value).then_inc(dt_steps, one(dt_steps))
                        dve.wait_ge(dt_steps, made(dt_steps))
                        dve.tensor_tensor(residue, value, parts[:, :], ALU.subtract).then_inc(dt_steps, one(dt_steps))
                        dve.wait_ge(dt_steps, made(dt_steps))
                        dve.tensor_copy(parts[64:128, :], residue[64:128]).then_inc(dt_steps, one(dt_steps))
                        dve.wait_ge(dt_steps, made(dt_steps))
                        dve.tensor_tensor(parts[96:128, :], residue[96:128], parts[96:128, :],
                                          ALU.subtract).then_inc(dt_steps, one(dt_steps))

                    split(dt_parts, exp_dt, rest)
                    assert made(dt_steps) == DT_STEPS
                    dve.wait_ge(a_free, a_at[("kd",)] + 1)
                    dve.scalar_tensor_tensor(out=log_p, in0=sig_k, scalar=K_MAX, in1=exp_dt,
                                             op0=ALU.mult, op1=ALU.mult).then_inc(dt_steps, one(dt_steps))
                    dve.wait_ge(dt_steps, made(dt_steps))
                    dve.tensor_scalar(log_p, log_p, 1.0, None, ALU.add).then_inc(dt_steps, one(dt_steps))
                    split(c_parts, log_p, rest)
                    assert made(dt_steps) == C_STEPS

                    def drain_c(g):
                        dve.wait_ge(v_full, v_at[("c", g)] + 1)
                        dve.tensor_copy(coef[:, 1, grp(g)], v_bank(("c", g))[:, :]).then_inc(v_free, one(v_free))

                    dve.wait_ge(a_free, a_at[("val", 1)] + 1)
                    dve.wait_ge(pads, 3)
                    for k in range(KW):
                        for h in range(2):
                            if made(conv_steps) > 1:
                                dve.wait_ge(conv_steps, made(conv_steps) - 1)
                            if k == 0:
                                ins = dve.tensor_scalar(conv[:, h, :], v_pad[:, h, 0:T], cw_sb[:, h, 0:1],
                                                        cb_sb[:, h:h + 1], ALU.mult, ALU.add)
                            else:
                                ins = dve.scalar_tensor_tensor(
                                    out=conv[:, h, :], in0=v_pad[:, h, k:k + T], scalar=cw_sb[:, h, k:k + 1],
                                    in1=conv[:, h, :], op0=ALU.mult, op1=ALU.add)
                            ins.then_inc(conv_steps, one(conv_steps))
                    for g in range(UG):
                        drain_c(g)

                    def products(u):
                        lo, hi, M = u * UT, (u + 1) * UT, UG * NC
                        if u == 0:
                            dve.wait_ge(a_free, a_at[("dtb", UG - 1)] + 1)
                            dve.wait_ge(na_done, UG)
                            dve.wait_ge(v_free, made(v_free))
                            dve.wait_ge(conv_steps, made(conv_steps))
                        else:
                            dve.wait_ge(a_free, a_at[("c", G - 1)] + 1)
                            dve.wait_ge(na_done, G)
                            dve.wait_ge(main_steps, made(main_steps))
                        dve.tensor_copy(NT[:, ZS, lo:hi:L], coef[:, 0, lo:hi:L]).then_inc(rec_steps, one(rec_steps))
                        dve.tensor_copy(NT[:, SZ, lo:hi:L], dt_rep[:, lo:hi:L]).then_inc(rec_steps, one(rec_steps))
                        dve.tensor_copy(NT[:, SS, lo:hi:L], coef[:, 1, lo:hi:L]).then_inc(rec_steps, one(rec_steps))
                        for t in range(1, L):
                            dve.wait_ge(rec_steps, made(rec_steps) - (1 if t > 1 else 0))
                            dve.tensor_tensor(
                                step_b[:, t % 2], NT[:, 0:2, lo + t - 1:hi:L],
                                dt_rep[:, lo + t:hi:L].unsqueeze(1).to_broadcast([128, 2, M]),
                                ALU.mult).then_inc(rec_steps, one(rec_steps))
                            dve.wait_ge(rec_steps, made(rec_steps) - 1)
                            dve.tensor_tensor(
                                step_a,
                                NT[:, 2:4, lo + t - 1:hi:L].unsqueeze(1).to_broadcast([128, 2, 2, M]),
                                coef[:, :, lo + t:hi:L].unsqueeze(2).to_broadcast([128, 2, 2, M]),
                                ALU.mult).then_inc(rec_steps, one(rec_steps))
                            dve.wait_ge(rec_steps, made(rec_steps))
                            dve.tensor_tensor(NT[:, 0:2, lo + t:hi:L], NT[:, 0:2, lo + t - 1:hi:L],
                                              step_a[:, 0], ALU.add).then_inc(rec_steps, one(rec_steps))
                            dve.tensor_tensor(NT[:, 2:4, lo + t:hi:L], step_b[:, t % 2], step_a[:, 1],
                                              ALU.add).then_inc(rec_steps, one(rec_steps))
                            if t >= L - UG:
                                g = u * UG + t - (L - UG)
                                dve.wait_ge(lnw_done, g + 1)
                                dve.tensor_tensor_scan(winv[:, grp(g)], chunk_sb[:, :], winv[:, grp(g)],
                                                       0.0, ALU.mult, ALU.add).then_inc(sums_done, 1)
                        assert made(rec_steps) == REC_STEPS * (u + 1)

                    def own_blocks(u):
                        dve.wait_ge(rec_steps, made(rec_steps))
                        for c in range(CT):
                            dve.wait_ge(v_full, v_at[("ub", u, c)] + 1)
                            dve.tensor_tensor(
                                u_bd(u)[:, c].rearrange("p t (m h d) -> p (t m) h d", h=HG, d=DH),
                                v_bank(("ub", u, c))[:, :].rearrange("p (m h d) -> p m h d", h=HG, d=DH),
                                own_sb[:, :].unsqueeze(1).unsqueeze(3).to_broadcast([128, TT * UG, HG, DH]),
                                ALU.mult).then_inc(v_free, one(v_free))

                    def inverse_norms(u):
                        dve.wait_ge(norm_root, u + 1)
                        dve.tensor_scalar(rn[:, :], rn[:, :], EPS_NORM, None, ALU.add).then_inc(rn_steps, one(rn_steps))
                        dve.wait_ge(rn_steps, made(rn_steps))
                        dve.reciprocal(rn[:, :], rn[:, :]).then_inc(rn_steps, one(rn_steps))
                        dve.wait_ge(rn_steps, made(rn_steps))
                        dve.wait_ge(v_full, v_at[("dtn", u)] + 1)
                        dtn = v_bank(("dtn", u))
                        dve.tensor_tensor(rn[0:32, :], rn[0:32, :], dtn[0:32, :],
                                          ALU.mult).then_inc(rn_steps, one(rn_steps))
                        dve.tensor_tensor(rn[64:96, :], rn[64:96, :], dtn[64:96, :],
                                          ALU.mult).then_inc(v_free, one(v_free))
                        dve.wait_ge(v_free, made(v_free))
                        dve.tensor_copy(rn_hm[:, :], rn[:, :]).then_inc(rn_steps, one(rn_steps))
                        dve.wait_ge(rn_steps, made(rn_steps))
                        dve.tensor_tensor(rn[:, :], rn[:, :], rn_hm[:, :], ALU.subtract).then_inc(rn_steps, one(rn_steps))
                        dve.wait_ge(rn_steps, made(rn_steps))
                        dve.tensor_copy(rn_hm[0:64, :], rn[0:64, :]).then_inc(rn_steps, one(rn_steps))
                        dve.wait_ge(rn_steps, made(rn_steps))
                        dve.tensor_tensor(rn_lo[:, :], rn[0:64, :], rn_hm[0:64, :],
                                          ALU.subtract).then_inc(rn_steps, one(rn_steps))
                        assert made(rn_steps) == RN_STEPS * (u + 1)

                    def normalise(g):
                        for c in (BX, CZ, CX, BZ):
                            dve.wait_ge(a_free, a_at[("bc", g, c)] + 1)
                            dve.wait_ge(v_full, v_at[("rn", g, c)] + 1)
                            dve.tensor_tensor(raw(g)[:, c, :], raw(g)[:, c, :],
                                              v_bank(("rn", g, c))[:, :], ALU.mult).then_inc(v_free, one(v_free))

                    def plane(p, g):
                        return NT[:, p, grp(g)]

                    def before(a):
                        return a.rearrange("p (c t) -> p c t", t=L)[:, :, 0:L - 1]

                    def after(a):
                        return a.rearrange("p (c t) -> p c t", t=L)[:, :, 1:L]

                    def q_kappa(g):
                        r = raw(g)
                        dve.wait_ge(pool_main, 3 * g + 1)
                        dve.wait_ge(v_free, made(v_free))
                        dve.tensor_tensor(r[:, BZ, :], r[:, BZ, :], nag[:, g % 2, :],
                                                        ALU.subtract).then_inc(main_steps, one(main_steps))
                        dve.tensor_tensor(after(prod[:, 0, 1, :]), before(plane(ZZ, g)),
                                                        after(r[:, BX, :]), ALU.mult).then_inc(main_steps, one(main_steps))
                        if made(main_steps) > 1:
                            dve.wait_ge(main_steps, made(main_steps) - 1)
                        dve.tensor_tensor(after(prod[:, 1, 0, :]), before(plane(ZS, g)),
                                                        after(r[:, BX, :]), ALU.mult).then_inc(main_steps, one(main_steps))
                        if made(main_steps) > 1:
                            dve.wait_ge(main_steps, made(main_steps) - 1)
                        dve.tensor_tensor(after(prod[:, 0, 0, :]), before(plane(SS, g)),
                                                        after(r[:, BZ, :]), ALU.mult).then_inc(main_steps, one(main_steps))
                        if made(main_steps) > 1:
                            dve.wait_ge(main_steps, made(main_steps) - 1)
                        dve.tensor_tensor(after(prod[:, 1, 1, :]), before(plane(SZ, g)),
                                                        after(r[:, BZ, :]), ALU.mult).then_inc(main_steps, one(main_steps))
                        dve.wait_ge(pool_main, 3 * g + 3)
                        dve.wait_ge(phi_done, g // UG + 1)
                        if made(main_steps) > 1:
                            dve.wait_ge(main_steps, made(main_steps) - 1)
                        dve.tensor_tensor(
                            NT[:, 0:2, grp(g)], NT[:, 0:2, grp(g)],
                            r[:, CZ, :].unsqueeze(1).to_broadcast([128, 2, T]), ALU.mult).then_inc(main_steps, one(main_steps))
                        if made(main_steps) > 1:
                            dve.wait_ge(main_steps, made(main_steps) - 1)
                        dve.tensor_tensor(
                            NT[:, 2:4, grp(g)], NT[:, 2:4, grp(g)],
                            r[:, CX, :].unsqueeze(1).to_broadcast([128, 2, T]), ALU.mult).then_inc(main_steps, one(main_steps))
                        dve.wait_ge(main_steps, made(main_steps))
                        dve.tensor_tensor(NT[:, 0:2, grp(g)], NT[:, 0:2, grp(g)],
                                                        NT[:, 2:4, grp(g)], ALU.add).then_inc(main_steps, one(main_steps))
                        dve.wait_ge(main_steps, made(main_steps))
                        kv = NT[:, 2:4, grp(g)].rearrange("p j (c t) -> p j c t", t=L)
                        pv = prod[:, :, :, :].rearrange("p s j (c t) -> p s j c t", t=L)
                        dve.tensor_tensor(kv[:, :, :, 1:L], pv[:, 0, :, :, 1:L],
                                                        pv[:, 1, :, :, 1:L], ALU.subtract).then_inc(main_steps, one(main_steps))
                        dve.tensor_copy(kv[:, :, :, 0],
                                                      r[:, 0:2, :].rearrange("p j (c t) -> p j c t", t=L)[:, :, :, 0]).then_inc(main_steps, one(main_steps))
                        assert made(main_steps) == MAIN_STEPS * (g + 1)

                    def mask(g):
                        dve.wait_ge(v_full, v_at[("g", g)] + 1)
                        dve.tensor_tensor(
                            gm[:, grp(g)].rearrange("p (c t) -> p c t", t=L),
                            v_bank(("g", g))[:, :].rearrange("p (c t) -> p c t", t=L),
                            causal_sb[:, :].unsqueeze(1).to_broadcast([128, NC, L]), ALU.mult).then_inc(v_free, one(v_free))

                    for u in range(U):
                        products(u)
                        own_blocks(u)
                        inverse_norms(u)
                        if u:
                            dve.wait_ge(y_done, NC * u)
                        g0 = u * UG
                        normalise(g0)
                        normalise(g0 + 1)
                        for s in range(UG):
                            if s or u:
                                dve.wait_ge(main_steps, made(main_steps))
                            q_kappa(g0 + s)
                            if s >= 1:
                                mask(g0 + s - 1)
                                if s + 1 < UG:
                                    normalise(g0 + s + 1)
                        mask(g0 + UG - 1)

                    dve.wait_ge(main_steps, made(main_steps))
                    dve.tensor_tensor(su, u_tok[:, :, :],
                                      skip_sb[:, :].unsqueeze(1).to_broadcast([128, TT, DI]),
                                      ALU.mult).then_inc(su_done, 1)

                    dve.wait_ge(su_done, 1)
                    dve.wait_ge(gate_done, 2)
                    for j in range(2):
                        dve.wait_ge(y_done, (U - 1) * NC + 8 * (j + 1))
                        dve.tensor_tensor(
                            yf[:, 2 * j:2 * j + 2, :].rearrange("p t i -> p (t i)"), P[6 + j][:, :],
                            su[:, 2 * j:2 * j + 2, :].rearrange("p t i -> p (t i)"), ALU.add).then_inc(yf_steps, one(yf_steps))
                        dve.wait_ge(yf_steps, made(yf_steps))
                        dve.tensor_tensor(yf[:, 2 * j:2 * j + 2, :], yf[:, 2 * j:2 * j + 2, :],
                                                      sg[:, 2 * j:2 * j + 2, :], ALU.mult).then_inc(yf_steps, one(yf_steps))
                    dve.wait_ge(mix_full, 1)
                    dve.tensor_tensor(xres[:, :, :], xres[:, :, :],
                                                  P[0][:, :].rearrange("p (t d) -> p t d", t=TT), ALU.add).then_inc(ln_steps, one(ln_steps))
                    layer_norm(dve, ln_steps, ln_root, xres, xres)

            with nc.Block() as block:
                @block.sync
                def _(sp):
                    sp.dma_start(fb_sb, fcol).then_inc(ffn_in, 16)
                    sp.dma_start(fcb_sb[0:E + 1, :], fc2b).then_inc(ffn_in, 16)
                    sp.dma_start(fc2_raw, fc2T).then_inc(ffn_in, 16)
                    sp.dma_start(fc1_sb, fc1T).then_inc(ffn_in, 16)
                    sp.wait_ge(acc_steps, ACC_STEPS)
                    sp.dma_start(
                        out[bass.ds(b * T, T), :].rearrange("(t p) d -> p t d", p=128), acc).then_inc(stored, 16)
                    sp.wait_ge(stored, 16)

                @block.gpsimd
                def _(pool):
                    pool.wait_ge(ffn_in, 64)
                    for e in range(NE):
                        pool.tensor_scalar(fc2_sb[:, e, :], fc2_raw[:, e, :], fb_sb[:, e, 2:3], 1.0,
                                                     ALU.mult, ALU.mult).then_inc(scaled, 1)

                @block.tensor
                def _(pe):
                    for t in range(TT):
                        last = pe.transpose(P[0][:, t * 128:t * 128 + 128], xres[:, t, :], eye_sb[:, :])
                    last.then_inc(x1_full, 1)
                    pe.matmul(P[2][:, 0:S], wqkv_sb[:, 1, :], ctx_sb[:, :], start=True, stop=True).then_inc(qkv_full, 1)
                    for j in range(2):
                        pe.matmul(P[3][0:SH, j * 128:j * 128 + 128], ctx_sb[:, j * SH:(j + 1) * SH],
                                  wqkv_sb[:, 2, :], start=True, stop=False)
                        last = pe.matmul(P[3][0:SH, j * 128:j * 128 + 128], ones_sb[0:1, 0:SH], bv_sb[0:1, :],
                                         start=False, stop=True)
                    last.then_inc(qkv_full, 1)
                    pe.wait_ge(x1_done, 1)
                    pe.matmul(P[1][:, :], wqkv_sb[:, 0, :], x1T, start=True, stop=True).then_inc(qkv_full, 1)
                    pe.wait_ge(qkv_done, 3)
                    for t in range(TT):
                        last = pe.matmul(P[4 + t // 2][:, (t % 2) * S:(t % 2 + 1) * S],
                                         qT[:, t * 128:t * 128 + 128], kcT, start=True, stop=True)
                        last.then_inc(s_full, 1)
                    for t in range(TT):
                        pe.wait_ge(p_done, t + 1)
                        for j in range(2):
                            last = pe.transpose(
                                P[6 + t // 2][0:SH, (t % 2) * 256 + j * 128:(t % 2) * 256 + j * 128 + 128],
                                probs[:, t, j * SH:(j + 1) * SH], eye_sb[:, :])
                        last.then_inc(pt_full, 1)
                    for t in range(TT):
                        pe.wait_ge(pt_done, t // 2 + 1)
                        for j in range(2):
                            last = pe.matmul(P[0][:, t * 128:t * 128 + 128], pT[0:SH, t, j, :], v_sb[0:SH, j, :],
                                             start=(j == 0), stop=(j == 1))
                    last.then_inc(o_full, 1)
                    pe.wait_ge(x_steps, X_STEPS)
                    for t in range(TT):
                        last = pe.transpose(P[1][:, t * 128:t * 128 + 128], xres[:, t, :], eye_sb[:, :])
                    last.then_inc(x2_full, 1)
                    pe.wait_ge(x2_done, 1)
                    for t in range(TT):
                        last = pe.matmul(P[2][:, t * E:(t + 1) * E], x2T[:, t * 128:t * 128 + 128], gw_sb[:, :],
                                         start=True, stop=True)
                    last.then_inc(lg_full, 1)

                    pe.wait_ge(ffn_in, 64)

                    def up(i):
                        e = ORDER[i]
                        if i >= 2:
                            pe.wait_ge(gelu_done, i - 1)
                        pe.matmul(P[4 + i % 2][:, :], fc1_sb[:, e, 128:256], x2T,
                                             start=True, stop=True).then_inc(hg_full, 1)
                        if i >= 2:
                            pe.wait_ge(glu_done, i - 1)
                        pe.matmul(P[6 + i % 2][:, :], fc1_sb[:, e, 0:128], x2T,
                                             start=True, stop=True).then_inc(hx_full, 1)

                    def down(i):
                        e = ORDER[i]
                        pe.wait_ge(glu_done, i + 1)
                        pe.wait_ge(scaled, e + 1)
                        if e >= E:
                            for t in range(TT):
                                last = pe.matmul(P[3][:, t * 128:t * 128 + 128],
                                                 act_a[:, i % 2, t * 128:t * 128 + 128], fc2_sb[:, e, :],
                                                 start=(e == E and t == 0), stop=False, skip_group_check=True)
                            last.then_inc(base, 1)
                            if e == NE - 1:
                                pe.wait_ge(ct_done, 1)
                                for t in range(TT):
                                    last = pe.matmul(P[3][:, t * 128:t * 128 + 128],
                                                     combT[0:E + 1, t * 128:t * 128 + 128], fcb_sb[0:E + 1, :],
                                                     start=False, stop=(t == TT - 1), skip_group_check=True)
                                last.then_inc(base, 1)
                        else:
                            if e >= 2:
                                pe.wait_ge(acc_steps, 1 + TT * (e - 1))
                            for t in range(TT):
                                last = pe.matmul(P[e % 2][:, t * 128:t * 128 + 128],
                                                 act_a[:, i % 2, t * 128:t * 128 + 128], fc2_sb[:, e, :],
                                                 start=True, stop=True)
                            last.then_inc(e_full, 1)

                    up(0)
                    pe.wait_ge(route, ROUTE_STEPS)
                    for t in range(TT):
                        last = pe.transpose(P[2][0:E + 1, t * 128:t * 128 + 128], comb[:, t, :], eye_sb[:, :])
                    last.then_inc(ct_full, 1)
                    for i in range(NE):
                        if i + 1 < NE:
                            up(i + 1)
                        down(i)

                @block.scalar
                def _(act):
                    act.wait_ge(x1_full, 1)
                    act.activation(x1T, P[0][:, :], ACT.Copy).then_inc(x1_done, 1)
                    act.wait_ge(qkv_full, 1)
                    act.activation(kcT, P[2][:, 0:S], ACT.Identity, bias=bqk_sb[:, 1:2]).then_inc(qkv_done, 1)
                    act.wait_ge(qkv_full, 2)
                    act.activation(v_sb[0:SH].rearrange("p j d -> p (j d)"), P[3][0:SH, 0:256],
                                               ACT.Copy).then_inc(qkv_done, 1)
                    act.wait_ge(qkv_full, 3)
                    act.activation(qT, P[1][:, :], ACT.Identity, bias=bqk_sb[:, 0:1]).then_inc(qkv_done, 1)
                    for t in range(TT):
                        act.wait_ge(s_max, t // 2 + 1)
                        act.activation(probs[:, t, :], P[4 + t // 2][:, (t % 2) * S:(t % 2 + 1) * S],
                                                 ACT.Exp, bias=negmax[:, t:t + 1], accum_out=sums[:, t:t + 1]).then_inc(p_done, 1)
                    for j in range(2):
                        act.wait_ge(pt_full, 2 * j + 2)
                        act.activation(
                            pT[0:SH, 2 * j:2 * j + 2].rearrange("p t j q -> p (t j q)"), P[6 + j][0:SH, :],
                            ACT.Copy).then_inc(pt_done, 1)
                    act.wait_ge(x_steps, X_STEPS - 1 - TT)
                    act.activation(rstd[:, :], mv[:, :, 1], ACT.Sqrt, bias=eps_sb[:, :]).then_inc(ln2_root, 1)
                    act.wait_ge(x2_full, 1)
                    act.activation(x2T, P[1][:, :], ACT.Copy).then_inc(x2_done, 1)
                    for t in range(TT):
                        act.wait_ge(route, 2)
                        act.activation(score[:, t, :], P[2][:, t * E:(t + 1) * E], ACT.Exp,
                                                 bias=gmax[:, t:t + 1], accum_out=gsum[:, t:t + 1]).then_inc(lg_exp, 1)
                    for i in range(NE):
                        e = ORDER[i]
                        act.wait_ge(hg_full, i + 1)
                        if i >= 2:
                            act.wait_ge(glu_done, i - 1)
                        act.activation(ga[:, i % 2, :], P[4 + i % 2][:, :], ACT.Gelu,
                                                    bias=fb_sb[:, e, 0:1]).then_inc(gelu_done, 1)
                        if i == 0:
                            act.wait_ge(ct_full, 1)
                            act.activation(combT[0:E + 1, :], P[2][0:E + 1, :], ACT.Copy).then_inc(ct_done, 1)
                    act.wait_ge(acc_steps, ACC_STEPS - 1 - TT)
                    act.activation(rstd[:, :], mv[:, :, 1], ACT.Sqrt, bias=eps_sb[:, :]).then_inc(ln3_root, 1)

                @block.vector
                def _(dve):
                    for j in range(2):
                        dve.wait_ge(s_full, 2 * j + 2)
                        dve.tensor_reduce(
                            out=negmax[:, 2 * j:2 * j + 2],
                            in_=P[4 + j][:, 0:2 * S].rearrange("p (t s) -> p t s", s=S), axis=AX,
                            op=ALU.max, negate=True).then_inc(s_max, 1)
                    dve.wait_ge(p_done, TT)
                    dve.reciprocal(rsum, sums).then_inc(x_steps, one(x_steps))
                    dve.wait_ge(o_full, 1)
                    dve.wait_ge(x_steps, made(x_steps))
                    for t in range(TT):
                        dve.scalar_tensor_tensor(
                            out=xres[:, t, :], in0=P[0][:, t * 128:t * 128 + 128], scalar=rsum[:, t:t + 1],
                            in1=xres[:, t, :], op0=ALU.mult, op1=ALU.add).then_inc(x_steps, one(x_steps))
                    layer_norm(dve, x_steps, ln2_root, xres, xres)
                    assert made(x_steps) == X_STEPS
                    dve.wait_ge(lg_full, 1)
                    lg = P[2][:, 0:TT * E].rearrange("p (t e) -> p t e", t=TT)
                    dve.tensor_reduce(out=gmax, in_=lg, axis=AX, op=ALU.max, negate=True).then_inc(route, one(route))
                    dve.memset(comb[:, :, E:E + 1], 1.0).then_inc(route, one(route))
                    dve.wait_ge(lg_exp, TT)
                    dve.reciprocal(grec, gsum).then_inc(route, one(route))
                    dve.wait_ge(route, made(route))
                    dve.tensor_tensor(score, score, grec.unsqueeze(2).to_broadcast([128, TT, E]),
                                               ALU.mult).then_inc(route, one(route))
                    dve.wait_ge(route, made(route))
                    for t in range(TT):
                        dve.max(top8[:, t, :], score[:, t, :]).then_inc(route, one(route))
                    dve.wait_ge(route, made(route))
                    dve.tensor_reduce(out=topsum, in_=top8[:, :, 0:TOPK], axis=AX, op=ALU.add).then_inc(route, one(route))
                    dve.memset(top8[:, :, TOPK:8], -1.0).then_inc(route, one(route))
                    dve.wait_ge(route, made(route))
                    for t in range(TT):
                        dve.match_replace(left[:, t, :], top8[:, t, :], score[:, t, :], -2.0).then_inc(route, one(route))
                    dve.tensor_scalar(topsum, topsum, EPS_TOP, None, ALU.add).then_inc(route, one(route))
                    dve.wait_ge(route, made(route))
                    dve.reciprocal(topsum, topsum).then_inc(route, one(route))
                    dve.scalar_tensor_tensor(out=comb[:, :, 0:E], in0=left, scalar=0.0, in1=score,
                                                      op0=ALU.is_lt, op1=ALU.mult).then_inc(route, one(route))
                    dve.wait_ge(route, made(route))
                    dve.tensor_tensor(comb[:, :, 0:E], comb[:, :, 0:E],
                                               topsum.unsqueeze(2).to_broadcast([128, TT, E]), ALU.mult).then_inc(route, one(route))
                    assert made(route) == ROUTE_STEPS
                    dve.wait_ge(route, made(route))

                    def glu(i):
                        e = ORDER[i]
                        dve.wait_ge(hx_full, i + 1)
                        dve.wait_ge(gelu_done, i + 1)
                        dve.scalar_tensor_tensor(
                            out=act_a[:, i % 2, :], in0=P[6 + i % 2][:, :], scalar=fb_sb[:, e, 1:2],
                            in1=ga[:, i % 2, :], op0=ALU.add, op1=ALU.mult).then_inc(glu_done, 1)

                    def add_up(e):
                        dve.wait_ge(e_full, e + 1)
                        for t in range(TT):
                            if t == 0:
                                dve.wait_ge(acc_steps, made(acc_steps))
                            dve.scalar_tensor_tensor(
                                out=acc[:, t, :], in0=P[e % 2][:, t * 128:t * 128 + 128],
                                scalar=comb[:, t, e:e + 1], in1=acc[:, t, :], op0=ALU.mult, op1=ALU.add).then_inc(acc_steps, one(acc_steps))

                    for i in range(NE):
                        if i >= 2:
                            if i - 2 < 2:
                                dve.wait_ge(base, 1 if i == 2 else 3)
                            else:
                                dve.wait_ge(e_full, i - 3)
                        glu(i)
                        if i == 2:
                            dve.wait_ge(base, 3)
                            dve.tensor_tensor(
                                acc, P[3][:, :].rearrange("p (t d) -> p t d", t=TT), xres[:, :, :], ALU.add).then_inc(acc_steps, one(acc_steps))
                        if i >= 3:
                            add_up(i - 3)
                    add_up(E - 1)
                    layer_norm(dve, acc_steps, ln3_root, acc, acc)
                    assert made(acc_steps) == ACC_STEPS

            nc.all_engine_barrier(sems_to_clear=range(signals[0].num, signals[-1].num + 1))


def kernel(**inputs):
    import numpy as np
    import concourse.bacc as bacc
    from concourse.bass_utils import run_bass_kernel_spmd as run

    a = {k: np.asarray(v) for k, v in inputs.items()}
    w_in = a["L0_attn_W_in"]
    par = w_in[2 * DI:].reshape(H, 2, D)
    part = np.arange(128)
    f1 = a["L0_ffn_fc1_w"].transpose(2, 0, 1)
    s1 = a["L0_ffn_s_fc1_w"].reshape(2, 2, F, D).transpose(3, 1, 0, 2).reshape(D, 2, 2 * F)
    b1 = a["L0_ffn_fc1_b"].reshape(E, 2, F).transpose(2, 0, 1)[:, :, ::-1]
    sb1 = a["L0_ffn_s_fc1_b"].reshape(2, 2, F).transpose(2, 1, 0)[:, :, ::-1]
    f2 = a["L0_ffn_fc2_w"].transpose(2, 0, 1)
    s2 = a["L0_ffn_s_fc2_w"].reshape(D, 2, F).transpose(2, 1, 0)
    head_of = np.repeat(np.arange(H), NS)
    pick = (np.arange(UG)[:, None, None] * HG + np.arange(4)[None, :, None] * 16 + part // NS).reshape(-1)
    f = np.float32
    data = {
        "xT": a["x"].reshape(B * T, D).T,
        "x": a["x"].reshape(B * T, D),
        "ctxT": a["ctx_1024"].reshape(B * S, D).T,
        "A_log": a["L0_attn_A_log"].reshape(G, 128).T,
        "WinT": np.concatenate([w_in[:2 * DI], np.tile(par[:, 0], (4, 1)), np.tile(par[:, 1], (4, 1))]).T,
        "Wbc": a["L0_attn_W_bc"].reshape(G, HG, 4, NS, 2, 128).transpose(0, 5, 2, 4, 1, 3)
        .reshape(G * 128, 1024),
        "WoutT": a["L0_attn_W_out"].T.reshape(2, 128, D).transpose(1, 0, 2),
        "skip": a["L0_attn_skip"],
        "dtb": np.tile(a["L0_attn_dt_bias"], 4)[:, None],
        "cw": a["L0_attn_dw_weight"].reshape(2, 128, KW).transpose(1, 0, 2),
        "cb": a["L0_attn_dw_bias"].reshape(2, 128).T,
        "Wq": a["L0_xattn_Wq"], "bq": a["L0_xattn_bq"][:, None],
        "Wk": a["L0_xattn_Wk"], "bk": a["L0_xattn_bk"][:, None],
        "Wv": a["L0_xattn_Wv"], "bv": a["L0_xattn_bv"][None, :],
        "gwT": a["L0_ffn_gate_w"].T,
        "fc1T": np.concatenate([f1, s1], 1),
        "fcol": np.concatenate([
            np.concatenate([b1, sb1], 1),
            np.concatenate([a["L0_ffn_geglu_mult"].T, a["L0_ffn_s_geglu_mult"].reshape(2, F).T], 1)[:, :, None]], 2),
        "fc2T": np.concatenate([f2, s2], 1),
        "fc2b": np.concatenate([a["L0_ffn_fc2_b"], a["L0_ffn_s_fc2_b"][None, :]], 0),
        "heads": (((part[:, None] // 32 != 1) & (part[:, None] % H == head_of[None, :]))).astype(f),
        "dt_rows": ((part[:, None] // 32 != 1)
                    & (part[:, None] % H == (np.arange(U)[:, None] * 16 + part % 16).reshape(-1)[None, :])
                    ).astype(f),
        "rn_pick": (part[:, None] % 64 == pick[None, :]).astype(f),
        "onehot": ((124 + part[:, None] // NS == np.arange(252)[None, :])
                   | (188 + part[:, None] // NS == np.arange(252)[None, :])).astype(f),
        "tiled_eye": (part[:, None] % L == part[None, :] % L).astype(f),
        "causal": (np.arange(L)[None, :] >= part[:, None] % L).astype(f),
        "chunk_on": np.tile((np.arange(T) % L != 0).astype(f), (128, 1)),
        "own_head": (part[:, None] // NS == np.arange(HG)[None, :]).astype(f),
        "eye": np.eye(128, dtype=f),
    }
    nc = bacc.Bacc("TRN2", target_bir_lowering=False, num_devices=1)
    arrays, args = {}, {}
    for name, v in data.items():
        arrays[f"in_{name}"] = v = np.ascontiguousarray(v)
        args[name] = nc.dram_tensor(f"in_{name}", v.shape, mybir.dt.float32, kind="ExternalInput").ap()
    args["out"] = nc.dram_tensor("out_x", (B * T, D), mybir.dt.float32, kind="ExternalOutput").ap()
    build(nc, **args)
    r = run(nc, [arrays], core_ids=[0])
    return r.results[0]["out_x"].reshape(B, T, D)
```

```python
import concourse.bass as bass
from concourse import mybir
from contextlib import ExitStack

B, T, D = 4, 512, 128
DI, H, NS, DH, KW = 256, 32, 32, 8, 4
L = 32
NC = T // L
HG = 4
G = H // HG
UG = 4
U = G // UG
UT = UG * T
TT = T // 128
CT = 128 // L
S = 154
SH = S // 2
E, F, TOPK = 15, 128, 3
NE = E + 2
DT_MIN, DT_MAX, K_MAX = 1e-4, 0.1, 0.5
EXP_CAP = 0.106
LOG_TERMS = 9
EPS_NORM, EPS_LN, EPS_TOP = 1e-8, 1e-5, 1e-20
BZ, BX, CZ, CX = range(4)
ORDER = [E, E + 1] + list(range(E))
AHEAD = ((UG,), (UG + 1,), (UG + 2, UG + 3), ())
HEAD = [("val", 0), ("val", 1), ("dt",), ("kd",), ("ut", 0), ("ut", 1)]
LN_STEPS = 2 * TT + 1 + TT
DT_STEPS = 3 + (LOG_TERMS - 1) + 4
C_STEPS = DT_STEPS + 2 + 4
REC_STEPS = 3 + 4 * (L - 1)
RN_STEPS = 6
SCAN_AT = (13, 17, 20, 22)
MASK_AT = 12
RN_AT = (25, 30)
MAIN_STEPS = 10
STATE_STEPS = 3
X_STEPS = 1 + TT + LN_STEPS
ROUTE_STEPS = 4 + TT + 2 + TT + 4
ACC_STEPS = 1 + TT * E + LN_STEPS
ZZ, ZS, SZ, SS = range(4)


class Counts:

    def __init__(self):
        self.value = {}

    def one(self, sem):
        self.value[sem.num] = self.value.get(sem.num, 0) + 1
        return 1

    def made(self, sem):
        return self.value.get(sem.num, 0)


def ring_orders():
    act = [("dtb", g) for g in range(UG)]
    dve = [("c", g) for g in range(UG)]
    for u in range(U):
        act += [("bc", u * UG + s, c) for s in range(u, UG) for c in range(4)]
        dve += [("dtn", 2 * u)] + [("rn", u * UG, c) for c in (BX, CZ, CX, BZ)]
        act += [("ub", u, c) for c in range(CT)]
        for s in range(UG):
            g = u * UG + s
            act += [("kt", g, j) for j in range(2)]
            if u == 0 and s in (1, 2):
                act += [("bc", UG, s + 1)]
            if s + 1 < UG:
                dve += [("rn", g + 1, c) for c in (BX, CZ, CX, BZ)]
            dve.append(("g", g))
            if s == 0:
                dve.append(("dtn", 2 * u + 1))
            for k in AHEAD[s] if u == 0 else ():
                act += [("dtb", k), ("c", k)]
            if s == 0:
                act += [("bc", UG, 0), ("bc", UG, 1)] if u == 0 else [("gate", 0), ("gate", 1)] + HEAD[:2]
    act += HEAD[2:]
    return act, dve


def build(nc, xT, x, ctxT, WinT, Wbc, WoutT, skip, A_log, dtb, cw, cb, Wq, bq, Wk, bk, Wv, bv,
          gwT, fc1T, fcol, fc2T, fc2b, heads, dt_rows, rn_pick, onehot, tiled_eye, causal,
          chunk_on, own_head, eye, out):
    f32 = mybir.dt.float32
    bf16 = mybir.dt.bfloat16
    ALU = mybir.AluOpType
    ACT = mybir.ActivationFunctionType
    AX = mybir.AxisListType.X
    ctx = ExitStack()
    with ctx:
        def sb(name, *shape, dtype=f32):
            return ctx.enter_context(nc.sbuf_tensor(name, list(shape), dtype))

        signals = []
        counts = Counts()
        one, made = counts.one, counts.made

        def sig(name):
            s = ctx.enter_context(nc.semaphore(name))
            signals.append(s)
            return s

        heads_sb = sb("heads_sb", 128, H * NS, dtype=bf16)
        dt_rows_sb = sb("dt_rows_sb", 128, G // 2 * 128, dtype=bf16)
        rn_pick_sb = sb("rn_pick_sb", 128, 2 * 4 * 128, dtype=bf16)
        neg_a = sb("neg_a", 128, G)
        onehot_sb = sb("onehot_sb", 128, 252)
        tiled_sb = sb("tiled_sb", 128, 128)
        causal_sb = sb("causal_sb", 128, L)
        chunk_sb = sb("chunk_sb", 128, T)
        own_sb = sb("own_sb", 128, HG + 1)
        eye_sb = sb("eye_sb", 128, 128)
        win_sb = sb("win_sb", 128, 768)
        wout_sb = sb("wout_sb", 128, 2, 128)
        skip_sb = sb("skip_sb", 128, DI)
        dtb_sb = sb("dtb_sb", 128, 1)
        cw_sb = sb("cw_sb", 128, 2, KW)
        cb_sb = sb("cb_sb", 128, 2)
        wqkv_sb = sb("wqkv_sb", 128, 3, 128)
        bqk_sb = sb("bqk_sb", 128, 2)
        bv_sb = sb("bv_sb", 1, 128)
        ones_sb = sb("ones_sb", 1, 128)
        gw_sb = sb("gw_sb", 128, E)
        eps_sb = sb("eps_sb", 128, 1)

        x_in = sb("x_in", 128, T)
        NT = sb("NT", 128, 4, G * T)
        coef = sb("coef", 128, 2, G * T)
        dt_rep = sb("dt_rep", 128, G * T)
        winv = sb("winv", 128, G * T)
        raw_sb = sb("raw_sb", 128, 2, 4, T)
        wbc_sb = sb("wbc_sb", 128, 2, 4, 2, 128)
        vT = sb("vT", 128, 2, T)
        u_tok = sb("u_tok", 128, TT, DI)
        prod = sb("prod", 128, 2, 2, T)
        nag = sb("nag", 128, 2, T)
        dt_parts = sb("dt_parts", 128, T, dtype=bf16)
        c_parts = sb("c_parts", 128, T, dtype=bf16)
        rn = sb("rn", 128, T)
        rn_parts = sb("rn_parts", 128, 2, T, dtype=bf16)
        dX = sb("dX", 128, NC, 2, UG, DH)
        ctx_sb = sb("ctx_sb", 128, S)
        phi = sb("phi", 128, 4, G * NC)
        xres = sb("xres", 128, TT, D)
        stats = sb("stats", 128, TT, 6)
        mv = sb("mv", 128, TT, 2)
        rstd = sb("rstd", 128, TT)

        prodf = prod[:, :, :, :].rearrange("p a b t -> p (a b t)")
        step_a = prodf[:, 0:256].rearrange("p (r j m) -> p r j m", r=2, j=2)
        step_b = prodf[:, 256:512].rearrange("p (s j m) -> p s j m", s=2, j=2)

        def chain(u, first, end, steps):
            room = NT[:, 2, first:end] if u == 0 else prodf[:, 512 + first:512 + end]
            return room.rearrange("p (s m) -> p s m", s=steps)

        def x_bd(u):
            return chain(u, 0, 512, 2)

        def X(u):
            return chain(u, 512, 640, 2).rearrange("p s (j m) -> p s j m", j=2)

        def st(u):
            return chain(u, 640, 832, 3).rearrange("p s (j m) -> p s j m", j=2)
        conv = NT[:, 2, 0:2 * T].rearrange("p (h t) -> p h t", h=2)
        exp_dt = NT[:, 2, 2 * T:3 * T]
        sig_k = NT[:, 2, 3 * T:4 * T]
        v_pad = NT[:, 3, 0:2 * (T + 3)].rearrange("p (h t) -> p h t", h=2)
        log_p = NT[:, 3, 3 * T:4 * T]
        rest = NT[:, 3, UT:UT + T]
        x_next = NT[:, 1, T:2 * T]
        sq = nag
        gm = winv

        def minus_dt_a_g(g):
            return NT[:, 3, T:2 * T] if g == UG else nag[:, g % 2, :]

        def u_bd(u):
            return dt_rep[:, u * UT:(u + 1) * UT].rearrange("p (c t m) -> p c t m", c=CT, t=TT)

        def um(g):
            return coef[:, 0, g * T:(g + 1) * T].rearrange("p (t c m) -> p t c m", t=TT, c=CT)

        def kT(u):
            return coef[:, 1, u * UT:(u + 1) * UT].rearrange("p (s c t k) -> p s c t k", s=2, c=2, t=TT)
        wide = raw_sb[:, :, :, :].rearrange("p s c t -> p (s c t)")
        su = wide[:, 0:1024].rearrange("p (t i) -> p t i", t=TT)
        sg = wide[:, 1024:2048].rearrange("p (t i) -> p t i", t=TT)
        yf = wide[:, 2048:3072].rearrange("p (t i) -> p t i", t=TT)
        yfT = wide[:, 3072:4096].rearrange("p (j k t) -> p j k t", j=2, k=2)

        def raw(g):
            u, s = divmod(g, UG)
            if s < 2:
                return raw_sb[:, s]
            if u == 0:
                return NT[:, s, UT:2 * UT].rearrange("p (c t) -> p c t", c=4)
            return coef[:, s - 2, 0:UT].rearrange("p (c t) -> p c t", c=4)

        NTf = NT[:, :, :].rearrange("p a t -> p (a t)")
        at = [0]

        def over(n):
            at[0] += n
            return NTf[:, at[0] - n:at[0]]

        fc1_sb = over(NE * 256).rearrange("p (e f) -> p e f", e=NE)
        fc2_raw = over(NE * 128).rearrange("p (e f) -> p e f", e=NE)
        coeff = coef[:, :, :].rearrange("p a t -> p (a t)")
        at2 = [0]

        def over2(n):
            at2[0] += n
            return coeff[:, at2[0] - n:at2[0]]

        fc2_sb = over2(NE * 128).rearrange("p (e f) -> p e f", e=NE)
        fb_sb = over2(NE * 3).rearrange("p (e f) -> p e f", e=NE)
        fcb_sb = over2(128)
        x1T = over2(T)
        qT = over2(T)
        kcT = over2(S)
        v_sb = over2(2 * 128).rearrange("p (j d) -> p j d", j=2)
        probs = over2(TT * S).rearrange("p (t s) -> p t s", t=TT)
        pT = over2(TT * 2 * 128).rearrange("p (t j q) -> p t j q", t=TT, j=2)
        x2T = over2(T)
        combT = over2(T)
        ga = dt_rep[:, 0:1024].rearrange("p (s t) -> p s t", s=2)
        act_a = dt_rep[:, 1024:2048].rearrange("p (s t) -> p s t", s=2)
        acc = dt_rep[:, 2048:2560].rearrange("p (t d) -> p t d", t=TT)
        tiny = dt_rep[:, 2560:3072]
        negmax = tiny[:, 0:4]
        sums = tiny[:, 4:8]
        rsum = tiny[:, 8:12]
        score = tiny[:, 16:16 + TT * E].rearrange("p (t e) -> p t e", t=TT)
        top8 = tiny[:, 80:112].rearrange("p (t e) -> p t e", t=TT)
        left = tiny[:, 112:112 + TT * E].rearrange("p (t e) -> p t e", t=TT)
        comb = tiny[:, 176:240].rearrange("p (t e) -> p t e", t=TT)
        topsum = tiny[:, 240:244]
        gmax = tiny[:, 244:248]
        gsum = tiny[:, 248:252]
        grec = tiny[:, 252:256]

        P = [ctx.enter_context(nc.psum_tensor(f"bank{i}", [128, 512], f32)) for i in range(8)]

        consts_in = sig("consts_in")
        prep_act = sig("prep_act")
        prep_dve = sig("prep_dve")
        prep_pool = sig("prep_pool")
        x_loaded = sig("x_loaded")
        next_loaded = sig("next_loaded")
        wbc_loaded = [sig("wbc_loaded0"), sig("wbc_loaded1")]
        a_full = sig("a_full")
        a_free = sig("a_free")
        v_full = sig("v_full")
        v_free = sig("v_free")
        pads = sig("pads")
        pad_zeros = sig("pad_zeros")
        dt_steps = sig("dt_steps")
        conv_steps = sig("conv_steps")
        silu_done = sig("silu_done")
        na_done = sig("na_done")
        w_steps = sig("w_steps")
        lnw_done = sig("lnw_done")
        sq_done = sig("sq_done")
        rec_steps = sig("rec_steps")
        sums_done = sig("sums_done")
        inv_done = sig("inv_done")
        norm_acc = sig("norm_acc")
        norm_root = sig("norm_root")
        rn_steps = sig("rn_steps")
        pool_main = sig("pool_main")
        main_steps = sig("main_steps")
        phi_done = sig("phi_done")
        um_done = sig("um_done")
        dx_psum = sig("dx_psum")
        dx_done = sig("dx_done")
        su_done = sig("su_done")
        state_steps = sig("state_steps")
        xbd_done = sig("xbd_done")
        xbd_last = sig("xbd_last")
        y_done = sig("y_done")
        yf_steps = sig("yf_steps")
        yft_full = sig("yft_full")
        yft_done = sig("yft_done")
        mix_full = sig("mix_full")
        ln_steps = sig("ln_steps")
        ln_root = sig("ln_root")
        ctx_in = sig("ctx_in")
        ub_part = sig("ub_part")

        ffn_in = sig("ffn_in")
        x1_full = sig("x1_full")
        x1_done = sig("x1_done")
        qkv_full = sig("qkv_full")
        qkv_done = sig("qkv_done")
        s_full = sig("s_full")
        s_max = sig("s_max")
        p_done = sig("p_done")
        pt_full = sig("pt_full")
        pt_done = sig("pt_done")
        o_full = sig("o_full")
        x_steps = sig("x_steps")
        ln2_root = sig("ln2_root")
        x2_full = sig("x2_full")
        x2_done = sig("x2_done")
        lg_full = sig("lg_full")
        lg_exp = sig("lg_exp")
        route = sig("route")
        ct_full = sig("ct_full")
        ct_done = sig("ct_done")
        hg_full = sig("hg_full")
        hx_full = sig("hx_full")
        gelu_done = sig("gelu_done")
        glu_done = sig("glu_done")
        base = sig("base")
        e_full = sig("e_full")
        acc_steps = sig("acc_steps")
        ln3_root = sig("ln3_root")
        scaled = sig("scaled")
        stored = sig("stored")

        act_ring, dve_ring = ring_orders()
        a_at = {k: i for i, k in enumerate(act_ring)}
        v_at = {k: i for i, k in enumerate(dve_ring)}

        def a_bank(key):
            return P[a_at[key] % 2]

        def v_bank(key):
            return P[2 + v_at[key] % 2]

        def grp(g):
            return slice(g * T, (g + 1) * T)

        def layer_norm(dve, steps, root, src, dst):
            if made(steps):
                dve.wait_ge(steps, made(steps))
            for t in range(TT):
                dve.bn_stats(stats[:, t, :], src[:, t, :]).then_inc(steps, one(steps))
            dve.wait_ge(steps, made(steps))
            for t in range(TT):
                dve.bn_aggr(mv[:, t, :], stats[:, t, :]).then_inc(steps, one(steps))
            dve.wait_ge(root, 1)
            dve.reciprocal(rstd[:, :], rstd[:, :]).then_inc(steps, one(steps))
            dve.wait_ge(steps, made(steps))
            for t in range(TT):
                dve.tensor_scalar(dst[:, t, :], src[:, t, :], mv[:, t, 0:1], rstd[:, t:t + 1],
                                           ALU.subtract, ALU.mult).then_inc(steps, one(steps))

        def split(dve, steps, parts, value, residue):
            dve.wait_ge(steps, made(steps))
            dve.tensor_copy(parts, value).then_inc(steps, one(steps))
            dve.wait_ge(steps, made(steps))
            dve.tensor_tensor(residue, value, parts, ALU.subtract).then_inc(steps, one(steps))
            dve.wait_ge(steps, made(steps))
            dve.tensor_copy(parts[64:128], residue[64:128]).then_inc(steps, one(steps))
            dve.wait_ge(steps, made(steps))
            dve.tensor_tensor(parts[96:128], residue[96:128], parts[96:128],
                              ALU.subtract).then_inc(steps, one(steps))

        def head_product(pe, at, i, loads=1):
            k = at[HEAD[i]]
            if i == 0:
                pe.wait_ge(next_loaded, 16 * loads)
            if k >= 2:
                pe.wait_ge(a_free, k - 1)
            col = (256, 384, 512, 640)[i]
            pe.matmul(P[k % 2][:, :], win_sb[:, col:col + 128], x_next, start=True,
                      stop=True).then_inc(a_full, 1)

        def head_transposes(pe, at, j):
            k = at[("ut", j)]
            pe.wait_ge(silu_done, 2)
            pe.wait_ge(a_free, k - 1)
            for t in (2 * j, 2 * j + 1):
                for h in range(2):
                    last = pe.transpose(
                        P[k % 2][:, (t % 2) * 256 + h * 128:(t % 2) * 256 + h * 128 + 128],
                        vT[:, h, t * 128:t * 128 + 128], eye_sb[:, :])
            last.then_inc(a_full, 1)

        def head_drain(act, at, i):
            k = at[HEAD[i]]
            act.wait_ge(a_full, k + 1)
            if i == 2:
                act.activation(exp_dt, P[k % 2][:, :], ACT.Exp, bias=dtb_sb[:, :]).then_inc(a_free, 1)
            elif i == 3:
                act.activation(sig_k, P[k % 2][:, :], ACT.Sigmoid).then_inc(a_free, 1)
            else:
                act.activation(v_pad[:, i, 3:3 + T], P[k % 2][:, :], ACT.Copy).then_inc(a_free, 1)

        def head_silu(act):
            for h in range(2):
                act.wait_ge(conv_steps, 2 * KW)
                act.activation(vT[:, h, :], conv[:, h, :], ACT.Silu).then_inc(silu_done, 1)

        def head_u(act, at, j):
            k = at[("ut", j)]
            act.wait_ge(a_full, k + 1)
            act.activation(u_tok[:, 2 * j:2 * j + 2, :].rearrange("p t i -> p (t i)"), P[k % 2][:, :],
                           ACT.Copy).then_inc(a_free, 1)

        def head_conv(dve, at, k):
            if k == 0:
                dve.wait_ge(a_free, at[("val", 1)] + 1)
                dve.wait_ge(pad_zeros, 1)
            for h in range(2):
                if made(conv_steps) > 1:
                    dve.wait_ge(conv_steps, made(conv_steps) - 1)
                if k == 0:
                    ins = dve.tensor_scalar(conv[:, h, :], v_pad[:, h, 0:T], cw_sb[:, h, 0:1],
                                            cb_sb[:, h:h + 1], ALU.mult, ALU.add)
                else:
                    ins = dve.scalar_tensor_tensor(
                        out=conv[:, h, :], in0=v_pad[:, h, k:k + T], scalar=cw_sb[:, h, k:k + 1],
                        in1=conv[:, h, :], op0=ALU.mult, op1=ALU.add)
                ins.then_inc(conv_steps, one(conv_steps))

        def head_dt_start(dve, at):
            dve.wait_ge(a_free, at[("dt",)] + 1)
            dve.tensor_scalar(exp_dt, exp_dt, EXP_CAP, None, ALU.min).then_inc(dt_steps, one(dt_steps))
            dve.wait_ge(dt_steps, made(dt_steps))
            dve.tensor_scalar(log_p, exp_dt, -1.0 / LOG_TERMS * (-1) ** LOG_TERMS, None,
                                          ALU.mult).then_inc(dt_steps, one(dt_steps))

        def head_log(dve, k):
            dve.wait_ge(dt_steps, made(dt_steps))
            dve.scalar_tensor_tensor(
                out=log_p, in0=log_p, scalar=(1.0 if k % 2 else -1.0) / k, in1=exp_dt,
                op0=ALU.add, op1=ALU.mult).then_inc(dt_steps, one(dt_steps))

        def head_dt_parts(dve):
            dve.wait_ge(dt_steps, made(dt_steps))
            dve.tensor_scalar(exp_dt, log_p, DT_MIN, DT_MAX, ALU.max, ALU.min).then_inc(dt_steps, one(dt_steps))
            split(dve, dt_steps, dt_parts[:, :], exp_dt, rest)
            assert made(dt_steps) == DT_STEPS

        def head_c_parts(dve, at):
            dve.wait_ge(a_free, at[("kd",)] + 1)
            dve.scalar_tensor_tensor(out=log_p, in0=sig_k, scalar=K_MAX, in1=exp_dt,
                                     op0=ALU.mult, op1=ALU.mult).then_inc(dt_steps, one(dt_steps))
            dve.wait_ge(dt_steps, made(dt_steps))
            dve.tensor_scalar(log_p, log_p, 1.0, None, ALU.add).then_inc(dt_steps, one(dt_steps))
            split(dve, dt_steps, c_parts[:, :], log_p, rest)
            assert made(dt_steps) == C_STEPS

        CONSTS = [(onehot_sb, onehot), (tiled_sb, tiled_eye), (causal_sb, causal),
                  (chunk_sb, chunk_on), (own_sb, own_head), (gw_sb, gwT), (bv_sb, bv)]

        a_in = prodf[:, 0:G]
        heads_f = raw_sb[:, 0, 0:2, :].rearrange("p a t -> p (a t)")
        dt_rows_f = raw_sb[:, 0, 2, 0:G // 2 * 128]
        rn_pick_f = raw_sb[:, 1, 0:2].rearrange("p a t -> p (a t)")
        n_in = 16 * (len(CONSTS) + 11)
        first = {key: i for i, key in enumerate(HEAD)}
        with nc.Block() as block:
            @block.sync
            def _(sp):
                sp.dma_start(x_next, xT[:, 0:T]).then_inc(next_loaded, 16)
                sp.dma_start(win_sb[:, :], WinT).then_inc(next_loaded, 16)
                sp.dma_start(dtb_sb[:, :], dtb).then_inc(next_loaded, 16)
                sp.dma_start(cw_sb[:, :, :], cw).then_inc(next_loaded, 16)
                sp.dma_start(cb_sb[:, :], cb).then_inc(next_loaded, 16)
                sp.dma_start(eye_sb[:, :], eye).then_inc(next_loaded, 16)
                for dst, src in CONSTS:
                    sp.dma_start(dst[:, :], src).then_inc(consts_in, 16)
                sp.dma_start(wout_sb[:, :, :], WoutT).then_inc(consts_in, 16)
                sp.dma_start(skip_sb[:, :], skip.partition_broadcast(128)).then_inc(consts_in, 16)
                for j, w in enumerate((Wq, Wk, Wv)):
                    sp.dma_start(wqkv_sb[:, j, :], w).then_inc(consts_in, 16)
                sp.dma_start(bqk_sb[:, 0:1], bq).then_inc(consts_in, 16)
                sp.dma_start(bqk_sb[:, 1:2], bk).then_inc(consts_in, 16)
                sp.dma_start(a_in, A_log).then_inc(consts_in, 16)
                sp.dma_start(heads_f, heads).then_inc(consts_in, 16)
                sp.dma_start(dt_rows_f, dt_rows).then_inc(consts_in, 16)
                sp.dma_start(rn_pick_f, rn_pick).then_inc(consts_in, 16)

            @block.gpsimd
            def _(pool):
                pool.memset(v_pad[:, :, 0:3], 0.0).then_inc(pad_zeros, 1)
                pool.memset(ones_sb[:, :], 1.0).then_inc(prep_pool, 1)

            @block.tensor
            def _(pe):
                for i in range(4):
                    head_product(pe, first, i, loads=6)
                for j in range(2):
                    head_transposes(pe, first, j)

            @block.vector
            def _(dve):
                for k in range(KW):
                    head_conv(dve, first, k)
                head_dt_start(dve, first)
                for k in range(LOG_TERMS - 1, 0, -1):
                    head_log(dve, k)
                head_dt_parts(dve)
                head_c_parts(dve, first)
                dve.memset(eps_sb[:, :], EPS_LN).then_inc(prep_dve, 1)
                dve.wait_ge(consts_in, n_in)
                dve.tensor_copy(heads_sb[:, :], heads_f).then_inc(prep_dve, 1)
                dve.tensor_copy(dt_rows_sb[:, :], dt_rows_f).then_inc(prep_dve, 1)
                dve.tensor_copy(rn_pick_sb[:, :], rn_pick_f).then_inc(prep_dve, 1)
                dve.wait_ge(prep_act, 1)
                dve.tensor_scalar(neg_a[:, :], neg_a[:, :], -1.0, None, ALU.mult).then_inc(prep_dve, 1)

            @block.scalar
            def _(act):
                for i in range(4):
                    head_drain(act, first, i)
                head_silu(act)
                for j in range(2):
                    head_u(act, first, j)
                act.wait_ge(consts_in, n_in)
                act.activation(neg_a[:, :], a_in, ACT.Exp).then_inc(prep_act, 1)

        nc.all_engine_barrier(sems_to_clear=range(signals[0].num, signals[-1].num + 1))
        counts.value.clear()

        with nc.Fori(0, B) as b:
            with nc.Block() as block:
                @block.sync
                def _(sp):
                    sp.dma_start(x_in[:, :], xT[:, bass.ds(b * T, T)]).then_inc(x_loaded, 16)
                    sp.dma_start(
                        xres[:, :, :], x[bass.ds(b * T, T), :].rearrange("(t p) d -> p t d", p=128)).then_inc(x_loaded, 16)
                    sp.dma_start(ctx_sb[:, :], ctxT[:, bass.ds(b * S, S)]).then_inc(ctx_in, 16)
                    for g in range(G):
                        if g >= 2:
                            sp.wait_ge(a_full, a_at[("bc", g - 2, 3)] + 1)
                        sp.dma_start(
                            wbc_sb[:, g % 2].rearrange("p c k m -> p (c k m)"),
                            Wbc[g * 128:(g + 1) * 128, :]).then_inc(wbc_loaded[g % 2], 16)
                    sp.wait_ge(y_done, NC)
                    sp.dma_start(x_next, xT[:, bass.ds((b + 1) * T, T)]).then_inc(next_loaded, 16)
                    sp.wait_ge(ctx_in, 16)

                @block.tensor
                def _(pe):
                    def ring_a(key, weights, moving):
                        k = a_at[key]
                        if k >= 2:
                            pe.wait_ge(a_free, k - 1)
                        pe.matmul(P[k % 2][:, :], weights, moving, start=True, stop=True).then_inc(a_full, 1)

                    def ring_v(key, weights, moving):
                        k = v_at[key]
                        if k >= 2:
                            pe.wait_ge(v_free, k - 1)
                        pe.matmul(P[2 + k % 2][:, :], weights, moving, start=True,
                                  stop=True).then_inc(v_full, 1)

                    for g in range(UG):
                        ring_a(("dtb", g), heads_sb[:, g * 128:g * 128 + 128], dt_parts[:, :])
                        ring_v(("c", g), heads_sb[:, g * 128:g * 128 + 128], c_parts[:, :])

                    def bc(g, c):
                        o = a_bank(("bc", g, c))
                        if c == 0:
                            pe.wait_ge(wbc_loaded[g % 2], 16 * (g // 2 + 1))
                        pe.wait_ge(a_free, a_at[("bc", g, c)] - 1)
                        pe.matmul(o[:, :], wbc_sb[:, g % 2, c, 0, :], vT[:, 0, :], start=True, stop=False)
                        pe.matmul(o[:, :], wbc_sb[:, g % 2, c, 1, :], vT[:, 1, :], start=False,
                                  stop=True).then_inc(a_full, 1)

                    def norm_sum(u, n):
                        s, c = divmod(n, 4)
                        off = 124 - (c * 8 + s % 2 * HG)
                        pe.wait_ge(sq_done, 4 * UG * u + n + 1)
                        if u and n == 0:
                            pe.wait_ge(dx_done, 2 * HG * UG * u)
                        pe.matmul(P[4 + n // 8][:, :], onehot_sb[:, off:off + 128], sq[:, n % 2, :],
                                  start=(n % 8 == 0), stop=(n % 8 == 7)).then_inc(norm_acc, 1)

                    def u_blocks(u):
                        for c in range(CT):
                            k = a_at[("ub", u, c)]
                            pe.wait_ge(a_free, k - 1)
                            pe.matmul(P[k % 2][:, :].rearrange("p (t m) -> p t m", t=TT),
                                      tiled_sb[32 * c:32 * c + 32, :],
                                      u_tok[32 * c:32 * c + 32, :, u * 128:u * 128 + 128],
                                      start=True, stop=True).then_inc(a_full, 1)

                    def rn_cast(g):
                        pe.wait_ge(rn_steps, RN_STEPS * (g // 2 + 1))
                        for c in (BX, CZ, CX, BZ):
                            pick = (g % 2 * 4 + c) * 128
                            ring_v(("rn", g, c), rn_pick_sb[:, pick:pick + 128],
                                   rn_parts[:, g // 2 % 2, :])

                    def dt_rows_of(p):
                        ring_v(("dtn", p), dt_rows_sb[:, p * 128:p * 128 + 128], dt_parts[:, :])

                    def kt(g):
                        pe.wait_ge(main_steps, MAIN_STEPS * (g + 1))
                        for j in range(2):
                            o = a_bank(("kt", g, j))
                            pe.wait_ge(a_free, a_at[("kt", g, j)] - 1)
                            for t in range(TT):
                                last = pe.transpose(
                                    o[:, t * 128:t * 128 + 128],
                                    NT[:, 2 + j, g * T + t * 128:g * T + t * 128 + 128], eye_sb[:, :])
                            last.then_inc(a_full, 1)

                    def attend(g):
                        o = v_bank(("g", g))
                        pe.wait_ge(v_free, v_at[("g", g)] - 1)
                        for ch in range(NC):
                            s = slice(g * T + ch * L, g * T + ch * L + L)
                            for j in range(2):
                                for h in range(HG):
                                    r = slice(32 * h, 32 * h + 32)
                                    last = pe.matmul(o[r, ch * L:ch * L + L], NT[r, 2 + j, s], NT[r, j, s],
                                                     start=(j == 0), stop=(j == 1))
                        last.then_inc(v_full, 1)

                    def chunk_inputs(g):
                        pe.wait_ge(a_free, a_at[("kt", g, 1)] + 1)
                        pe.wait_ge(um_done, g + 1)
                        if g % UG == 0:
                            pe.wait_ge(norm_root, 2 * (g // UG + 1))
                        else:
                            pe.wait_ge(dx_done, 2 * HG * g)
                        for j in range(2):
                            for t in range(TT):
                                last = pe.matmul(P[4 + j][:, t * 128:t * 128 + 128],
                                                 kT(g // UG)[:, g % 2, j, t, :],
                                                 um(g)[:, t, :, :].rearrange("p c m -> p (c m)"),
                                                 start=True, stop=True)
                            last.then_inc(dx_psum, 1)

                    def outputs(u, ch):
                        t, c = divmod(ch, CT)
                        o = P[6 + t // 2]
                        if ch == 0:
                            pe.wait_ge(v_free, v_at[("g", u * UG + UG - 1)] + 1)
                        elif u == 0:
                            pe.wait_ge(xbd_done, HG * ch)
                        else:
                            pe.wait_ge(xbd_last, ch)
                        for m in range(UG):
                            g = u * UG + m
                            col = (t % 2) * DI + g * 32
                            oo = o[32 * c:32 * c + 32, col:col + 32]
                            s = slice(g * T + ch * L, g * T + ch * L + L)
                            last = pe.matmul(oo, gm[:, s], u_bd(u)[:, c, t, m * 32:m * 32 + 32],
                                             start=True, stop=(ch == 0))
                            if ch:
                                for j in range(2):
                                    last = pe.matmul(
                                        oo, NT[:, j, s],
                                        x_bd(u)[:, ch % 2, (j * UG + m) * 32:(j * UG + m) * 32 + 32],
                                        start=False, stop=(j == 1))
                        last.then_inc(y_done, 1)

                    def gate(j):
                        k = a_at[("gate", j)]
                        pe.wait_ge(x_loaded, 32)
                        pe.wait_ge(a_free, k - 1)
                        for t in (2 * j, 2 * j + 1):
                            last = pe.matmul(P[k % 2][:, (t % 2) * DI:(t % 2 + 1) * DI],
                                             x_in[:, t * 128:t * 128 + 128], win_sb[:, 0:DI],
                                             start=True, stop=True)
                        last.then_inc(a_full, 1)

                    for u in range(U):
                        for n in range(4 * UG):
                            if u == 0:
                                bc(n // 4, n % 4)
                            elif n < 4 * (UG - 1):
                                bc(UG + 1 + n // 4, n % 4)
                            if n >= 1:
                                norm_sum(u, n - 1)
                            if u:
                                outputs(u - 1, n)
                            if n == 9:
                                dt_rows_of(2 * u)
                            if u and n == 12:
                                rn_cast(UG)
                        if u == 0:
                            rn_cast(0)
                        norm_sum(u, 4 * UG - 1)
                        u_blocks(u)
                        for s in range(UG):
                            g = u * UG + s
                            kt(g)
                            if s == 1:
                                chunk_inputs(g)
                                if u == 0:
                                    bc(UG, 2)
                            if s + 1 < UG:
                                rn_cast(g + 1)
                            if s != 1:
                                chunk_inputs(g)
                            if s == 2 and u == 0:
                                bc(UG, 3)
                            for k in AHEAD[s] if u == 0 else ():
                                ring_a(("dtb", k), heads_sb[:, k * 128:k * 128 + 128], dt_parts[:, :])
                                ring_a(("c", k), heads_sb[:, k * 128:k * 128 + 128], c_parts[:, :])
                            attend(g)
                            if s == 0:
                                dt_rows_of(2 * u + 1)
                                if u == 0:
                                    bc(UG, 0)
                                    bc(UG, 1)
                                else:
                                    gate(0)
                                    gate(1)
                                    head_product(pe, a_at, 0)
                                    head_product(pe, a_at, 1)

                    def keys():
                        pe.wait_ge(dx_done, 2 * HG * G)
                        pe.wait_ge(ctx_in, 16)
                        pe.matmul(P[4][:, 0:S], wqkv_sb[:, 1, :], ctx_sb[:, :], start=True,
                                  stop=True).then_inc(qkv_full, 1)

                    def values():
                        for j in range(2):
                            pe.matmul(P[5][0:SH, j * 128:j * 128 + 128], ctx_sb[:, j * SH:(j + 1) * SH],
                                      wqkv_sb[:, 2, :], start=True, stop=False)
                            last = pe.matmul(P[5][0:SH, j * 128:j * 128 + 128], ones_sb[0:1, 0:SH],
                                             bv_sb[0:1, :], start=False, stop=True)
                        last.then_inc(qkv_full, 1)

                    def turn(j):
                        pe.wait_ge(yf_steps, 2 * (j + 1))
                        pe.wait_ge(qkv_done, j + 1)
                        for k in range(2):
                            for t in range(2):
                                last = pe.transpose(P[4 + j][:, k * 256 + t * 128:k * 256 + t * 128 + 128],
                                                    yf[:, 2 * j + t, k * 128:k * 128 + 128], eye_sb[:, :])
                        last.then_inc(yft_full, 1)

                    def mix(j):
                        pe.wait_ge(yft_done, j + 1)
                        pe.wait_ge(v_free, len(dve_ring))
                        for t in range(2):
                            for k in range(2):
                                last = pe.matmul(P[2 + j][:, t * 128:t * 128 + 128],
                                                 yfT[:, j, k, t * 128:t * 128 + 128],
                                                 wout_sb[:, k, :], start=(k == 0), stop=(k == 1))
                        last.then_inc(mix_full, 1)

                    outputs(U - 1, 0)
                    outputs(U - 1, 1)
                    outputs(U - 1, 2)
                    head_product(pe, a_at, 2)
                    outputs(U - 1, 3)
                    head_product(pe, a_at, 3)
                    outputs(U - 1, 4)
                    outputs(U - 1, 5)
                    outputs(U - 1, 6)
                    keys()
                    outputs(U - 1, 7)
                    values()
                    for ch in range(8, 12):
                        outputs(U - 1, ch)
                    turn(0)
                    outputs(U - 1, 12)
                    head_transposes(pe, a_at, 0)
                    outputs(U - 1, 13)
                    mix(0)
                    outputs(U - 1, 14)
                    head_transposes(pe, a_at, 1)
                    outputs(U - 1, 15)
                    turn(1)
                    mix(1)
                    pe.wait_ge(a_free, len(act_ring))

                @block.scalar
                def _(act):
                    def drain(key, o, i, func, **kw):
                        act.wait_ge(a_full, a_at[key] + 1)
                        act.activation(o, i, func, **kw).then_inc(a_free, 1)

                    def drain_dt(g):
                        act.wait_ge(a_full, a_at[("dtb", g)] + 1)
                        act.activation(coef[:, 0, grp(g)], a_bank(("dtb", g))[:, :], ACT.Copy,
                                       scale=neg_a[:, g:g + 1]).then_inc(na_done, 1)
                        act.activation(dt_rep[:, grp(g)], a_bank(("dtb", g))[:, :],
                                       ACT.Copy).then_inc(a_free, 1)

                    for g in range(UG):
                        drain_dt(g)

                    def squares(g, c, source):
                        n = 4 * g + c
                        if n >= 2:
                            act.wait_ge(norm_acc, n - 1)
                        act.activation(sq[:, n % 2, :], source, ACT.Square).then_inc(sq_done, 1)

                    def drain_bc(g, c):
                        act.wait_ge(a_full, a_at[("bc", g, c)] + 1)
                        if g == UG:
                            act.wait_ge(main_steps, MAIN_STEPS)
                        if g < UG:
                            squares(g, c, a_bank(("bc", g, c))[:, :])
                        act.activation(raw(g)[:, c, :], a_bank(("bc", g, c))[:, :],
                                       ACT.Copy).then_inc(a_free, 1)

                    def drain_gate(j):
                        act.wait_ge(a_full, a_at[("gate", j)] + 1)
                        act.wait_ge(main_steps, MAIN_STEPS * (UG + 1))
                        act.activation(sg[:, 2 * j:2 * j + 2, :].rearrange("p t i -> p (t i)"),
                                       a_bank(("gate", j))[:, :], ACT.Silu).then_inc(a_free, 1)

                    def drain_dx(g):
                        for j in range(2):
                            act.wait_ge(dx_psum, 2 * g + j + 1)
                            if g == UG:
                                act.wait_ge(state_steps, STATE_STEPS * (NC - 1))
                            for h in range(HG):
                                r = slice(32 * h, 32 * h + 32)
                                act.activation(
                                    dX[r, :, j, g % UG, :],
                                    P[4 + j][r, :].rearrange("p (n h d) -> p n h d", h=HG, d=DH)[:, :, h, :],
                                    ACT.Copy).then_inc(dx_done, 1)

                    def spread(ch):
                        act.wait_ge(state_steps, STATE_STEPS * ch)
                        if ch >= 2:
                            act.wait_ge(y_done, ch - 1)
                        for h in range(HG):
                            act.activation(
                                x_bd(0)[:, ch % 2].rearrange("p (m h d) -> p m h d", h=HG, d=DH)[:, :, h, :],
                                X(0)[:, ch % 2].rearrange("p j (g d) -> p (j g) d", d=DH),
                                ACT.Copy, scale=own_sb[:, h:h + 1]).then_inc(xbd_done, 1)

                    def inverses(first, end):
                        for g in range(first, end):
                            act.wait_ge(sums_done, g + 1)
                            act.activation(winv[:, grp(g)], winv[:, grp(g)], ACT.Exp,
                                           scale=-1.0).then_inc(inv_done, 1)

                    def own_blocks(u):
                        for c in range(CT):
                            act.wait_ge(a_full, a_at[("ub", u, c)] + 1)
                            for h in range(HG):
                                act.activation(
                                    u_bd(u)[:, c].rearrange("p t (m h d) -> p (t m) h d", h=HG, d=DH)[:, :, h, :],
                                    a_bank(("ub", u, c))[:, :].rearrange(
                                        "p (m h d) -> p m h d", h=HG, d=DH)[:, :, h, :],
                                    ACT.Copy, scale=own_sb[:, h:h + 1]).then_inc(a_free if h == HG - 1 else ub_part, 1)

                    def norm_roots(p):
                        act.wait_ge(norm_acc, 8 * (p + 1))
                        if p:
                            act.wait_ge(rn_steps, RN_STEPS * p)
                        act.activation(rn[:, :], P[4 + p % 2][:, :], ACT.Sqrt).then_inc(norm_root, 1)

                    def logs(u):
                        for g in range(u * UG, (u + 1) * UG):
                            act.wait_ge(w_steps, 2 * (g + 1))
                            act.activation(winv[:, grp(g)], winv[:, grp(g)], ACT.Ln).then_inc(lnw_done, 1)

                    for u in range(U):
                        if u:
                            act.wait_ge(main_steps, MAIN_STEPS * UG)
                            act.wait_ge(dx_psum, 2 * UG)
                        for n in range(4 * UG):
                            if u == 0:
                                drain_bc(n // 4, n % 4)
                            else:
                                if n < 4 * (UG - 1):
                                    drain_bc(UG + 1 + n // 4, n % 4)
                                act.wait_ge(a_free, a_at[("bc", UG + n // 4, n % 4)] + 1)
                                squares(UG + n // 4, n % 4, raw(UG + n // 4)[:, n % 4, :])
                            if u == 0 and n == 3:
                                logs(u)
                            if n == 8:
                                norm_roots(2 * u)
                            if n in (10, 12):
                                inverses(u * UG + n - 10, u * UG + n - 8)
                            if u and n + 1 < NC:
                                spread(n + 1)
                        norm_roots(2 * u + 1)
                        act.wait_ge(rec_steps, REC_STEPS * (u + 1))
                        own_blocks(u)
                        for g in range(u * UG, (u + 1) * UG):
                            if g % UG >= 2:
                                act.wait_ge(dx_psum, 2 * (g - 1))
                            for j in range(2):
                                drain(("kt", g, j), kT(u)[:, g % 2, j].rearrange("p t k -> p (t k)"),
                                      a_bank(("kt", g, j))[:, :], ACT.Copy)
                            drain_dx(g)
                            if g in (1, 2):
                                drain_bc(UG, g + 1)
                            for k in AHEAD[g] if u == 0 else ():
                                drain_dt(k)
                                drain(("c", k), coef[:, 1, grp(k)], a_bank(("c", k))[:, :], ACT.Copy)
                            if g == UG - 1:
                                logs(1)
                            if g == 0:
                                drain_bc(UG, 0)
                                drain_bc(UG, 1)
                            elif g == UG:
                                drain_gate(0)
                                drain_gate(1)
                                head_drain(act, a_at, 0)
                                head_drain(act, a_at, 1)
                    for i in range(2, 4):
                        head_drain(act, a_at, i)
                    act.wait_ge(qkv_full, 1)
                    act.activation(kcT, P[4][:, 0:S], ACT.Identity, bias=bqk_sb[:, 1:2]).then_inc(qkv_done, 1)
                    act.wait_ge(qkv_full, 2)
                    act.activation(v_sb[0:SH].rearrange("p j d -> p (j d)"), P[5][0:SH, 0:256],
                                   ACT.Copy).then_inc(qkv_done, 1)
                    head_silu(act)
                    act.wait_ge(su_done, 1)

                    def drain_turned(j):
                        act.wait_ge(yft_full, j + 1)
                        act.activation(yfT[:, j].rearrange("p k t -> p (k t)"), P[4 + j][:, :],
                                       ACT.Copy).then_inc(yft_done, 1)

                    drain_turned(0)
                    for j in range(2):
                        head_u(act, a_at, j)
                    drain_turned(1)
                    act.wait_ge(ln_steps, 10)
                    act.activation(rstd[:, :], mv[:, :, 1], ACT.Sqrt, bias=eps_sb[:, :]).then_inc(ln_root, 1)

                @block.gpsimd
                def _(pool):
                    pool.memset(NT[:, ZZ, 0:UT:L], 1.0).then_inc(pads, 1)
                    pool.memset(NT[:, ZZ, UT::L], 1.0).then_inc(pads, 1)

                    def find_w(g):
                        pool.wait_ge(a_free, a_at[("dtb", g)] + 1)
                        pool.wait_ge(na_done, g + 1)
                        pool.tensor_tensor(winv[:, grp(g)], dt_rep[:, grp(g)], coef[:, 0, grp(g)],
                                           ALU.mult).then_inc(w_steps, 1)
                        if g < UG:
                            pool.wait_ge(v_free, v_at[("c", g)] + 1)
                        else:
                            pool.wait_ge(a_free, a_at[("c", g)] + 1)
                        pool.wait_ge(w_steps, 2 * g + 1)
                        pool.tensor_tensor(winv[:, grp(g)], coef[:, 1, grp(g)], winv[:, grp(g)],
                                           ALU.subtract).then_inc(w_steps, 1)

                    def prepare(g):
                        r = raw(g)
                        pool.wait_ge(v_free, v_at[("rn", g, BX)] + 1)
                        if g >= 2:
                            pool.wait_ge(main_steps, MAIN_STEPS * (g - 1))
                        pool.tensor_tensor(minus_dt_a_g(g), coef[:, 0, grp(g)], r[:, BX, :],
                                           ALU.mult).then_inc(pool_main, 1)
                        for c in (CZ, CX):
                            pool.wait_ge(v_free, v_at[("rn", g, c)] + 1)
                            pool.tensor_tensor(r[:, c, :], r[:, c, :], winv[:, grp(g)],
                                               ALU.mult).then_inc(pool_main, 1)
                        pool.wait_ge(pool_main, 3 * g + 2)
                        pool.tensor_tensor(
                            um(g), u_tok[:, :, g * 32:g * 32 + 32].unsqueeze(2)
                            .to_broadcast([128, TT, CT, 32]),
                            own_sb[:, 0:HG].unsqueeze(1).unsqueeze(3).to_broadcast([128, TT, CT, 32]),
                            ALU.mult).then_inc(um_done, 1)

                    def transitions(u):
                        pool.wait_ge(rec_steps, REC_STEPS * (u + 1))
                        for g in range(u * UG, (u + 1) * UG):
                            pool.wait_ge(inv_done, g + 1)
                            pool.tensor_tensor(
                                phi[:, :, g * NC:(g + 1) * NC], NT[:, :, g * T + L - 1:(g + 1) * T:L],
                                winv[:, g * T + L - 1:(g + 1) * T:L].unsqueeze(1)
                                .to_broadcast([128, 4, NC]), ALU.mult).then_inc(phi_done, 1)

                    def states(u):
                        pool.wait_ge(dx_done, 2 * HG * UG * (u + 1))
                        phv = phi[:, :, u * UG * NC:(u + 1) * UG * NC].rearrange(
                            "p (a j) (g c) -> p a j g c", a=2, g=UG)
                        for ch in range(NC - 1):
                            if ch == 0:
                                pool.wait_ge(main_steps, MAIN_STEPS * UG * (u + 1))
                                if u == 0:
                                    pool.wait_ge(v_free, v_at[("g", 1)] + 1)
                                pool.tensor_copy(
                                    st(u)[:, 0], dX[:, 0].rearrange("p j g d -> p j (g d)")).then_inc(
                                        state_steps, one(state_steps))
                            else:
                                pool.wait_ge(state_steps, made(state_steps))
                                pool.tensor_tensor(
                                    st(u)[:, 0], X(u)[:, ch % 2], dX[:, ch].rearrange("p j g d -> p j (g d)"),
                                    ALU.add).then_inc(state_steps, one(state_steps))
                            pool.wait_ge(state_steps, made(state_steps))
                            pool.tensor_tensor(
                                st(u)[:, 1:3].rearrange("p j a (g d) -> p a j g d", g=UG),
                                phv[:, :, :, :, ch].unsqueeze(4).to_broadcast([128, 2, 2, UG, DH]),
                                st(u)[:, 0].rearrange("p j (g d) -> p j g d", g=UG).unsqueeze(1)
                                .to_broadcast([128, 2, 2, UG, DH]), ALU.mult).then_inc(
                                    state_steps, one(state_steps))
                            pool.wait_ge(state_steps, made(state_steps))
                            if ch >= 2 and u == 0:
                                pool.wait_ge(xbd_done, HG * (ch - 1))
                            elif ch >= 2:
                                pool.wait_ge(xbd_last, ch - 1)
                            pool.tensor_tensor(X(u)[:, (ch + 1) % 2], st(u)[:, 1], st(u)[:, 2],
                                               ALU.add).then_inc(state_steps, one(state_steps))
                            if u == 0 and ch == NC - 2:
                                transitions(1)
                                prepare(UG)

                    for g in range(UG):
                        find_w(g)
                    for u in range(U):
                        if u == 0:
                            transitions(0)
                        for g in range(u * UG, (u + 1) * UG):
                            if g != UG:
                                prepare(g)
                            if g == UG + 1:
                                pool.wait_ge(dx_psum, 2 * UG)
                                pool.wait_ge(main_steps, MAIN_STEPS * UG + 1)
                                pool.memset(v_pad[:, :, 0:3], 0.0).then_inc(pad_zeros, 1)
                            if u + 1 < U and g % UG:
                                find_w(g - 1 + UG)
                        if u + 1 < U:
                            find_w((u + 2) * UG - 1)
                        states(u)

                @block.vector
                def _(dve):
                    def drain_c(g):
                        dve.wait_ge(v_full, v_at[("c", g)] + 1)
                        dve.tensor_copy(coef[:, 1, grp(g)], v_bank(("c", g))[:, :]).then_inc(v_free, one(v_free))

                    for g in range(UG):
                        drain_c(g)

                    def products(u):
                        lo, hi, M = u * UT, (u + 1) * UT, UG * NC
                        if u == 0:
                            dve.wait_ge(a_free, a_at[("dtb", UG - 1)] + 1)
                            dve.wait_ge(na_done, UG)
                            dve.wait_ge(v_free, made(v_free))
                            dve.wait_ge(pads, 2)
                        else:
                            dve.wait_ge(a_free, a_at[("c", G - 1)] + 1)
                            dve.wait_ge(na_done, G)
                            dve.wait_ge(main_steps, made(main_steps))
                        dve.tensor_copy(NT[:, ZS, lo:hi:L], coef[:, 0, lo:hi:L]).then_inc(rec_steps, one(rec_steps))
                        dve.tensor_copy(NT[:, SZ, lo:hi:L], dt_rep[:, lo:hi:L]).then_inc(rec_steps, one(rec_steps))
                        dve.tensor_copy(NT[:, SS, lo:hi:L], coef[:, 1, lo:hi:L]).then_inc(rec_steps, one(rec_steps))
                        for t in range(1, L):
                            dve.wait_ge(rec_steps, made(rec_steps) - (1 if t > 1 else 0))
                            dve.tensor_tensor(
                                step_b[:, t % 2], NT[:, 0:2, lo + t - 1:hi:L],
                                dt_rep[:, lo + t:hi:L].unsqueeze(1).to_broadcast([128, 2, M]),
                                ALU.mult).then_inc(rec_steps, one(rec_steps))
                            dve.wait_ge(rec_steps, made(rec_steps) - 1)
                            dve.tensor_tensor(
                                step_a,
                                NT[:, 2:4, lo + t - 1:hi:L].unsqueeze(1).to_broadcast([128, 2, 2, M]),
                                coef[:, :, lo + t:hi:L].unsqueeze(2).to_broadcast([128, 2, 2, M]),
                                ALU.mult).then_inc(rec_steps, one(rec_steps))
                            dve.wait_ge(rec_steps, made(rec_steps))
                            dve.tensor_tensor(NT[:, 0:2, lo + t:hi:L], NT[:, 0:2, lo + t - 1:hi:L],
                                              step_a[:, 0], ALU.add).then_inc(rec_steps, one(rec_steps))
                            dve.tensor_tensor(NT[:, 2:4, lo + t:hi:L], step_b[:, t % 2], step_a[:, 1],
                                              ALU.add).then_inc(rec_steps, one(rec_steps))
                            if u and t == MASK_AT:
                                mask(UG - 1)
                            if t == RN_AT[u]:
                                inverse_norms(2 * u)
                            if t in SCAN_AT:
                                g = u * UG + SCAN_AT.index(t)
                                dve.wait_ge(lnw_done, g + 1)
                                dve.tensor_tensor_scan(winv[:, grp(g)], chunk_sb[:, :], winv[:, grp(g)],
                                                       0.0, ALU.mult, ALU.add).then_inc(sums_done, 1)
                        assert made(rec_steps) == REC_STEPS * (u + 1)

                    def inverse_norms(p):
                        dve.wait_ge(norm_root, p + 1)
                        dve.tensor_scalar(rn[:, :], rn[:, :], EPS_NORM, None, ALU.add).then_inc(rn_steps, one(rn_steps))
                        dve.wait_ge(rn_steps, made(rn_steps))
                        dve.reciprocal(rn[:, :], rn[:, :]).then_inc(rn_steps, one(rn_steps))
                        dve.wait_ge(rn_steps, made(rn_steps))
                        dve.wait_ge(v_full, v_at[("dtn", p)] + 1)
                        dve.scalar_tensor_tensor(
                            out=rn[:, :], in0=v_bank(("dtn", p))[:, :], scalar=own_sb[:, HG:HG + 1],
                            in1=rn[:, :], op0=ALU.add, op1=ALU.mult).then_inc(v_free, one(v_free))
                        dve.wait_ge(v_free, made(v_free))
                        split(dve, rn_steps, rn_parts[:, p % 2, :], rn[:, :], rn[:, :])
                        assert made(rn_steps) == RN_STEPS * (p + 1)

                    def normalise(g):
                        for c in (BX, CZ, CX, BZ):
                            dve.wait_ge(a_free, a_at[("bc", g, c)] + 1)
                            dve.wait_ge(v_full, v_at[("rn", g, c)] + 1)
                            dve.tensor_tensor(raw(g)[:, c, :], raw(g)[:, c, :],
                                              v_bank(("rn", g, c))[:, :], ALU.mult).then_inc(v_free, one(v_free))

                    def plane(p, g):
                        return NT[:, p, grp(g)]

                    def before(a):
                        return a.rearrange("p (c t) -> p c t", t=L)[:, :, 0:L - 1]

                    def after(a):
                        return a.rearrange("p (c t) -> p c t", t=L)[:, :, 1:L]

                    def q_kappa(g):
                        r = raw(g)
                        dve.wait_ge(pool_main, 3 * g + 1)
                        dve.wait_ge(v_free, made(v_free))
                        dve.tensor_tensor(r[:, BZ, :], r[:, BZ, :], minus_dt_a_g(g),
                                                        ALU.subtract).then_inc(main_steps, one(main_steps))
                        dve.tensor_tensor(after(prod[:, 0, 1, :]), before(plane(ZZ, g)),
                                                        after(r[:, BX, :]), ALU.mult).then_inc(main_steps, one(main_steps))
                        if made(main_steps) > 1:
                            dve.wait_ge(main_steps, made(main_steps) - 1)
                        dve.tensor_tensor(after(prod[:, 1, 0, :]), before(plane(ZS, g)),
                                                        after(r[:, BX, :]), ALU.mult).then_inc(main_steps, one(main_steps))
                        if made(main_steps) > 1:
                            dve.wait_ge(main_steps, made(main_steps) - 1)
                        dve.tensor_tensor(after(prod[:, 0, 0, :]), before(plane(SS, g)),
                                                        after(r[:, BZ, :]), ALU.mult).then_inc(main_steps, one(main_steps))
                        if made(main_steps) > 1:
                            dve.wait_ge(main_steps, made(main_steps) - 1)
                        dve.tensor_tensor(after(prod[:, 1, 1, :]), before(plane(SZ, g)),
                                                        after(r[:, BZ, :]), ALU.mult).then_inc(main_steps, one(main_steps))
                        dve.wait_ge(pool_main, 3 * g + 3)
                        dve.wait_ge(phi_done, g + 1)
                        if made(main_steps) > 1:
                            dve.wait_ge(main_steps, made(main_steps) - 1)
                        dve.tensor_tensor(
                            NT[:, 0:2, grp(g)], NT[:, 0:2, grp(g)],
                            r[:, CZ, :].unsqueeze(1).to_broadcast([128, 2, T]), ALU.mult).then_inc(main_steps, one(main_steps))
                        if made(main_steps) > 1:
                            dve.wait_ge(main_steps, made(main_steps) - 1)
                        dve.tensor_tensor(
                            NT[:, 2:4, grp(g)], NT[:, 2:4, grp(g)],
                            r[:, CX, :].unsqueeze(1).to_broadcast([128, 2, T]), ALU.mult).then_inc(main_steps, one(main_steps))
                        dve.wait_ge(main_steps, made(main_steps))
                        dve.tensor_tensor(NT[:, 0:2, grp(g)], NT[:, 0:2, grp(g)],
                                                        NT[:, 2:4, grp(g)], ALU.add).then_inc(main_steps, one(main_steps))
                        dve.wait_ge(main_steps, made(main_steps))
                        kv = NT[:, 2:4, grp(g)].rearrange("p j (c t) -> p j c t", t=L)
                        pv = prod[:, :, :, :].rearrange("p s j (c t) -> p s j c t", t=L)
                        dve.tensor_tensor(kv[:, :, :, 1:L], pv[:, 0, :, :, 1:L],
                                                        pv[:, 1, :, :, 1:L], ALU.subtract).then_inc(main_steps, one(main_steps))
                        dve.tensor_copy(kv[:, :, :, 0],
                                                      r[:, 0:2, :].rearrange("p j (c t) -> p j c t", t=L)[:, :, :, 0]).then_inc(main_steps, one(main_steps))
                        assert made(main_steps) == MAIN_STEPS * (g + 1)

                    def mask(g):
                        dve.wait_ge(v_full, v_at[("g", g)] + 1)
                        dve.tensor_tensor(
                            gm[:, grp(g)].rearrange("p (c t) -> p c t", t=L),
                            v_bank(("g", g))[:, :].rearrange("p (c t) -> p c t", t=L),
                            causal_sb[:, :].unsqueeze(1).to_broadcast([128, NC, L]), ALU.mult).then_inc(v_free, one(v_free))

                    for u in range(U):
                        products(u)
                        dve.wait_ge(rec_steps, made(rec_steps))
                        g0 = u * UG
                        normalise(g0)
                        for s in range(UG):
                            if s or u:
                                dve.wait_ge(main_steps, made(main_steps))
                            q_kappa(g0 + s)
                            if s > 0:
                                mask(g0 + s - 1)
                            if s == 1:
                                inverse_norms(2 * u + 1)
                            if s + 1 < UG:
                                normalise(g0 + s + 1)
                        if u:
                            mask(g0 + UG - 1)

                    dve.wait_ge(main_steps, made(main_steps))
                    dve.tensor_tensor(su, u_tok[:, :, :],
                                      skip_sb[:, :].unsqueeze(1).to_broadcast([128, TT, DI]),
                                      ALU.mult).then_inc(su_done, 1)
                    def gated(j):
                        dve.wait_ge(a_free, a_at[("gate", j)] + 1)
                        dve.wait_ge(y_done, (U - 1) * NC + 8 * (j + 1))
                        dve.tensor_tensor(
                            yf[:, 2 * j:2 * j + 2, :].rearrange("p t i -> p (t i)"), P[6 + j][:, :],
                            su[:, 2 * j:2 * j + 2, :].rearrange("p t i -> p (t i)"),
                            ALU.add).then_inc(yf_steps, one(yf_steps))
                        dve.wait_ge(yf_steps, made(yf_steps))
                        dve.tensor_tensor(yf[:, 2 * j:2 * j + 2, :], yf[:, 2 * j:2 * j + 2, :],
                                          sg[:, 2 * j:2 * j + 2, :], ALU.mult).then_inc(yf_steps, one(yf_steps))

                    def residual(j):
                        dve.wait_ge(mix_full, j + 1)
                        dve.tensor_tensor(
                            xres[:, 2 * j:2 * j + 2, :], xres[:, 2 * j:2 * j + 2, :],
                            P[2 + j][:, 0:2 * D].rearrange("p (t d) -> p t d", t=2),
                            ALU.add).then_inc(ln_steps, one(ln_steps))

                    for ch in range(1, NC):
                        dve.wait_ge(state_steps, STATE_STEPS * (NC - 1 + ch))
                        if ch >= 2:
                            dve.wait_ge(y_done, NC + ch - 1)
                        dve.tensor_tensor(
                            x_bd(1)[:, ch % 2].rearrange("p (m h d) -> p m h d", h=HG, d=DH),
                            X(1)[:, ch % 2].rearrange("p j (g d) -> p (j g) d", d=DH).unsqueeze(2)
                            .to_broadcast([128, 2 * UG, HG, DH]),
                            own_sb[:, 0:HG].unsqueeze(1).unsqueeze(3).to_broadcast([128, 2 * UG, HG, DH]),
                            ALU.mult).then_inc(xbd_last, 1)
                        if 2 <= ch < 2 + KW:
                            head_conv(dve, a_at, ch - 2)
                        if ch == 9:
                            gated(0)
                    residual(0)

                    gated(1)
                    residual(1)
                    layer_norm(dve, ln_steps, ln_root, xres, xres)

            with nc.Block() as block:
                @block.sync
                def _(sp):
                    sp.dma_start(fb_sb, fcol).then_inc(ffn_in, 16)
                    sp.dma_start(fcb_sb[0:E + 1, :], fc2b).then_inc(ffn_in, 16)
                    sp.dma_start(fc2_raw, fc2T).then_inc(ffn_in, 16)
                    sp.dma_start(fc1_sb, fc1T).then_inc(ffn_in, 16)
                    sp.wait_ge(acc_steps, ACC_STEPS)
                    sp.dma_start(
                        out[bass.ds(b * T, T), :].rearrange("(t p) d -> p t d", p=128), acc).then_inc(stored, 16)
                    sp.wait_ge(stored, 16)

                @block.gpsimd
                def _(pool):
                    pool.wait_ge(ffn_in, 64)
                    for e in range(NE):
                        pool.tensor_scalar(fc2_sb[:, e, :], fc2_raw[:, e, :], fb_sb[:, e, 2:3], 1.0,
                                                     ALU.mult, ALU.mult).then_inc(scaled, 1)

                @block.tensor
                def _(pe):
                    for t in range(TT):
                        last = pe.transpose(P[0][:, t * 128:t * 128 + 128], xres[:, t, :], eye_sb[:, :])
                    last.then_inc(x1_full, 1)
                    pe.wait_ge(x1_done, 1)
                    pe.matmul(P[1][:, :], wqkv_sb[:, 0, :], x1T, start=True, stop=True).then_inc(qkv_full, 1)
                    pe.wait_ge(qkv_done, 3)
                    for t in range(TT):
                        last = pe.matmul(P[4 + t // 2][:, (t % 2) * S:(t % 2 + 1) * S],
                                         qT[:, t * 128:t * 128 + 128], kcT, start=True, stop=True)
                        last.then_inc(s_full, 1)
                    for t in range(TT):
                        pe.wait_ge(p_done, t + 1)
                        for j in range(2):
                            last = pe.transpose(
                                P[6 + t // 2][0:SH, (t % 2) * 256 + j * 128:(t % 2) * 256 + j * 128 + 128],
                                probs[:, t, j * SH:(j + 1) * SH], eye_sb[:, :])
                        last.then_inc(pt_full, 1)
                    for t in range(TT):
                        pe.wait_ge(pt_done, t // 2 + 1)
                        for j in range(2):
                            last = pe.matmul(P[0][:, t * 128:t * 128 + 128], pT[0:SH, t, j, :], v_sb[0:SH, j, :],
                                             start=(j == 0), stop=(j == 1))
                    last.then_inc(o_full, 1)
                    pe.wait_ge(x_steps, X_STEPS)
                    for t in range(TT):
                        last = pe.transpose(P[1][:, t * 128:t * 128 + 128], xres[:, t, :], eye_sb[:, :])
                    last.then_inc(x2_full, 1)
                    pe.wait_ge(x2_done, 1)
                    for t in range(TT):
                        last = pe.matmul(P[2][:, t * E:(t + 1) * E], x2T[:, t * 128:t * 128 + 128], gw_sb[:, :],
                                         start=True, stop=True)
                    last.then_inc(lg_full, 1)

                    pe.wait_ge(ffn_in, 64)

                    def up(i):
                        e = ORDER[i]
                        if i >= 2:
                            pe.wait_ge(gelu_done, i - 1)
                        pe.matmul(P[4 + i % 2][:, :], fc1_sb[:, e, 128:256], x2T,
                                             start=True, stop=True).then_inc(hg_full, 1)
                        if i >= 2:
                            pe.wait_ge(glu_done, i - 1)
                        pe.matmul(P[6 + i % 2][:, :], fc1_sb[:, e, 0:128], x2T,
                                             start=True, stop=True).then_inc(hx_full, 1)

                    def down(i):
                        e = ORDER[i]
                        pe.wait_ge(glu_done, i + 1)
                        pe.wait_ge(scaled, e + 1)
                        if e >= E:
                            for t in range(TT):
                                last = pe.matmul(P[3][:, t * 128:t * 128 + 128],
                                                 act_a[:, i % 2, t * 128:t * 128 + 128], fc2_sb[:, e, :],
                                                 start=(e == E and t == 0), stop=False, skip_group_check=True)
                            last.then_inc(base, 1)
                            if e == NE - 1:
                                pe.wait_ge(ct_done, 1)
                                for t in range(TT):
                                    last = pe.matmul(P[3][:, t * 128:t * 128 + 128],
                                                     combT[0:E + 1, t * 128:t * 128 + 128], fcb_sb[0:E + 1, :],
                                                     start=False, stop=(t == TT - 1), skip_group_check=True)
                                last.then_inc(base, 1)
                        else:
                            if e >= 2:
                                pe.wait_ge(acc_steps, 1 + TT * (e - 1))
                            for t in range(TT):
                                last = pe.matmul(P[e % 2][:, t * 128:t * 128 + 128],
                                                 act_a[:, i % 2, t * 128:t * 128 + 128], fc2_sb[:, e, :],
                                                 start=True, stop=True)
                            last.then_inc(e_full, 1)

                    up(0)
                    pe.wait_ge(route, ROUTE_STEPS)
                    for t in range(TT):
                        last = pe.transpose(P[2][0:E + 1, t * 128:t * 128 + 128], comb[:, t, :], eye_sb[:, :])
                    last.then_inc(ct_full, 1)
                    for i in range(NE):
                        if i + 1 < NE:
                            up(i + 1)
                        down(i)

                @block.scalar
                def _(act):
                    act.wait_ge(x1_full, 1)
                    act.activation(x1T, P[0][:, :], ACT.Copy).then_inc(x1_done, 1)
                    act.wait_ge(qkv_full, 3)
                    act.activation(qT, P[1][:, :], ACT.Identity, bias=bqk_sb[:, 0:1]).then_inc(qkv_done, 1)
                    for t in range(TT):
                        act.wait_ge(s_max, t // 2 + 1)
                        act.activation(probs[:, t, :], P[4 + t // 2][:, (t % 2) * S:(t % 2 + 1) * S],
                                                 ACT.Exp, bias=negmax[:, t:t + 1], accum_out=sums[:, t:t + 1]).then_inc(p_done, 1)
                    for j in range(2):
                        act.wait_ge(pt_full, 2 * j + 2)
                        act.activation(
                            pT[0:SH, 2 * j:2 * j + 2].rearrange("p t j q -> p (t j q)"), P[6 + j][0:SH, :],
                            ACT.Copy).then_inc(pt_done, 1)
                    act.wait_ge(x_steps, X_STEPS - 1 - TT)
                    act.activation(rstd[:, :], mv[:, :, 1], ACT.Sqrt, bias=eps_sb[:, :]).then_inc(ln2_root, 1)
                    act.wait_ge(x2_full, 1)
                    act.activation(x2T, P[1][:, :], ACT.Copy).then_inc(x2_done, 1)
                    for t in range(TT):
                        act.wait_ge(route, 2)
                        act.activation(score[:, t, :], P[2][:, t * E:(t + 1) * E], ACT.Exp,
                                                 bias=gmax[:, t:t + 1], accum_out=gsum[:, t:t + 1]).then_inc(lg_exp, 1)
                    for i in range(NE):
                        e = ORDER[i]
                        act.wait_ge(hg_full, i + 1)
                        if i >= 2:
                            act.wait_ge(glu_done, i - 1)
                        act.activation(ga[:, i % 2, :], P[4 + i % 2][:, :], ACT.Gelu,
                                                    bias=fb_sb[:, e, 0:1]).then_inc(gelu_done, 1)
                        if i == 0:
                            act.wait_ge(ct_full, 1)
                            act.activation(combT[0:E + 1, :], P[2][0:E + 1, :], ACT.Copy).then_inc(ct_done, 1)
                    act.wait_ge(acc_steps, ACC_STEPS - 1 - TT)
                    act.activation(rstd[:, :], mv[:, :, 1], ACT.Sqrt, bias=eps_sb[:, :]).then_inc(ln3_root, 1)

                @block.vector
                def _(dve):
                    for j in range(2):
                        dve.wait_ge(s_full, 2 * j + 2)
                        dve.tensor_reduce(
                            out=negmax[:, 2 * j:2 * j + 2],
                            in_=P[4 + j][:, 0:2 * S].rearrange("p (t s) -> p t s", s=S), axis=AX,
                            op=ALU.max, negate=True).then_inc(s_max, 1)
                    dve.wait_ge(p_done, TT)
                    dve.reciprocal(rsum, sums).then_inc(x_steps, one(x_steps))
                    dve.wait_ge(o_full, 1)
                    dve.wait_ge(x_steps, made(x_steps))
                    for t in range(TT):
                        dve.scalar_tensor_tensor(
                            out=xres[:, t, :], in0=P[0][:, t * 128:t * 128 + 128], scalar=rsum[:, t:t + 1],
                            in1=xres[:, t, :], op0=ALU.mult, op1=ALU.add).then_inc(x_steps, one(x_steps))
                    layer_norm(dve, x_steps, ln2_root, xres, xres)
                    assert made(x_steps) == X_STEPS
                    dve.wait_ge(lg_full, 1)
                    lg = P[2][:, 0:TT * E].rearrange("p (t e) -> p t e", t=TT)
                    dve.tensor_reduce(out=gmax, in_=lg, axis=AX, op=ALU.max, negate=True).then_inc(route, one(route))
                    dve.memset(comb[:, :, E:E + 1], 1.0).then_inc(route, one(route))
                    dve.wait_ge(lg_exp, TT)
                    dve.reciprocal(grec, gsum).then_inc(route, one(route))
                    dve.wait_ge(route, made(route))
                    dve.tensor_tensor(score, score, grec.unsqueeze(2).to_broadcast([128, TT, E]),
                                               ALU.mult).then_inc(route, one(route))
                    dve.wait_ge(route, made(route))
                    for t in range(TT):
                        dve.max(top8[:, t, :], score[:, t, :]).then_inc(route, one(route))
                    dve.wait_ge(route, made(route))
                    dve.tensor_reduce(out=topsum, in_=top8[:, :, 0:TOPK], axis=AX, op=ALU.add).then_inc(route, one(route))
                    dve.memset(top8[:, :, TOPK:8], -1.0).then_inc(route, one(route))
                    dve.wait_ge(route, made(route))
                    for t in range(TT):
                        dve.match_replace(left[:, t, :], top8[:, t, :], score[:, t, :], -2.0).then_inc(route, one(route))
                    dve.tensor_scalar(topsum, topsum, EPS_TOP, None, ALU.add).then_inc(route, one(route))
                    dve.wait_ge(route, made(route))
                    dve.reciprocal(topsum, topsum).then_inc(route, one(route))
                    dve.scalar_tensor_tensor(out=comb[:, :, 0:E], in0=left, scalar=0.0, in1=score,
                                                      op0=ALU.is_lt, op1=ALU.mult).then_inc(route, one(route))
                    dve.wait_ge(route, made(route))
                    dve.tensor_tensor(comb[:, :, 0:E], comb[:, :, 0:E],
                                               topsum.unsqueeze(2).to_broadcast([128, TT, E]), ALU.mult).then_inc(route, one(route))
                    assert made(route) == ROUTE_STEPS
                    dve.wait_ge(route, made(route))

                    def glu(i):
                        e = ORDER[i]
                        dve.wait_ge(hx_full, i + 1)
                        dve.wait_ge(gelu_done, i + 1)
                        dve.scalar_tensor_tensor(
                            out=act_a[:, i % 2, :], in0=P[6 + i % 2][:, :], scalar=fb_sb[:, e, 1:2],
                            in1=ga[:, i % 2, :], op0=ALU.add, op1=ALU.mult).then_inc(glu_done, 1)

                    def add_up(e):
                        dve.wait_ge(e_full, e + 1)
                        for t in range(TT):
                            if t == 0:
                                dve.wait_ge(acc_steps, made(acc_steps))
                            dve.scalar_tensor_tensor(
                                out=acc[:, t, :], in0=P[e % 2][:, t * 128:t * 128 + 128],
                                scalar=comb[:, t, e:e + 1], in1=acc[:, t, :], op0=ALU.mult, op1=ALU.add).then_inc(acc_steps, one(acc_steps))

                    for i in range(NE):
                        if i >= 2:
                            if i - 2 < 2:
                                dve.wait_ge(base, 1 if i == 2 else 3)
                            else:
                                dve.wait_ge(e_full, i - 3)
                        glu(i)
                        if i == 2:
                            dve.wait_ge(base, 3)
                            dve.tensor_tensor(
                                acc, P[3][:, :].rearrange("p (t d) -> p t d", t=TT), xres[:, :, :], ALU.add).then_inc(acc_steps, one(acc_steps))
                        if i >= 3:
                            add_up(i - 3)
                        if i == 3:
                            head_dt_start(dve, a_at)
                        if 4 <= i < 4 + LOG_TERMS - 1:
                            head_log(dve, LOG_TERMS + 3 - i)
                        if i == 12:
                            head_dt_parts(dve)
                        if i == 14:
                            head_c_parts(dve, a_at)
                    add_up(E - 1)
                    layer_norm(dve, acc_steps, ln3_root, acc, acc)
                    assert made(acc_steps) == ACC_STEPS

            nc.all_engine_barrier(sems_to_clear=range(signals[0].num, signals[-1].num + 1))


def kernel(**inputs):
    import numpy as np
    import concourse.bacc as bacc
    from concourse.bass_utils import run_bass_kernel_spmd as run

    a = {k: np.asarray(v) for k, v in inputs.items()}
    w_in = a["L0_attn_W_in"]
    par = w_in[2 * DI:].reshape(H, 2, D)
    part = np.arange(128)
    f1 = a["L0_ffn_fc1_w"].transpose(2, 0, 1)
    s1 = a["L0_ffn_s_fc1_w"].reshape(2, 2, F, D).transpose(3, 1, 0, 2).reshape(D, 2, 2 * F)
    b1 = a["L0_ffn_fc1_b"].reshape(E, 2, F).transpose(2, 0, 1)[:, :, ::-1]
    sb1 = a["L0_ffn_s_fc1_b"].reshape(2, 2, F).transpose(2, 1, 0)[:, :, ::-1]
    f2 = a["L0_ffn_fc2_w"].transpose(2, 0, 1)
    s2 = a["L0_ffn_s_fc2_w"].reshape(D, 2, F).transpose(2, 1, 0)
    head_of = np.repeat(np.arange(H), NS)
    pick = (np.arange(2)[:, None, None] * HG + np.arange(4)[None, :, None] * 8 + part // NS).reshape(-1)
    f = np.float32
    data = {
        "xT": np.concatenate([a["x"].reshape(B * T, D).T, np.zeros((D, T), np.float32)], 1),
        "x": a["x"].reshape(B * T, D),
        "ctxT": a["ctx_1024"].reshape(B * S, D).T,
        "A_log": a["L0_attn_A_log"].reshape(G, 128).T,
        "WinT": np.concatenate([w_in[:2 * DI], np.tile(par[:, 0], (4, 1)), np.tile(par[:, 1], (4, 1))]).T,
        "Wbc": a["L0_attn_W_bc"].reshape(G, HG, 4, NS, 2, 128).transpose(0, 5, 2, 4, 1, 3)
        .reshape(G * 128, 1024),
        "WoutT": a["L0_attn_W_out"].T.reshape(2, 128, D).transpose(1, 0, 2),
        "skip": a["L0_attn_skip"],
        "dtb": np.tile(a["L0_attn_dt_bias"], 4)[:, None],
        "cw": a["L0_attn_dw_weight"].reshape(2, 128, KW).transpose(1, 0, 2),
        "cb": a["L0_attn_dw_bias"].reshape(2, 128).T,
        "Wq": a["L0_xattn_Wq"], "bq": a["L0_xattn_bq"][:, None],
        "Wk": a["L0_xattn_Wk"], "bk": a["L0_xattn_bk"][:, None],
        "Wv": a["L0_xattn_Wv"], "bv": a["L0_xattn_bv"][None, :],
        "gwT": a["L0_ffn_gate_w"].T,
        "fc1T": np.concatenate([f1, s1], 1),
        "fcol": np.concatenate([
            np.concatenate([b1, sb1], 1),
            np.concatenate([a["L0_ffn_geglu_mult"].T, a["L0_ffn_s_geglu_mult"].reshape(2, F).T], 1)[:, :, None]], 2),
        "fc2T": np.concatenate([f2, s2], 1),
        "fc2b": np.concatenate([a["L0_ffn_fc2_b"], a["L0_ffn_s_fc2_b"][None, :]], 0),
        "heads": (((part[:, None] // 32 != 1) & (part[:, None] % H == head_of[None, :]))).astype(f),
        "dt_rows": ((part[:, None] // 32 != 1)
                    & (part[:, None] % H == (np.arange(G // 2)[:, None] * 8 + part % 8).reshape(-1)[None, :])
                    & (np.tile(part, G // 2) % 32 < 16)[None, :]).astype(f),
        "rn_pick": ((part[:, None] // 32 != 1) & (part[:, None] % 32 == pick[None, :])).astype(f),
        "onehot": ((np.arange(252)[None, :] >= 124)
                   & (part[:, None] // NS == (np.arange(252)[None, :] - 124) % 32)).astype(f),
        "tiled_eye": (part[:, None] % L == part[None, :] % L).astype(f),
        "causal": (np.arange(L)[None, :] >= part[:, None] % L).astype(f),
        "chunk_on": np.tile((np.arange(T) % L != 0).astype(f), (128, 1)),
        "own_head": np.concatenate([part[:, None] // NS == np.arange(HG)[None, :],
                                    part[:, None] % 32 >= 16], 1).astype(f),
        "eye": np.eye(128, dtype=f),
    }
    nc = bacc.Bacc("TRN2", target_bir_lowering=False, num_devices=1)
    arrays, args = {}, {}
    for name, v in data.items():
        arrays[f"in_{name}"] = v = np.ascontiguousarray(v)
        args[name] = nc.dram_tensor(f"in_{name}", v.shape, mybir.dt.float32, kind="ExternalInput").ap()
    args["out"] = nc.dram_tensor("out_x", (B * T, D), mybir.dt.float32, kind="ExternalOutput").ap()
    build(nc, **args)
    r = run(nc, [arrays], core_ids=[0])
    return r.results[0]["out_x"].reshape(B, T, D)
```
